# Optimizing a Trainium2 kernel written in Bass

```python
import numpy as np
import jax
import jax.numpy as jnp

def _softmax(x, axis=-1):
    return jax.nn.softmax(x, axis=axis)

def _gelu(x):
    return jax.nn.gelu(x, approximate=True)

def _silu(x):
    return jax.nn.silu(x)

def _sigmoid(x):
    return jax.nn.sigmoid(x)

def _layernorm(x, axis=-1, eps=1e-05):
    m = jnp.mean(x, axis=axis, keepdims=True)
    v = jnp.var(x, axis=axis, keepdims=True)
    return (x - m) / jnp.sqrt(v + eps)

def _scatter_add(tgt, idx, src, axis=0):
    return tgt.at[idx].add(src)

def _segment_sum(src, seg, n):
    return jax.ops.segment_sum(src, seg, n)
kernel_name = 'mk_metaformer_d2_conv_nchw256_r4_412091'

def setup_inputs(seed: int=0):
    np.random.seed(seed)
    _w = jnp.asarray

    def _rec_inputs():
        import jax
        import jax.numpy as jnp
        _gk = jax.random.key(seed)
        x = 7.22e-05 + 1 * jax.random.normal(jax.random.fold_in(_gk, 1), (8, 64, 16, 16), jnp.float32)
        return x
    x = _rec_inputs()

    def _L0_conv_setup():
        import jax, jax.numpy as jnp
        import numpy as np
        B, C1, C2, H, W = (8, 64, 64, 16, 16)
        GC = 8
        C = C1 * 1 // GC * GC
        G = C // GC
        K = 9
        DK = 3
        OM = (G * K * 3 + 7) // 8 * 8
        EPS = 1e-05

        def _dcn_core(v, off, mask):
            Cg = v.shape[-1]
            dy = jnp.repeat(jnp.arange(-1.0, 2.0), 3)
            dx = jnp.tile(jnp.arange(-1.0, 2.0), 3)
            hh = jnp.arange(H, dtype=jnp.float32)[:, None, None, None]
            ww = jnp.arange(W, dtype=jnp.float32)[None, :, None, None]
            ys = hh + dy + off[..., 0]
            xs = ww + dx + off[..., 1]
            ys = ys.transpose(0, 1, 2, 4, 3).reshape(B, H * W * K, G)
            xs = xs.transpose(0, 1, 2, 4, 3).reshape(B, H * W * K, G)
            vf = v.reshape(B, H * W, G, Cg)
            y0, x0 = (jnp.floor(ys), jnp.floor(xs))
            out = jnp.zeros((B, H * W * K, G, Cg), jnp.float32)
            for oy in (0.0, 1.0):
                for ox in (0.0, 1.0):
                    yy, xx = (y0 + oy, x0 + ox)
                    wgt = (1.0 - jnp.abs(ys - yy)) * (1.0 - jnp.abs(xs - xx))
                    valid = (yy >= 0) & (yy < H) & (xx >= 0) & (xx < W)
                    idx = (jnp.clip(yy, 0, H - 1) * W + jnp.clip(xx, 0, W - 1)).astype(jnp.int32)
                    g = jnp.take_along_axis(vf, idx[..., None], axis=1)
                    out = out + jnp.where(valid, wgt, 0.0)[..., None] * g
            out = out.reshape(B, H * W, K, G, Cg)
            mk = mask.transpose(0, 1, 2, 4, 3).reshape(B, H * W, K, G)
            return jnp.einsum('npkgc,npkg->npgc', out, mk).reshape(B, H, W, G * Cg)
        ks = jax.random.split(jax.random.key(seed), 16)
        s = lambda k, sh, sc=0.05: jax.random.normal(k, sh, jnp.float32) * sc
        return {'x': jax.random.normal(ks[0], (B, C1, H, W), jnp.float32), 'cv1_w': s(ks[1], (C, C1)), 'cv1_b': s(ks[2], (C,)), 'vp_w': s(ks[3], (C, C)), 'vp_b': s(ks[4], (C,)), 'dw_w': s(ks[5], (C, 1, DK, DK)), 'dw_b': s(ks[6], (C,)), 'om_w': s(ks[7], (OM, C), 0.01), 'om_b': s(ks[8], (OM,), 0.01), 'op_w': s(ks[9], (C, C)), 'cv2_w': s(ks[10], (C2, C)), 'bn_g': jnp.ones((C2,), jnp.float32), 'bn_b': jnp.zeros((C2,), jnp.float32), 'bn_m': jnp.zeros((C2,), jnp.float32), 'bn_v': jnp.ones((C2,), jnp.float32)}
    _L0_conv_all = _L0_conv_setup()
    _L0_conv_in = {k: v for k, v in _L0_conv_all.items() if k in ('cv1_w', 'cv1_b', 'vp_w', 'vp_b', 'dw_w', 'dw_b', 'om_w', 'om_b', 'op_w', 'cv2_w', 'bn_g', 'bn_b', 'bn_m', 'bn_v')}
    del _L0_conv_all

    def _L0_ffn_setup():
        import jax, jax.numpy as jnp
        import numpy as np
        N_EXPERTS = 8
        TOP_K = 2
        key = jax.random.key(seed)
        ks = jax.random.split(key, 5)
        B, T, C, E, H = (8, 512, 64, 8, 682)
        scale = 1.0 / np.sqrt(C)
        return {'x': jax.random.normal(ks[0], (B, T, C), dtype=jnp.float32), 'router_w': jax.random.normal(ks[1], (E, C), dtype=jnp.float32) * scale, 'w1': jax.random.normal(ks[2], (E, H, C), dtype=jnp.float32) * scale, 'w2': jax.random.normal(ks[3], (E, C, H), dtype=jnp.float32) * (1.0 / np.sqrt(H)), 'w3': jax.random.normal(ks[4], (E, H, C), dtype=jnp.float32) * scale}
    _L0_ffn_all = _L0_ffn_setup()
    _L0_ffn_in = {k: v for k, v in _L0_ffn_all.items() if k in ('router_w', 'w1', 'w2', 'w3')}
    del _L0_ffn_all

    def _L1_conv_setup():
        import jax, jax.numpy as jnp
        import numpy as np
        HEADS = 8
        DIM_HEAD = 32
        SCALE = DIM_HEAD ** (-0.5)
        key = jax.random.key(seed)
        k1, k2, k3, k4 = jax.random.split(key, 4)
        x = jax.random.normal(k1, (16, 64, 16, 16), dtype=jnp.float32)
        w_qkv = jax.random.normal(k2, (3 * HEADS * DIM_HEAD, 64), dtype=jnp.float32) * 0.05
        w_out = jax.random.normal(k3, (64, HEADS * DIM_HEAD), dtype=jnp.float32) * 0.05
        b_out = jax.random.normal(k4, (64,), dtype=jnp.float32) * 0.05
        return {'x': x, 'w_qkv': w_qkv, 'w_out': w_out, 'b_out': b_out}
    _L1_conv_all = _L1_conv_setup()
    _L1_conv_in = {k: v for k, v in _L1_conv_all.items() if k in ('w_qkv', 'w_out', 'b_out')}
    del _L1_conv_all

    def _L1_ffn_setup():
        import jax, jax.numpy as jnp
        import numpy as np
        D_MODEL = 64
        N_EXPERTS = 16
        HIDDEN = 128
        SCALE = 0.02
        key = jax.random.key(seed)
        ks = jax.random.split(key, 5)
        x = jax.random.normal(ks[0], (4, 2048, D_MODEL), dtype=jnp.float32)
        gate_w = jax.random.normal(ks[1], (D_MODEL, N_EXPERTS), dtype=jnp.float32) * SCALE
        gate_b = jnp.zeros((N_EXPERTS,), dtype=jnp.float32)
        w1 = jax.random.normal(ks[2], (N_EXPERTS, D_MODEL, HIDDEN), dtype=jnp.float32) * SCALE
        w2 = jax.random.normal(ks[3], (N_EXPERTS, D_MODEL, HIDDEN), dtype=jnp.float32) * SCALE
        w3 = jax.random.normal(ks[4], (N_EXPERTS, HIDDEN, D_MODEL), dtype=jnp.float32) * SCALE
        return {'x': x, 'gate_w': gate_w, 'gate_b': gate_b, 'w1': w1, 'w2': w2, 'w3': w3}
    _L1_ffn_all = _L1_ffn_setup()
    _L1_ffn_in = {k: v for k, v in _L1_ffn_all.items() if k in ('gate_w', 'gate_b', 'w1', 'w2', 'w3')}
    del _L1_ffn_all
    return {'x': x, 'L0_conv_cv1_w': _L0_conv_in['cv1_w'], 'L0_conv_cv1_b': _L0_conv_in['cv1_b'], 'L0_conv_vp_w': _L0_conv_in['vp_w'], 'L0_conv_vp_b': _L0_conv_in['vp_b'], 'L0_conv_dw_w': _L0_conv_in['dw_w'], 'L0_conv_dw_b': _L0_conv_in['dw_b'], 'L0_conv_om_w': _L0_conv_in['om_w'], 'L0_conv_om_b': _L0_conv_in['om_b'], 'L0_conv_op_w': _L0_conv_in['op_w'], 'L0_conv_cv2_w': _L0_conv_in['cv2_w'], 'L0_conv_bn_g': _L0_conv_in['bn_g'], 'L0_conv_bn_b': _L0_conv_in['bn_b'], 'L0_conv_bn_m': _L0_conv_in['bn_m'], 'L0_conv_bn_v': _L0_conv_in['bn_v'], 'L0_ffn_router_w': _L0_ffn_in['router_w'], 'L0_ffn_w1': _L0_ffn_in['w1'], 'L0_ffn_w2': _L0_ffn_in['w2'], 'L0_ffn_w3': _L0_ffn_in['w3'], 'L1_conv_w_qkv': _L1_conv_in['w_qkv'], 'L1_conv_w_out': _L1_conv_in['w_out'], 'L1_conv_b_out': _L1_conv_in['b_out'], 'L1_ffn_gate_w': _L1_ffn_in['gate_w'], 'L1_ffn_gate_b': _L1_ffn_in['gate_b'], 'L1_ffn_w1': _L1_ffn_in['w1'], 'L1_ffn_w2': _L1_ffn_in['w2'], 'L1_ffn_w3': _L1_ffn_in['w3']}

def reference(x, L0_conv_cv1_w, L0_conv_cv1_b, L0_conv_vp_w, L0_conv_vp_b, L0_conv_dw_w, L0_conv_dw_b, L0_conv_om_w, L0_conv_om_b, L0_conv_op_w, L0_conv_cv2_w, L0_conv_bn_g, L0_conv_bn_b, L0_conv_bn_m, L0_conv_bn_v, L0_ffn_router_w, L0_ffn_w1, L0_ffn_w2, L0_ffn_w3, L1_conv_w_qkv, L1_conv_w_out, L1_conv_b_out, L1_ffn_gate_w, L1_ffn_gate_b, L1_ffn_w1, L1_ffn_w2, L1_ffn_w3):
    import jax
    import jax.numpy as jnp

    def _L0_conv_ref(x, cv1_w, cv1_b, vp_w, vp_b, dw_w, dw_b, om_w, om_b, op_w, cv2_w, bn_g, bn_b, bn_m, bn_v):
        import jax, jax.numpy as jnp
        import numpy as np
        B, C1, C2, H, W = (8, 64, 64, 16, 16)
        GC = 8
        C = C1 * 1 // GC * GC
        G = C // GC
        K = 9
        DK = 3
        OM = (G * K * 3 + 7) // 8 * 8
        EPS = 1e-05

        def _dcn_core(v, off, mask):
            Cg = v.shape[-1]
            dy = jnp.repeat(jnp.arange(-1.0, 2.0), 3)
            dx = jnp.tile(jnp.arange(-1.0, 2.0), 3)
            hh = jnp.arange(H, dtype=jnp.float32)[:, None, None, None]
            ww = jnp.arange(W, dtype=jnp.float32)[None, :, None, None]
            ys = hh + dy + off[..., 0]
            xs = ww + dx + off[..., 1]
            ys = ys.transpose(0, 1, 2, 4, 3).reshape(B, H * W * K, G)
            xs = xs.transpose(0, 1, 2, 4, 3).reshape(B, H * W * K, G)
            vf = v.reshape(B, H * W, G, Cg)
            y0, x0 = (jnp.floor(ys), jnp.floor(xs))
            out = jnp.zeros((B, H * W * K, G, Cg), jnp.float32)
            for oy in (0.0, 1.0):
                for ox in (0.0, 1.0):
                    yy, xx = (y0 + oy, x0 + ox)
                    wgt = (1.0 - jnp.abs(ys - yy)) * (1.0 - jnp.abs(xs - xx))
                    valid = (yy >= 0) & (yy < H) & (xx >= 0) & (xx < W)
                    idx = (jnp.clip(yy, 0, H - 1) * W + jnp.clip(xx, 0, W - 1)).astype(jnp.int32)
                    g = jnp.take_along_axis(vf, idx[..., None], axis=1)
                    out = out + jnp.where(valid, wgt, 0.0)[..., None] * g
            out = out.reshape(B, H * W, K, G, Cg)
            mk = mask.transpose(0, 1, 2, 4, 3).reshape(B, H * W, K, G)
            return jnp.einsum('npkgc,npkg->npgc', out, mk).reshape(B, H, W, G * Cg)
        y = jnp.einsum('nchw,oc->nohw', x, cv1_w) + cv1_b[None, :, None, None]
        t = y.transpose(0, 2, 3, 1)
        v = (t @ vp_w.T + vp_b).reshape(B, H, W, G, GC)
        dw = jax.lax.conv_general_dilated(y, dw_w, (1, 1), 'SAME', feature_group_count=C, dimension_numbers=('NCHW', 'OIHW', 'NCHW'))
        dw = dw + dw_b[None, :, None, None]
        om = dw.transpose(0, 2, 3, 1) @ om_w.T + om_b
        om = om[..., :G * K * 3].reshape(B, H, W, G, K * 3)
        off = om[..., :2 * K].reshape(B, H, W, G, K, 2)
        mask = om[..., 2 * K:]
        d = _dcn_core(v, off, mask) @ op_w.T
        z = d @ cv2_w.T
        z = (z - bn_m) * (bn_g / jnp.sqrt(bn_v + EPS)) + bn_b
        z = z * jax.nn.sigmoid(z)
        return z.transpose(0, 3, 1, 2)

    def _L0_ffn_ref(x, router_w, w1, w2, w3):
        import jax, jax.numpy as jnp
        import numpy as np
        N_EXPERTS = 8
        TOP_K = 2
        B, T, C = x.shape
        flat = x.reshape(-1, C)
        logits = flat @ router_w.T
        probs = jax.nn.softmax(logits, axis=-1)
        topk_probs, topk_idx = jax.lax.top_k(probs, TOP_K)
        topk_probs = topk_probs / (jnp.sum(topk_probs, axis=-1, keepdims=True) + 1e-09)
        onehot = jax.nn.one_hot(topk_idx, N_EXPERTS, dtype=flat.dtype)
        gates = jnp.einsum('nk,nke->ne', topk_probs, onehot)
        h1 = jnp.einsum('nc,ehc->neh', flat, w1)
        h3 = jnp.einsum('nc,ehc->neh', flat, w3)
        h = jax.nn.silu(h1) * h3
        y = jnp.einsum('neh,ech->nec', h, w2)
        out = jnp.einsum('ne,nec->nc', gates, y)
        return out.reshape(B, T, C)

    def _L1_conv_ref(x, w_qkv, w_out, b_out):
        import jax, jax.numpy as jnp
        import numpy as np
        HEADS = 8
        DIM_HEAD = 32
        SCALE = DIM_HEAD ** (-0.5)
        b, c, h, w = x.shape
        n = h * w
        qkv = jnp.einsum('bchw,oc->bohw', x, w_qkv)
        qkv = qkv.reshape(b, 3, HEADS, DIM_HEAD, n)
        q, k, v = (qkv[:, 0], qkv[:, 1], qkv[:, 2])
        q = jax.nn.softmax(q, axis=-2) * SCALE
        k = jax.nn.softmax(k, axis=-1)
        context = jnp.einsum('bhdn,bhen->bhde', k, v)
        out = jnp.einsum('bhde,bhdn->bhen', context, q)
        out = out.reshape(b, HEADS * DIM_HEAD, h, w)
        return jnp.einsum('bchw,oc->bohw', out, w_out) + b_out[None, :, None, None]

    def _L1_ffn_ref(x, gate_w, gate_b, w1, w2, w3):
        import jax, jax.numpy as jnp
        import numpy as np
        D_MODEL = 64
        N_EXPERTS = 16
        HIDDEN = 128
        SCALE = 0.02
        n_experts = w1.shape[0]
        logits = jnp.einsum('bsd,de->bse', x, gate_w) + gate_b
        probs = jax.nn.softmax(logits, axis=-1)
        top_probs, top_idx = jax.lax.top_k(probs, 2)
        top_probs = top_probs / jnp.sum(top_probs, axis=-1, keepdims=True)
        dispatch = jnp.sum(jax.nn.one_hot(top_idx, n_experts, dtype=x.dtype) * top_probs[..., None], axis=-2)
        h1 = jnp.einsum('bsd,edh->bseh', x, w1)
        h2 = jnp.einsum('bsd,edh->bseh', x, w2)
        hidden = jax.nn.silu(h1) * h2
        expert_out = jnp.einsum('bseh,eho->bseo', hidden, w3)
        return jnp.einsum('bseo,bse->bso', expert_out, dispatch)

    def _gn(v, G=32, eps=1e-05):
        B_, C_, H_, W_ = v.shape
        g = v.reshape(B_, G, C_ // G, H_, W_)
        m = jnp.mean(g, axis=(2, 3, 4), keepdims=True)
        s = jnp.var(g, axis=(2, 3, 4), keepdims=True)
        return ((g - m) / jnp.sqrt(s + eps)).reshape(v.shape)

    def _ln_c(v, eps=1e-06):
        m = jnp.mean(v, axis=1, keepdims=True)
        s = jnp.var(v, axis=1, keepdims=True)
        return (v - m) / jnp.sqrt(s + eps)

    def _ln_t(v, eps=1e-05):
        m = jnp.mean(v, axis=-1, keepdims=True)
        s = jnp.var(v, axis=-1, keepdims=True)
        return (v - m) / jnp.sqrt(s + eps)

    def _to_tokens(v):
        B_, C_, H_, W_ = v.shape
        return v.reshape(B_, C_, H_ * W_).transpose(0, 2, 1)

    def _from_tokens(t, like):
        B_, C_, H_, W_ = like.shape
        return t.transpose(0, 2, 1).reshape(B_, C_, H_, W_)
    x = x + _L0_conv_ref(_ln_c(x), L0_conv_cv1_w, L0_conv_cv1_b, L0_conv_vp_w, L0_conv_vp_b, L0_conv_dw_w, L0_conv_dw_b, L0_conv_om_w, L0_conv_om_b, L0_conv_op_w, L0_conv_cv2_w, L0_conv_bn_g, L0_conv_bn_b, L0_conv_bn_m, L0_conv_bn_v)
    t = _to_tokens(x)
    t = t + _L0_ffn_ref(_ln_t(t), L0_ffn_router_w, L0_ffn_w1, L0_ffn_w2, L0_ffn_w3)
    x = _from_tokens(t, x)
    x = x + _L1_conv_ref(_ln_c(x), L1_conv_w_qkv, L1_conv_w_out, L1_conv_b_out)
    t = _to_tokens(x)
    t = t + _L1_ffn_ref(_ln_t(t), L1_ffn_gate_w, L1_ffn_gate_b, L1_ffn_w1, L1_ffn_w2, L1_ffn_w3)
    x = _from_tokens(t, x)
    return x

_drawn_inputs = setup_inputs


def setup_inputs(seed=0):
    import zlib

    import numpy as np

    out = dict(_drawn_inputs(seed))
    spreads = {'L0_conv_bn_g': (1.0, 0.2),
     'L0_conv_bn_b': (0.0, 0.8),
     'L0_conv_bn_m': (0.0, 0.8),
     'L0_conv_bn_v': (1.0, 0.6),
     'L1_ffn_gate_b': (0.0, 2.0)}
    factors = {'L0_conv_cv1_w': 5.922,
     'L0_conv_cv1_b': 8.0,
     'L0_conv_vp_w': 8.0,
     'L0_conv_vp_b': 8.0,
     'L0_conv_dw_w': 8.0,
     'L0_conv_dw_b': 8.0,
     'L0_conv_om_w': 8.0,
     'L0_conv_om_b': 6.71,
     'L0_conv_op_w': 8.0,
     'L0_conv_cv2_w': 7.27,
     'L1_conv_w_qkv': 64.0,
     'L1_conv_w_out': 64.0,
     'L1_ffn_gate_w': 64.0,
     'L1_ffn_w1': 64.0,
     'L1_ffn_w2': 64.0,
     'L1_ffn_w3': 64.0,
     'L0_ffn_router_w': 8.0,
     'L0_ffn_w1': 8.0,
     'L0_ffn_w2': 8.0,
     'L0_ffn_w3': 8.0,
     'L1_conv_b_out': 64.0}
    for name, (base, spread) in spreads.items():
        noise = np.random.default_rng([zlib.crc32(name.encode()), seed]).standard_normal(out[name].shape)
        drawn = base * np.exp(spread * noise) if base else spread * noise
        out[name] = jnp.asarray(drawn.astype(out[name].dtype))
    for name, factor in factors.items():
        out[name] = (out[name] * factor).astype(out[name].dtype)
    return out
```

```python
from contextlib import ExitStack

import concourse.bass as bass
from concourse import mybir

B, C, H, W = 8, 64, 16, 16
PIX = H * W
P = 128
TT = PIX // P
G, GC, K = 8, 8, 9
GH = 4
NH = G // GH
E0, HID0, CH0 = 8, 682, 114
CPE0 = -(-HID0 // CH0)
E1, CH1 = 16, 128
NC0, NC1 = E0 * CPE0, E1
PAIRS0, PAIRS1 = NC0 // 2, NC1 // 2
PAIRS = PAIRS0 + PAIRS1
PPE0 = CPE0 // 2
UNITS = K * TT * NH
ADDS = UNITS - TT * NH
GU0, GU1 = E0 // 2, E1 // 2
SLOTS = 4
HEADS, DH = 8, 32
HD = HEADS * DH
SCALE = DH ** -0.5
AUG = C + 4
STAGE = 1024
LAG = 2


def build(nc, A, out):
    f32, f32r, u32 = mybir.dt.float32, mybir.dt.float32r, mybir.dt.uint32
    ACT, ALU, AX = mybir.ActivationFunctionType, mybir.AluOpType, mybir.AxisListType.X

    def V(base, dims):
        return bass.AP(base.tensor, base.offset, [list(base.ap[0])] + [list(d) for d in dims])

    with ExitStack() as ctx:
        def sb(name, shape, dt=f32):
            return ctx.enter_context(nc.sbuf_tensor("sb_" + name, shape, dt))

        def ps(name, shape):
            return ctx.enter_context(nc.psum_tensor("ps_" + name, shape, f32))

        def sem(name):
            return ctx.enter_context(nc.semaphore(name))

        w1s = sb("w1s", [P, NC0 * CH0], f32r)
        w3s = sb("w3s", [P, NC0 * CH0], f32r)
        w2s = sb("w2s", [P, NC0, 2 * C], f32r)
        u1s = sb("u1s", [P, NC1 * CH1], f32r)
        u2s = sb("u2s", [P, NC1 * CH1], f32r)
        u3s = sb("u3s", [P, NC1, 2 * C], f32r)
        ident = sb("ident", [P, P])
        negb = sb("negb", [P, 1])
        gmask = sb("gmask", [P, GH])
        iota = sb("iota", [P, W])
        bmask = sb("bmask", [P, P])
        cv1 = sb("cv1", [C, C])
        vp = sb("vp", [C + 1, C])
        opw = sb("opw", [C, C])
        cv2 = sb("cv2", [C, C])
        dww = sb("dww", [C, K])
        vecs = sb("vecs", [C, 7])
        bns = sb("bns", [C, 4])
        omx = sb("omx", [AUG, K * NH * P])
        omym = sb("omym", [AUG, 2 * K * G])
        rw = sb("rw", [C, E0])
        gw = sb("gw", [C + 1, E1])
        wq = sb("wq", [C, HD])
        wk = sb("wk", [C, HD])
        wv = sb("wv", [C, HD])
        wo = sb("wo", [P, 2, C])
        epst = sb("epst", [P, 2, TT])
        mhalf = sb("mhalf", [P, TT])

        xT = sb("xT", [C, PIX])
        xnT = sb("xnT", [C, PIX])
        ypad = sb("ypad", [C + 1, H + 2, W + 2])
        dwT = sb("dwT", [AUG, PIX])
        bdh = sb("bdh", [P, NH, GH * GC * H], f32r)
        bdl = sb("bdl", [P, NH, GH * GC * H], f32r)
        ym = sb("ym", [P, TT, 2 * K * G])
        hy = sb("hy", [P, TT, K * G * H])
        hat = sb("hat", [P, NH * PIX])
        hatr = sb("hatr", [P, NH * PIX], f32r)
        hx = sb("hx", [P, 3, NH, PIX], f32r)
        prod = sb("prod", [P, 2, GH * GC * H])
        acc = sb("acc", [P, TT, NH, GH * GC * H])
        yrep = [acc[0:C + 1, 1, :, :].rearrange("p h n -> p (h n)"), prod[0:C + 1, :, :].rearrange("p a n -> p (a n)")]
        dsum = sb("dsum", [P, TT, C])
        oT = sb("oT", [C, PIX])
        dT = zT = xnT
        x1T = sb("x1T", [C, PIX])

        sil = sb("sil", [P, 2, 2 * PIX])
        hid = sb("hid", [P, 2, 2 * PIX])
        hh = sb("hh", [P, 2, 2 * PIX], f32r)
        hl = sb("hl", [P, 2, 2 * PIX], f32r)
        xgh = sb("xgh", [P, SLOTS, 2 * PIX], f32r)
        xgl = sb("xgl", [P, SLOTS, 2 * PIX], f32r)
        NE = (E0, E1)
        st = [sb(f"st{j}", [P, TT, 6]) for j in range(4)]
        mv = [sb(f"mv{j}", [P, TT, 2]) for j in range(4)]
        rs = [sb(f"rs{j}", [P, TT]) for j in range(4)]
        xn = [sb(f"xn{j}", [P, TT, (1 + j % 2) * C]) for j in range(4)]
        xh = [sb(f"xh{m}", [P, PIX], f32r) for m in range(2)]
        xl = [sb(f"xl{m}", [P, PIX], f32r) for m in range(2)]
        xf = [sb(f"xf{m}", [C + 1, PIX]) for m in range(2)]
        lg = [sb(f"lg{m}", [P, TT, NE[m]]) for m in range(2)]
        ex = [sb(f"ex{m}", [P, TT, NE[m]]) for m in range(2)]
        mx = [sb(f"mx{m}", [P, TT, 8]) for m in range(2)]
        ix = [sb(f"ix{m}", [P, TT, 8], u32) for m in range(2)]
        ixf = [sb(f"ixf{m}", [P, TT, 2]) for m in range(2)]
        nm = [sb(f"nm{m}", [P, TT]) for m in range(2)]
        sm = [sb(f"sm{m}", [P, TT]) for m in range(2)]
        em = [sb(f"em{m}", [P, TT, 2]) for m in range(2)]
        pk = [sb(f"pk{m}", [P, TT, 2]) for m in range(2)]
        ks_ = [sb(f"ks{m}", [P, TT, 2]) for m in range(2)]
        oh = [sb(f"oh{m}", [P, TT, 2, NE[m]]) for m in range(2)]
        gt = [sb(f"gt{m}", [P, TT, NE[m]]) for m in range(2)]
        xg = sb("xg", [P, 2, TT, 2, 2 * C])

        ylo = sb("ylo", [C, PIX])
        x2T = sb("x2T", [C, PIX])
        xn2T = ylo
        qT = sb("qT", [P, 2, PIX])
        qm = sb("qm", [P, TT * HEADS])
        qz = sb("qz", [P, TT * HEADS])
        qr = sb("qr", [P, TT * HEADS])
        km = sb("km", [P, 2])
        kz = sb("kz", [P, 2])
        kr = sb("kr", [P, 2, 2])
        cT = sb("cT", [P, 2, P])
        mT = sb("mT", [P, 2, C])
        x3T = sb("x3T", [C, PIX])
        outT = ylo
        q_s, k_s = sil[:, 0, :], sil[:, 1, :]
        v_s, kT_s = hid[:, 0, :], hid[:, 1, :]

        h1 = [ps(f"h1_{j}", [P, 2 * PIX]) for j in range(2)]
        h3 = [ps(f"h3_{j}", [P, 2 * PIX]) for j in range(2)]
        yb = ps("y", [P, PIX * 2])
        tb = [ps(f"t_{j}", [P, 2 * PIX]) for j in range(2)]
        mb = ps("m", [P, 2 * PIX])

        s_const = sem("s_const")
        s_stage = [sem(f"s_stage{j}") for j in range(2)]
        s_act_whi = sem("s_act_whi")
        s_dve_w = sem("s_dve_w")
        s_dve_set = sem("s_dve_set")
        s_dve_bn = sem("s_dve_bn")
        s_act_bn = sem("s_act_bn")
        s_ld_x = sem("s_ld_x")
        s_st = sem("s_st")
        s_pe_xt, s_pe_xnt, s_pe_y, s_pe_v, s_pe_ym = map(sem, ("s_pe_xt", "s_pe_xnt", "s_pe_y", "s_pe_v", "s_pe_ym"))
        s_pe_xr, s_pe_t = sem("s_pe_xr"), sem("s_pe_t")
        s_pe_dt, s_pe_o, s_pe_z, s_pe_x1t = map(sem, ("s_pe_dt", "s_pe_o", "s_pe_z", "s_pe_x1t"))
        s_act_xnt, s_act_y, s_act_bh, s_act_ym = map(sem, ("s_act_xnt", "s_act_y", "s_act_bh", "s_act_ym"))
        s_act_hyabs, s_act_hy = sem("s_act_hyabs"), sem("s_act_hy")
        s_act_abs, s_act_hat = sem("s_act_abs"), sem("s_act_hat")
        s_act_dt, s_act_o, s_act_z = map(sem, ("s_act_dt", "s_act_o", "s_act_z"))
        s_dve_yr = sem("s_dve_yr")
        s_dve_dw, s_dve_bd = sem("s_dve_dw"), sem("s_dve_bd")
        s_dve_hr, s_dve_hx = sem("s_dve_hr"), sem("s_dve_hx")
        s_dve_p, s_dve_dr = sem("s_dve_p"), sem("s_dve_dr")
        s_dve_x1 = sem("s_dve_x1")
        s_pool_bl = sem("s_pool_bl")
        s_pool_dy, s_pool_hy, s_pool_acc = map(sem, ("s_pool_dy", "s_pool_hy", "s_pool_acc"))
        s_dve_st = [sem(f"s_dve_st{j}") for j in range(4)]
        s_dve_mv = [sem(f"s_dve_mv{j}") for j in range(4)]
        s_pool_ve = [sem(f"s_pool_ve{j}") for j in range(4)]
        s_pool_rs = [sem(f"s_pool_rs{j}") for j in range(4)]
        s_dve_xn = [sem(f"s_dve_xn{j}") for j in range(4)]
        def two(name):
            return [sem(f"{name}{m}") for m in range(2)]
        s_pe_xs, s_act_xh, s_act_xf, s_dve_xl = two("s_pe_xs"), two("s_act_xh"), two("s_act_xf"), two("s_dve_xl")
        s_pe_lg, s_act_lg = two("s_pe_lg"), two("s_act_lg")
        s_dve_mx, s_dve_ix, s_dve_nm = two("s_dve_mx"), two("s_dve_ix"), two("s_dve_nm")  
        s_act_ex = two("s_act_ex")
        s_dve_gt = two("s_dve_gt")
        s_pool_xg, s_pe_g, s_act_g, s_dve_g = two("s_pool_xg"), two("s_pe_g"), two("s_act_g"), two("s_dve_g")
        GT, GU = (12, 11), (GU0, GU1)
        s_pe_h1, s_pe_h3, s_pe_y2 = map(sem, ("s_pe_h1", "s_pe_h3", "s_pe_down"))
        s_act_s, s_act_hh, s_dve_hid, s_pool_hl = map(sem, ("s_act_s", "s_act_hh", "s_dve_hid", "s_pool_hl"))
        s_act_yl, s_dve_ys, s_dve_x2, s_dve_ys4, s_dve_x4, s_act_yl4 = map(sem, ("s_act_yl", "s_dve_ys", "s_dve_x2", "s_dve_ys4", "s_dve_x4", "s_act_yl4"))
        (s_pe_x2t, s_pe_xn2t, s_act_xn2t, s_pe_q, s_pe_k, s_pe_vv, s_act_v, s_dve_qm, s_dve_qs, s_act_q,
         s_dve_qz, s_dve_qr, s_dve_qn, s_pe_qt, s_act_qt, s_dve_km, s_act_k, s_pe_kt, s_act_kt, s_pe_c,
         s_dve_c, s_dve_kr, s_pe_mm, s_dve_m, s_pe_at, s_dve_x3, s_pe_x3t) = map(sem, (
            "s_pe_x2t", "s_pe_xn2t", "s_act_xn2t", "s_pe_q", "s_pe_k", "s_pe_vv", "s_act_v", "s_dve_qm", "s_dve_qs", "s_act_q",
            "s_dve_qz", "s_dve_qr", "s_dve_qn", "s_pe_qt", "s_act_qt", "s_dve_km", "s_act_k", "s_pe_kt", "s_act_kt", "s_pe_c",
            "s_dve_c", "s_dve_kr", "s_pe_mm", "s_dve_m", "s_pe_at", "s_dve_x3", "s_pe_x3t"))

        pieces = []
        half = CPE0 * CH0
        for name, dst in (("w1T", w1s), ("w3T", w3s)):
            for e in range(E0):
                pieces.append((A[name][:, e * half:(e + 1) * half], half, "rows", dst[:, e * half:(e + 1) * half]))
        per = STAGE // C
        for c in range(0, NC0, per):
            pieces.append((A["w2T"][:, c:c + per, :], STAGE, "cols", w2s[0:CH0, c:c + per, :]))
        for name, dst in (("u1T", u1s), ("u2T", u2s)):
            for c in range(0, NC1 * CH1, STAGE):
                pieces.append((A[name][:, c:c + STAGE], STAGE, "rows", dst[:, c:c + STAGE]))
        for c in range(0, NC1, per):
            pieces.append((A["u3T"][:, c:c + per, :], STAGE, "cols", u3s[:, c:c + per, :]))
        stage = acc[:, :, :, :].rearrange("p t h n -> p t (h n)")
        stage_hi = xgh[:, :, :].rearrange("p (a b) n -> p a (b n)", a=2)
        staged = [0, 0]
        piece_ready = []
        for j, (_, _, kind, _) in enumerate(pieces):
            staged[j % 2] += 32 if kind == "rows" else 16
            piece_ready.append(staged[j % 2])

        consts = [(ident, "ident"), (negb, "negb"), (gmask, "gmask"), (iota, "iota"), (bmask, "bmask"),
                  (cv1, "cv1T"), (vp, "vpT"), (opw, "opT"), (cv2, "cv2T"), (dww, "dww"),
                  (rw, "rwT"), (gw, "gwT"), (wq, "wqT"), (wk, "wkT"), (wv, "wvT"), (wo, "woT")]
        n_const = 16 * (len(consts) + 7 + 4 + 1)

        block = ctx.enter_context(nc.Block())

        def settled(eng):
            eng.wait_ge(s_const, n_const)

        @block.sync
        def _(sp):
            for dst, name in consts:
                d = dst[tuple(slice(None) for _ in dst.shape)]
                sp.dma_start(d, A[name]).then_inc(s_const, 16)
            for j, name in enumerate(("cv1_b", "dw_b", "bn_g", "bn_b", "bn_m", "bn_v", "b_out")):
                sp.dma_start(vecs[:, j:j + 1], A[name]).then_inc(s_const, 16)
            sp.dma_start(omx[0:C + 1, :], A["omxT"]).then_inc(s_const, 16)
            sp.dma_start(omx[C + 1:AUG, :], A["omxC"]).then_inc(s_const, 16)
            sp.dma_start(omym[0:C + 1, :], A["omymT"]).then_inc(s_const, 16)
            sp.dma_start(omym[C + 1:AUG, :], A["omymC"]).then_inc(s_const, 16)
            sp.dma_start(dwT[C:AUG, :], A["pixC"]).then_inc(s_const, 16)
            for j, (src, cols, kind, _dst) in enumerate(pieces):
                if j >= 2:
                    sp.wait_ge(s_dve_w, j - 1)
                if kind == "rows":
                    for r in range(2):
                        sp.dma_start(stage[C * r:C * r + C, j % 2, 0:cols], src).then_inc(s_stage[j % 2], 16)
                else:
                    rows = src.shape[0]
                    sp.dma_start(stage[0:rows, j % 2, 0:cols], src.rearrange("p c n -> p (c n)")).then_inc(s_stage[j % 2], 16)
            with sp.Fori(0, B) as n:
                sp.wait_ge(s_dve_x1, n)
                sp.dma_start(xT[:, :], A["x"][n]).then_inc(s_ld_x, 16)
                sp.wait_ge(s_dve_x4, n + 1)
                sp.dma_start(out[n], outT[:, :]).then_inc(s_st, 16)
            sp.wait_ge(s_st, 16 * B)

        @block.tensor
        def _(pe):
            mm, tr = nc.tensor.matmul, nc.tensor.transpose

            def transposes_to_tokens(bank, src):
                for t in range(TT):
                    last = tr(bank[:, t * C:(t + 1) * C], src[:, t * P:(t + 1) * P], ident[0:C, 0:C])
                return last

            def transposes_to_channels(bank, src):
                for t in range(TT):
                    last = tr(bank[0:C, t * P:(t + 1) * P], src[:, t, :], ident[:, :])
                return last

            def transposes_doubled(bank, src):
                for t in range(TT):
                    last = tr(bank[:, t * P:(t + 1) * P], src[:, t, :], ident[:, :])
                return last

            def a_pre(n):
                pe.wait_ge(s_ld_x, 16 * n + 16)
                for t in range(TT):
                    last = mm(mb[:, t * C:(t + 1) * C], xT[:, t * P:(t + 1) * P], ident[0:C, 0:C], start=True, stop=True)
                last.then_inc(s_pe_xt, 1)
                pe.wait_ge(s_dve_xn[0], n + 1)
                for t in range(TT):
                    last = mm(mb[0:C, t * P:(t + 1) * P], xn[0][:, t, :], ident[:, :], start=True, stop=True)
                last.then_inc(s_pe_xnt, 1)
                settled(pe)
                pe.wait_ge(s_act_xnt, n + 1)
                mm(mb[0:C, 0:PIX], cv1[:, :], xnT[:, :], start=True, stop=True).then_inc(s_pe_y, 1)
                for b in range(2):
                    pe.wait_ge(s_dve_yr, 2 * n + b + 1)
                    for r in range(H // 2):
                        last = mm(tb[b][:, r * C:(r + 1) * C], yrep[b][:, r * P:(r + 1) * P], vp[:, :],
                                  start=True, stop=True)
                    last.then_inc(s_pe_v, 1)
                pe.wait_ge(s_dve_dw, K * n + K)
                for t in range(TT):
                    last = mm(mb[:, t * 2 * K * G:(t + 1) * 2 * K * G], dwT[:, t * P:(t + 1) * P], omym[:, :],
                              start=True, stop=True)
                last.then_inc(s_pe_ym, 1)

            def a_unit_x(n, k):
                if k == 0:
                    pe.wait_ge(s_act_ym, n + 1)
                else:
                    pe.wait_ge(s_act_abs, K * n + k)
                for h in range(NH):
                    o = (k * NH + h) * P
                    last = mm(mb[:, h * PIX:(h + 1) * PIX], omx[:, o:o + P], dwT[:, :], start=True, stop=True)
                last.then_inc(s_pe_xr, 1)

            def a_unit_t(n, k):
                pe.wait_ge(s_dve_hx, K * n + k + 1)
                if k == 0:
                    pe.wait_ge(s_act_bh, n + 1)
                    pe.wait_ge(s_pool_bl, n + 1)
                for t in range(TT):
                    for h in range(NH):
                        u = (k * TT + t) * NH + h
                        if u >= 2:
                            pe.wait_ge(s_dve_p, UNITS * n + u - 1)
                        w = hx[:, k % 3, h, t * P:(t + 1) * P]
                        mm(tb[u % 2][:, :], w, bdh[:, h, :], start=True, stop=False)
                        mm(tb[u % 2][:, :], w, bdl[:, h, :], start=False, stop=True).then_inc(s_pe_t, 1)

            def route(n, m, bx, bl):
                j = 1 + 2 * m
                pe.wait_ge(s_dve_xn[j], n + 1)
                transposes_doubled(bx, xn[j]).then_inc(s_pe_xs[m], 1)
                pe.wait_ge(s_act_xf[m], n + 1)
                pe.wait_ge(s_dve_xl[m], n + 1)
                rows, w = (C, rw) if m == 0 else (C + 1, gw)
                for t in range(TT):
                    last = mm(bl[:, t * NE[m]:(t + 1) * NE[m]], xf[m][0:rows, t * P:(t + 1) * P], w[:, :],
                              start=True, stop=True)
                last.then_inc(s_pe_lg[m], 1)

            def gate_unit(n, m, u, bank):
                pe.wait_ge(s_pool_xg[m], GU[m] * n + u + 1)
                for e in range(2):
                    for t in range(TT):
                        last = tr(bank[:, (e * TT + t) * P:(e * TT + t + 1) * P],
                                  xg[:, u % 2, t, e, :], ident[:, :])
                last.then_inc(s_pe_g[m], 1)

            def a_tail(n):
                settled(pe)
                pe.wait_ge(s_dve_dr, n + 1)
                transposes_to_channels(mb, dsum).then_inc(s_pe_dt, 1)
                settled(pe)
                pe.wait_ge(s_act_dt, n + 1)
                mm(mb[0:C, 0:PIX], opw[:, :], dT[:, :], start=True, stop=True).then_inc(s_pe_o, 1)
                settled(pe)
                pe.wait_ge(s_act_o, n + 1)
                mm(mb[0:C, 0:PIX], cv2[:, :], oT[:, :], start=True, stop=True).then_inc(s_pe_z, 1)
                settled(pe)
                pe.wait_ge(s_dve_x1, n + 1)
                transposes_to_tokens(mb, x1T).then_inc(s_pe_x1t, 1)
                route(n, 0, mb, mb)
                for u in range(GU0):
                    if u >= 2:
                        pe.wait_ge(s_dve_g[0], GU0 * n + u - 1)
                    gate_unit(n, 0, u, tb[u % 2])

            def up(n, j):
                first, m = (0, 0) if j < PAIRS0 else (PAIRS0, 1)
                ch = (CH0, CH1)[m]
                wa, wb = ((w1s, w3s), (u1s, u2s))[m]
                if j == 0:
                    pe.wait_ge(s_dve_xl[0], n + 1)
                    pe.wait_ge(s_act_xh[0], n + 1)
                if j == PAIRS0:
                    pe.wait_ge(s_dve_g[1], GU1 * n + SLOTS)
                if j == PAIRS0 + SLOTS:
                    pe.wait_ge(s_dve_g[1], GU1 * n + GU1)
                if j % PAIRS0 >= 2:
                    pe.wait_ge(s_act_s, PAIRS * n + j - 1)
                for c in range(2):
                    o = (2 * (j - first) + c) * ch
                    d = h1[j % 2][0:ch, c * PIX:(c + 1) * PIX]
                    mm(d, wa[:, o:o + ch], xh[m][:, :], start=True, stop=False)
                    last = mm(d, wa[:, o:o + ch], xl[m][:, :], start=False, stop=True)
                last.then_inc(s_pe_h1, 1)
                if j < PAIRS0 and j % PPE0 == 0 and (j // PPE0) % 2 == 0:
                    pe.wait_ge(s_dve_g[0], GU0 * n + j // PPE0 // 2 + 1)
                if j % PAIRS0 >= 2:
                    pe.wait_ge(s_dve_hid, PAIRS * n + j - 1)
                for c in range(2):
                    o = (2 * (j - first) + c) * ch
                    e = j // PPE0 if m == 0 else 2 * (j - first) + c
                    slot, x = (e // 2) % SLOTS, slice((e % 2) * PIX, (e % 2 + 1) * PIX)
                    d = h3[j % 2][0:ch, c * PIX:(c + 1) * PIX]
                    mm(d, wb[:, o:o + ch], xgh[:, slot, x], start=True, stop=False)
                    last = mm(d, wb[:, o:o + ch], xgl[:, slot, x], start=False, stop=True)
                last.then_inc(s_pe_h3, 1)

            def down(n, j):
                first, end, m = (0, PAIRS0, 0) if j < PAIRS0 else (PAIRS0, PAIRS, 1)
                ch, w = ((CH0, w2s), (CH1, u3s))[m]
                if j == 0:
                    pe.wait_ge(s_dve_x4, n)
                pe.wait_ge(s_pool_hl, PAIRS * n + j + 1)
                for c in range(2):
                    for z, part in enumerate((hh, hl)):
                        last = mm(yb[:, 0:PIX], w[0:ch, 2 * (j - first) + c, :], part[0:ch, j % 2, c * PIX:(c + 1) * PIX],
                                  start=(j == first and c == 0 and z == 0), stop=(j == end - 1 and c == 1 and z == 1))
                last.then_inc(s_pe_y2, 1)

            def attention(n):
                settled(pe)
                pe.wait_ge(s_dve_x2, n + 1)
                transposes_to_tokens(h1[0], x2T).then_inc(s_pe_x2t, 1)
                settled(pe)
                pe.wait_ge(s_dve_xn[2], n + 1)
                transposes_to_channels(h1[1], xn[2]).then_inc(s_pe_xn2t, 1)
                pe.wait_ge(s_act_xn2t, n + 1)
                for t in range(TT):
                    last = mm(h1[0][:, t * HD:(t + 1) * HD], xn2T[:, t * P:(t + 1) * P], wq[:, :], start=True, stop=True)
                last.then_inc(s_pe_q, 1)
                for c in range(2):
                    last = mm(h1[1][:, c * PIX:(c + 1) * PIX], wk[:, c * P:(c + 1) * P], xn2T[:, :], start=True, stop=True)
                last.then_inc(s_pe_k, 1)
                for t in range(TT):
                    last = mm(h3[0][:, t * HD:(t + 1) * HD], xn2T[:, t * P:(t + 1) * P], wv[:, :], start=True, stop=True)
                last.then_inc(s_pe_vv, 1)
                pe.wait_ge(s_act_k, 2 * n + 2)
                for t in range(TT):
                    for c in range(2):
                        last = tr(h3[1][:, t * HD + c * P:t * HD + (c + 1) * P],
                                  k_s[:, c * PIX + t * P:c * PIX + (t + 1) * P], ident[:, :])
                last.then_inc(s_pe_kt, 1)
                pe.wait_ge(s_act_v, n + 1)
                pe.wait_ge(s_act_kt, n + 1)
                for c in range(2):
                    for t in range(TT):
                        o = t * HD + c * P
                        last = mm(h3[0][:, c * P:(c + 1) * P], v_s[:, o:o + P], kT_s[:, o:o + P], start=(t == 0), stop=(t == TT - 1))
                last.then_inc(s_pe_c, 1)
                pe.wait_ge(s_dve_qn, n + 1)
                for c in range(2):
                    for t in range(TT):
                        last = tr(h1[0][:, c * PIX + t * P:c * PIX + (t + 1) * P],
                                  q_s[:, t * HD + c * P:t * HD + (c + 1) * P], ident[:, :])
                last.then_inc(s_pe_qt, 1)
                pe.wait_ge(s_dve_c, n + 1)
                for c in range(2):
                    last = mm(h1[1][:, c * C:(c + 1) * C], cT[:, c, :], wo[:, c, :], start=True, stop=True)
                last.then_inc(s_pe_mm, 1)
                pe.wait_ge(s_dve_m, n + 1)
                pe.wait_ge(s_act_qt, n + 1)
                for c in range(2):
                    last = mm(yb[0:C, 0:PIX], mT[:, c, :], qT[:, c, :], start=(c == 0), stop=(c == 1))
                last.then_inc(s_pe_at, 1)
                settled(pe)
                pe.wait_ge(s_dve_x3, n + 1)
                transposes_to_tokens(h1[0], x3T).then_inc(s_pe_x3t, 1)
                route(n, 1, h1[1], h3[0])
                for u, bank in enumerate((h3[1], h1[0], h1[1], h3[0])):
                    gate_unit(n, 1, u, bank)

            def late_gates(n):
                for u, bank, j in ((4, h1[0], 2), (5, h3[0], 2), (6, h1[1], 3), (7, h3[1], 3)):
                    pe.wait_ge(s_act_s, PAIRS * n + PAIRS0 + j + 1)
                    pe.wait_ge(s_dve_hid, PAIRS * n + PAIRS0 + j + 1)
                    gate_unit(n, 1, u, bank)

            pe.wait_ge(s_const, n_const)
            pe.wait_ge(s_dve_set, 7)
            pe.wait_ge(s_dve_w, len(pieces))
            with pe.Fori(0, B) as n:
                a_pre(n)
                a_unit_x(n, 0)
                for k in range(K):
                    if k + 1 < K:
                        a_unit_x(n, k + 1)
                    a_unit_t(n, k)
                a_tail(n)
                for j in range(PAIRS0):
                    up(n, j)
                    if j >= LAG:
                        down(n, j - LAG)
                for j in range(PAIRS0 - LAG, PAIRS0):
                    down(n, j)
                attention(n)
                for j in range(PAIRS0, PAIRS):
                    if j == PAIRS0 + SLOTS:
                        late_gates(n)
                    up(n, j)
                    if j >= PAIRS0 + LAG:
                        down(n, j - LAG)
                for j in range(PAIRS - LAG, PAIRS):
                    down(n, j)

        @block.scalar
        def _(act):
            af = nc.scalar.activation

            act.wait_ge(s_const, n_const)
            act.wait_ge(s_dve_bn, 1)
            af(bns[:, 1:2], bns[:, 0:1], ACT.Sqrt).then_inc(s_act_bn, 1)
            for j, (_src, cols, kind, dst) in enumerate(pieces):
                act.wait_ge(s_stage[j % 2], piece_ready[j])
                if kind == "rows":
                    if j >= 2:
                        act.wait_ge(s_dve_w, j - 1)
                    af(stage_hi[:, j % 2, 0:cols], stage[:, j % 2, 0:cols], ACT.Copy).then_inc(s_act_whi, 1)
                else:
                    rows = dst.shape[0]
                    af(dst[:, :, 0:C], stage[0:rows, j % 2, 0:cols].rearrange("p (c n) -> p c n", n=C),
                       ACT.Copy).then_inc(s_act_whi, 1)

            def a_pre(n):
                act.wait_ge(s_pe_xnt, n + 1)
                af(xnT[:, :], mb[0:C, 0:PIX], ACT.Copy).then_inc(s_act_xnt, 1)
                act.wait_ge(s_pe_y, n + 1)
                af(ypad[0:C, 1:1 + H, 1:1 + W], mb[0:C, 0:PIX].rearrange("p (h w) -> p h w", w=W),
                   ACT.Identity, bias=vecs[:, 0:1]).then_inc(s_act_y, 1)
                act.wait_ge(s_dve_bd, 4 * n + 4)
                af(bdh[:, :, :], acc[:, 0, :, :], ACT.Copy).then_inc(s_act_bh, 1)
                act.wait_ge(s_pe_ym, n + 1)
                af(ym[:, :, :], mb[:, 0:TT * 2 * K * G].rearrange("p (t c) -> p t c", t=TT), ACT.Copy).then_inc(s_act_ym, 1)
                for t in range(TT):
                    act.wait_ge(s_pool_dy, TT * n + t + 1)
                    af(hy[:, t, :], hy[:, t, :], ACT.Abs).then_inc(s_act_hyabs, 1)
                for t in range(TT):
                    act.wait_ge(s_act_hyabs, TT * n + t + 1)
                    af(hy[:, t, :], hy[:, t, :], ACT.Relu, scale=-1.0, bias=1.0).then_inc(s_act_hy, 1)

            def a_unit(n, k):
                act.wait_ge(s_pe_xr, K * n + k + 1)
                act.wait_ge(s_dve_hx, K * n + k)
                af(hat[:, :], mb[:, :], ACT.Abs).then_inc(s_act_abs, 1)
                act.wait_ge(s_act_abs, K * n + k + 1)
                af(hat[:, :], hat[:, :], ACT.Relu, scale=-1.0, bias=1.0).then_inc(s_act_hat, 1)

            def route(n, m, bx, bl):
                act.wait_ge(s_pe_xs[m], n + 1)
                af(xf[m][0:C, :], bx[0:C, 0:PIX], ACT.Copy).then_inc(s_act_xf[m], 1)
                af(xh[m][:, :], bx[:, 0:PIX], ACT.Copy).then_inc(s_act_xh[m], 1)
                act.wait_ge(s_pe_lg[m], n + 1)
                af(lg[m][:, :, :], bl[:, 0:TT * NE[m]].rearrange("p (t e) -> p t e", t=TT), ACT.Copy).then_inc(s_act_lg[m], 1)
                act.wait_ge(s_act_lg[m], n + 1)
                act.wait_ge(s_dve_nm[m], n + 1)
                for t in range(TT):
                    af(ex[m][:, t, :], lg[m][:, t, :], ACT.Exp, bias=nm[m][:, t:t + 1],
                       accum_out=sm[m][:, t:t + 1]).then_inc(s_act_ex[m], 1)
                    af(em[m][:, t, :], mx[m][:, t, 0:2], ACT.Exp, bias=nm[m][:, t:t + 1]).then_inc(s_act_ex[m], 1)

            def gate_unit(n, m, u, bank):
                act.wait_ge(s_pe_g[m], GU[m] * n + u + 1)
                af(xgh[:, u % SLOTS, :], bank[:, :], ACT.Copy).then_inc(s_act_g[m], 1)

            def a_tail(n):
                act.wait_ge(s_pe_dt, n + 1)
                af(dT[:, :], mb[0:C, 0:PIX], ACT.Copy).then_inc(s_act_dt, 1)
                act.wait_ge(s_pe_o, n + 1)
                af(oT[:, :], mb[0:C, 0:PIX], ACT.Copy).then_inc(s_act_o, 1)
                act.wait_ge(s_pe_z, n + 1)
                af(zT[:, :], mb[0:C, 0:PIX], ACT.Silu, scale=bns[:, 2:3], bias=bns[:, 3:4]).then_inc(s_act_z, 1)
                route(n, 0, mb, mb)
                for u in range(GU0):
                    gate_unit(n, 0, u, tb[u % 2])

            def silu(n, j):
                ch = CH0 if j < PAIRS0 else CH1
                act.wait_ge(s_pe_h1, PAIRS * n + j + 1)
                act.wait_ge(s_dve_hid, PAIRS * n + max(0, j - 1))
                af(sil[0:ch, j % 2, :], h1[j % 2][0:ch, :], ACT.Silu).then_inc(s_act_s, 1)

            def high(n, j):
                ch = CH0 if j < PAIRS0 else CH1
                act.wait_ge(s_dve_hid, PAIRS * n + j + 1)
                act.wait_ge(s_pe_y2, PAIRS * n + max(0, j - 1))
                af(hh[0:ch, j % 2, :], hid[0:ch, j % 2, :], ACT.Copy).then_inc(s_act_hh, 1)

            def attention(n):
                act.wait_ge(s_pe_xn2t, n + 1)
                af(xn2T[:, :], h1[1][0:C, 0:PIX], ACT.Copy).then_inc(s_act_xn2t, 1)
                act.wait_ge(s_dve_km, n + 1)
                for c in range(2):
                    af(k_s[:, c * PIX:(c + 1) * PIX], h1[1][:, c * PIX:(c + 1) * PIX], ACT.Exp, bias=km[:, c:c + 1],
                       accum_out=kz[:, c:c + 1]).then_inc(s_act_k, 1)
                act.wait_ge(s_pe_vv, n + 1)
                af(v_s, h3[0][:, :], ACT.Copy).then_inc(s_act_v, 1)
                act.wait_ge(s_dve_qs, n + 1)
                af(q_s, q_s, ACT.Exp).then_inc(s_act_q, 1)
                act.wait_ge(s_pe_kt, n + 1)
                af(kT_s, h3[1][:, :], ACT.Copy).then_inc(s_act_kt, 1)
                act.wait_ge(s_pe_qt, n + 1)
                af(qT[:, :, :], h1[0][:, :].rearrange("p (c n) -> p c n", c=2), ACT.Copy).then_inc(s_act_qt, 1)
                route(n, 1, h1[1], h3[0])
                for u, bank in enumerate((h3[1], h1[0], h1[1], h3[0])):
                    gate_unit(n, 1, u, bank)

            with act.Fori(0, B) as n:
                a_pre(n)
                for k in range(K):
                    a_unit(n, k)
                a_tail(n)
                for j in range(PAIRS0):
                    silu(n, j)
                    if j >= 1:
                        high(n, j - 1)
                high(n, PAIRS0 - 1)
                act.wait_ge(s_pe_y2, PAIRS * n + PAIRS0)
                act.wait_ge(s_st, 16 * n)
                af(ylo[:, :], yb[C:P, 0:PIX], ACT.Copy).then_inc(s_act_yl, 1)
                attention(n)
                for j in range(PAIRS0, PAIRS):
                    if j == PAIRS0 + SLOTS:
                        high(n, j - 1)
                        for u, bank in ((4, h1[0]), (5, h3[0]), (6, h1[1]), (7, h3[1])):
                            gate_unit(n, 1, u, bank)
                    silu(n, j)
                    if j >= PAIRS0 + 1 and j != PAIRS0 + SLOTS:
                        high(n, j - 1)
                high(n, PAIRS - 1)
                act.wait_ge(s_pe_y2, PAIRS * n + PAIRS)
                af(ylo[:, :], yb[C:P, 0:PIX], ACT.Copy).then_inc(s_act_yl4, 1)

        @block.vector
        def _(dve):
            v = nc.vector
            v.memset(ypad[0:C, :, :], 0.0).then_inc(s_dve_set, 1)
            v.memset(ypad[C:C + 1, :, :], 1.0).then_inc(s_dve_set, 1)
            v.memset(xf[1][C:C + 1, :], 1.0).then_inc(s_dve_set, 1)
            v.memset(epst[:, 0, :], 1e-6).then_inc(s_dve_set, 1)
            v.memset(epst[:, 1, :], 1e-5).then_inc(s_dve_set, 1)
            v.memset(mhalf[:, :], -0.5).then_inc(s_dve_set, 1)
            v.memset(xf[0][C:C + 1, :], 1.0).then_inc(s_dve_set, 1)
            dve.wait_ge(s_const, n_const)
            v.tensor_scalar(bns[:, 0:1], vecs[:, 5:6], 1e-5, None, ALU.add).then_inc(s_dve_bn, 1)
            dve.wait_ge(s_act_bn, 1)
            v.reciprocal(bns[:, 0:1], bns[:, 1:2]).then_inc(s_dve_bn, 1)
            dve.wait_ge(s_dve_bn, 2)
            v.tensor_tensor(bns[:, 2:3], vecs[:, 2:3], bns[:, 0:1], ALU.mult).then_inc(s_dve_bn, 1)
            dve.wait_ge(s_dve_bn, 3)
            v.tensor_tensor(bns[:, 1:2], vecs[:, 4:5], bns[:, 2:3], ALU.mult).then_inc(s_dve_bn, 1)
            dve.wait_ge(s_dve_bn, 4)
            v.tensor_tensor(bns[:, 3:4], vecs[:, 3:4], bns[:, 1:2], ALU.subtract).then_inc(s_dve_bn, 1)
            for j, (_src, cols, kind, dst) in enumerate(pieces):
                dve.wait_ge(s_act_whi, j + 1)
                if kind == "rows":
                    v.scalar_tensor_tensor(out=dst, in0=stage_hi[:, j % 2, 0:cols], scalar=negb[:, 0:1],
                                           in1=stage[:, j % 2, 0:cols], op0=ALU.mult, op1=ALU.add).then_inc(s_dve_w, 1)
                else:
                    rows = dst.shape[0]
                    v.tensor_tensor(dst[:, :, C:2 * C], stage[0:rows, j % 2, 0:cols].rearrange("p (c n) -> p c n", n=C),
                                    dst[:, :, 0:C], ALU.subtract).then_inc(s_dve_w, 1)

            def layer_norm(n, j, bank):
                for t in range(TT):
                    last = v.bn_stats(st[j][:, t, :], bank[:, t * C:(t + 1) * C])
                last.then_inc(s_dve_st[j], 1)
                settled(dve)
                dve.wait_ge(s_dve_st[j], n + 1)
                for t in range(TT):
                    last = v.bn_aggr(mv[j][:, t, :], st[j][:, t, :])
                last.then_inc(s_dve_mv[j], 1)
                dve.wait_ge(s_pool_rs[j], n + 1)
                d = 1 + j % 2
                for t in range(TT):
                    last = v.tensor_scalar(V(xn[j][:, t, :], [[C, d], [1, C]]), V(bank[:, t * C:TT * C], [[0, d], [1, C]]),
                                           mv[j][:, t, 0:1], rs[j][:, t:t + 1], ALU.subtract, ALU.mult)
                last.then_inc(s_dve_xn[j], 1)

            def a_pre(n):
                dve.wait_ge(s_pe_xt, n + 1)
                layer_norm(n, 0, mb)
                dve.wait_ge(s_act_y, n + 1)
                for b in range(2):
                    row = ypad[:, 1 + b * (H // 2), 1:1 + W]
                    v.tensor_copy(V(yrep[b], [[P, H // 2], [W, P // W], [1, W]]),
                                  V(row, [[W + 2, H // 2], [0, P // W], [1, W]])).then_inc(s_dve_yr, 1)
                dve.wait_ge(s_pe_xr, K * n)
                for k in range(K):
                    win = ypad[0:C, k // 3:k // 3 + H, k % 3:k % 3 + W]
                    o = dwT[0:C, :].rearrange("p (h w) -> p h w", w=W)
                    if k == 0:
                        v.tensor_scalar(o, win, dww[:, 0:1], vecs[:, 1:2], ALU.mult, ALU.add).then_inc(s_dve_dw, 1)
                    else:
                        dve.wait_ge(s_dve_dw, K * n + k)
                        v.scalar_tensor_tensor(out=o, in0=win, scalar=dww[:, k:k + 1], in1=o, op0=ALU.mult,
                                               op1=ALU.add).then_inc(s_dve_dw, 1)
                for b in range(2):
                    dve.wait_ge(s_pe_v, 2 * n + b + 1)
                    for h in range(NH):
                        o = V(acc[:, 0, h, b * (H // 2):GH * GC * H], [[1, H // 2], [GC * H, GH], [H, GC]])
                        src = V(tb[b][:, h * GH * GC:2 * PIX], [[C, H // 2], [GC, GH], [1, GC]])
                        v.tensor_tensor(o, src, V(gmask[:, :], [[0, H // 2], [1, GH], [0, GC]]), ALU.mult).then_inc(s_dve_bd, 1)

            def a_unit_x(n, k):
                dve.wait_ge(s_act_hat, K * n + k + 1)
                v.tensor_copy(hatr[:, :], hat[:, :]).then_inc(s_dve_hr, 1)
                dve.wait_ge(s_dve_hr, K * n + k + 1)
                if k >= 3:
                    dve.wait_ge(s_pe_t, UNITS * n + (k - 2) * TT * NH)
                v.scalar_tensor_tensor(out=V(hx[:, k % 3, :, :], [[1, NH * PIX]]), in0=hatr[:, :], scalar=negb[:, 0:1],
                                       in1=hat[:, :], op0=ALU.mult, op1=ALU.add).then_inc(s_dve_hx, 1)

            def a_unit_t(n, k):
                if k == 0:
                    dve.wait_ge(s_pool_hy, TT * n + TT)
                    dve.wait_ge(s_act_bh, n + 1)
                    dve.wait_ge(s_pool_bl, n + 1)
                for t in range(TT):
                    for h in range(NH):
                        u = (k * TT + t) * NH + h
                        dve.wait_ge(s_pe_t, UNITS * n + u + 1)
                        o = acc[:, t, h, :] if k == 0 else prod[:, u % 2, :]
                        if u >= TT * NH + 2:
                            dve.wait_ge(s_pool_acc, ADDS * n + u - TT * NH - 1)
                        w = V(hy[:, t, (k * G + h * GH) * H:K * G * H], [[H, GH], [0, GC], [1, H]])
                        v.tensor_tensor(o.rearrange("p (g c q) -> p g c q", g=GH, q=H),
                                        tb[u % 2][:, :].rearrange("p (g c q) -> p g c q", g=GH, q=H), w,
                                        ALU.mult).then_inc(s_dve_p, 1)

            def route(n, m, bx):
                dve.wait_ge(s_act_xh[m], n + 1)
                v.tensor_tensor(xl[m][:, :], bx[:, 0:PIX], xh[m][:, :], ALU.subtract).then_inc(s_dve_xl[m], 1)
                settled(dve)
                dve.wait_ge(s_act_lg[m], n + 1)
                for t in range(TT):
                    last = v.max(mx[m][:, t, :], lg[m][:, t, :])
                last.then_inc(s_dve_mx[m], 1)
                dve.wait_ge(s_dve_mx[m], n + 1)
                v.tensor_scalar(nm[m][:, :], mx[m][:, :, 0], -1.0, None, ALU.mult).then_inc(s_dve_nm[m], 1)
                for t in range(TT):
                    last = v.max_index(ix[m][:, t, :], mx[m][:, t, :], lg[m][:, t, :])
                last.then_inc(s_dve_ix[m], 1)
                base = GT[m] * n
                count = [0]

                def step(ins):
                    count[0] += 1
                    ins.then_inc(s_dve_gt[m], 1)
                    dve.wait_ge(s_dve_gt[m], base + count[0])

                dve.wait_ge(s_dve_ix[m], n + 1)
                step(v.tensor_copy(ixf[m][:, :, :], ix[m][:, :, 0:2]))
                dve.wait_ge(s_act_ex[m], 2 * TT * n + 2 * TT)
                step(v.reciprocal(sm[m][:, :], sm[m][:, :]))
                step(v.tensor_tensor(pk[m][:, :, :], em[m][:, :, :], V(sm[m][:, :], [[1, TT], [0, 2]]), ALU.mult))
                step(v.tensor_tensor(ks_[m][:, :, 0], pk[m][:, :, 0], pk[m][:, :, 1], ALU.add))
                if m == 0:
                    step(v.tensor_scalar(ks_[m][:, :, 0], ks_[m][:, :, 0], 1e-9, None, ALU.add))
                step(v.reciprocal(ks_[m][:, :, 1], ks_[m][:, :, 0]))
                step(v.tensor_tensor(pk[m][:, :, :], pk[m][:, :, :], V(ks_[m][:, :, 1:2], [[2, TT], [0, 2]]), ALU.mult))
                for t in range(TT):
                    for z in range(2):
                        step(v.tensor_scalar(oh[m][:, t, z, :], iota[:, 0:NE[m]], ixf[m][:, t, z:z + 1], pk[m][:, t, z:z + 1],
                                             ALU.is_equal, ALU.mult))
                step(v.tensor_tensor(gt[m][:, :, :], oh[m][:, :, 0, :], oh[m][:, :, 1, :], ALU.add))
                assert count[0] == GT[m]

            def gate_unit(n, m, u, bank):
                dve.wait_ge(s_act_g[m], GU[m] * n + u + 1)
                v.tensor_tensor(xgl[:, u % SLOTS, :], bank[:, :], xgh[:, u % SLOTS, :], ALU.subtract).then_inc(s_dve_g[m], 1)

            def a_tail(n):
                dve.wait_ge(s_pool_acc, ADDS * n + ADDS)
                for t in range(TT):
                    last = v.tensor_reduce(dsum[:, t, :], V(acc[:, t, :, :], [[H, C], [1, H]]), AX, ALU.add)
                last.then_inc(s_dve_dr, 1)
                dve.wait_ge(s_act_z, n + 1)
                v.tensor_tensor(x1T[:, :], xT[:, :], zT[:, :], ALU.add).then_inc(s_dve_x1, 1)
                dve.wait_ge(s_pe_x1t, n + 1)
                layer_norm(n, 1, mb)
                route(n, 0, mb)
                for u in range(GU0):
                    gate_unit(n, 0, u, tb[u % 2])

            def hidden(n, j):
                ch = CH0 if j < PAIRS0 else CH1
                dve.wait_ge(s_act_s, PAIRS * n + j + 1)
                dve.wait_ge(s_pe_h3, PAIRS * n + j + 1)
                dve.wait_ge(s_pool_hl, PAIRS * n + max(0, j - 1))
                v.tensor_tensor(hid[0:ch, j % 2, :], h3[j % 2][0:ch, :], sil[0:ch, j % 2, :], ALU.mult).then_inc(s_dve_hid, 1)

            def attention(n):
                dve.wait_ge(s_pe_x2t, n + 1)
                layer_norm(n, 2, h1[0])
                dve.wait_ge(s_pe_k, n + 1)
                v.tensor_reduce(km[:, :], h1[1][:, :].rearrange("p (c n) -> p c n", c=2), AX, ALU.max, negate=True).then_inc(s_dve_km, 1)
                v.tensor_reduce(qm[:, :], h1[0][:, :].rearrange("p (a d) -> p a d", d=DH), AX, ALU.max).then_inc(s_dve_qm, 1)
                dve.wait_ge(s_dve_qm, n + 1)
                q3 = V(q_s, [[DH, TT * HEADS], [1, DH]])
                v.tensor_tensor(q3, h1[0][:, :].rearrange("p (a d) -> p a d", d=DH), V(qm[:, :], [[1, TT * HEADS], [0, DH]]),
                                ALU.subtract).then_inc(s_dve_qs, 1)
                dve.wait_ge(s_act_q, n + 1)
                v.tensor_reduce(qz[:, :], q3, AX, ALU.add).then_inc(s_dve_qz, 1)
                dve.wait_ge(s_dve_qz, n + 1)
                v.reciprocal(qr[:, :], qz[:, :]).then_inc(s_dve_qr, 1)
                dve.wait_ge(s_dve_qr, n + 1)
                v.tensor_tensor(q3, q3, V(qr[:, :], [[1, TT * HEADS], [0, DH]]), ALU.mult).then_inc(s_dve_qn, 1)
                dve.wait_ge(s_act_k, 2 * n + 2)
                v.reciprocal(kr[:, :, 0], kz[:, :]).then_inc(s_dve_kr, 1)
                dve.wait_ge(s_pe_c, n + 1)
                v.tensor_tensor(cT[:, :, :], h3[0][:, 0:2 * P].rearrange("p (c d) -> p c d", c=2),
                                V(bmask[:, :], [[0, 2], [1, P]]), ALU.mult).then_inc(s_dve_c, 1)
                dve.wait_ge(s_dve_kr, 2 * n + 1)
                v.tensor_scalar(kr[:, :, 1], kr[:, :, 0], SCALE, None, ALU.mult).then_inc(s_dve_kr, 1)
                dve.wait_ge(s_dve_kr, 2 * n + 2)
                dve.wait_ge(s_pe_mm, n + 1)
                v.tensor_tensor(mT[:, :, :], h1[1][:, 0:2 * C].rearrange("p (c o) -> p c o", c=2),
                                V(kr[:, :, 1:2], [[2, 2], [0, C]]), ALU.mult).then_inc(s_dve_m, 1)
                dve.wait_ge(s_pe_at, n + 1)
                v.scalar_tensor_tensor(out=x3T[:, :], in0=yb[0:C, 0:PIX], scalar=vecs[:, 6:7], in1=x2T[:, :], op0=ALU.add,
                                       op1=ALU.add).then_inc(s_dve_x3, 1)
                dve.wait_ge(s_pe_x3t, n + 1)
                layer_norm(n, 3, h1[0])
                route(n, 1, h1[1])
                for u, bank in enumerate((h3[1], h1[0], h1[1], h3[0])):
                    gate_unit(n, 1, u, bank)

            with dve.Fori(0, B) as n:
                a_pre(n)
                a_unit_x(n, 0)
                for k in range(K):
                    if k + 1 < K:
                        a_unit_x(n, k + 1)
                    a_unit_t(n, k)
                a_tail(n)
                for j in range(PAIRS0):
                    hidden(n, j)
                dve.wait_ge(s_act_yl, n + 1)
                v.tensor_tensor(ylo[:, :], ylo[:, :], x1T[:, :], ALU.add).then_inc(s_dve_ys, 1)
                dve.wait_ge(s_dve_ys, n + 1)
                v.tensor_tensor(x2T[:, :], yb[0:C, 0:PIX], ylo[:, :], ALU.add).then_inc(s_dve_x2, 1)
                attention(n)
                for j in range(PAIRS0, PAIRS):
                    if j == PAIRS0 + SLOTS:
                        for u, bank in ((4, h1[0]), (5, h3[0]), (6, h1[1]), (7, h3[1])):
                            gate_unit(n, 1, u, bank)
                    hidden(n, j)
                dve.wait_ge(s_act_yl4, n + 1)
                v.tensor_tensor(ylo[:, :], ylo[:, :], x3T[:, :], ALU.add).then_inc(s_dve_ys4, 1)
                dve.wait_ge(s_dve_ys4, n + 1)
                v.tensor_tensor(outT[:, :], yb[0:C, 0:PIX], ylo[:, :], ALU.add).then_inc(s_dve_x4, 1)

        @block.gpsimd
        def _(pool):
            g = nc.gpsimd
            pool.wait_ge(s_const, n_const)
            pool.wait_ge(s_dve_set, 7)

            def rsqrt(n, j, eps):
                pool.wait_ge(s_dve_mv[j], n + 1)
                g.tensor_tensor(rs[j][:, :], mv[j][:, :, 1], epst[:, eps, :], ALU.add).then_inc(s_pool_ve[j], 1)
                pool.wait_ge(s_pool_ve[j], n + 1)
                g.tensor_tensor(rs[j][:, :], rs[j][:, :], mhalf[:, :], ALU.pow).then_inc(s_pool_rs[j], 1)

            def a_pre(n):
                rsqrt(n, 0, 0)
                pool.wait_ge(s_act_bh, n + 1)
                g.tensor_tensor(bdl[:, :, :], acc[:, 0, :, :], bdh[:, :, :], ALU.subtract).then_inc(s_pool_bl, 1)
                pool.wait_ge(s_act_ym, n + 1)
                for t in range(TT):
                    g.tensor_tensor(V(hy[:, t, :], [[H, K * G], [1, H]]), V(ym[:, t, :], [[1, K * G], [0, H]]),
                                    V(iota[:, :], [[0, K * G], [1, H]]), ALU.subtract).then_inc(s_pool_dy, 1)
                for t in range(TT):
                    pool.wait_ge(s_act_hy, TT * n + t + 1)
                    w = V(hy[:, t, :], [[H, K * G], [1, H]])
                    g.tensor_tensor(w, w, V(ym[:, t, K * G:2 * K * G], [[1, K * G], [0, H]]), ALU.mult).then_inc(s_pool_hy, 1)

            def a_unit(n, k):
                for t in range(TT):
                    for h in range(NH):
                        u = (k * TT + t) * NH + h
                        a = u - TT * NH
                        pool.wait_ge(s_dve_p, UNITS * n + u + 1)
                        if a >= TT * NH:
                            pool.wait_ge(s_pool_acc, ADDS * n + a - TT * NH + 1)
                        g.tensor_tensor(acc[:, t, h, :], acc[:, t, h, :], prod[:, u % 2, :], ALU.add).then_inc(s_pool_acc, 1)

            def gated(n, m, us):
                for u in us:
                    if u == 0:
                        pool.wait_ge(s_dve_gt[m], GT[m] * (n + 1))
                        pool.wait_ge(s_pe_g[1 - m], (GU0 * (n + 1), GU1 * n)[1 - m])
                    elif u >= 2:
                        pool.wait_ge(s_pe_g[m], GU[m] * n + u - 1)
                    g.tensor_tensor(xg[:, u % 2, :, :, :], V(xn[1 + 2 * m][:, :, :], [[2 * C, TT], [0, 2], [1, 2 * C]]),
                                    V(gt[m][:, :, 2 * u:NE[m]], [[NE[m], TT], [1, 2], [0, 2 * C]]), ALU.mult).then_inc(s_pool_xg[m], 1)

            def low(n, j):
                ch = CH0 if j < PAIRS0 else CH1
                pool.wait_ge(s_act_hh, PAIRS * n + j + 1)
                g.tensor_tensor(hl[0:ch, j % 2, :], hid[0:ch, j % 2, :], hh[0:ch, j % 2, :], ALU.subtract).then_inc(s_pool_hl, 1)

            with pool.Fori(0, B) as n:
                a_pre(n)
                for k in range(1, K):
                    a_unit(n, k)
                rsqrt(n, 1, 1)
                gated(n, 0, range(GU0))
                for j in range(PAIRS0):
                    low(n, j)
                rsqrt(n, 2, 0)
                rsqrt(n, 3, 1)
                gated(n, 1, range(SLOTS))
                for j in range(PAIRS0, PAIRS):
                    if j == PAIRS0 + SLOTS:
                        gated(n, 1, range(SLOTS, GU1))
                    low(n, j)


def lay_out(i):
    import numpy as np
    a = {k: np.asarray(v) for k, v in i.items()}
    f = np.float32
    L = {}
    T = np.ascontiguousarray
    L["x"] = T(a["x"].reshape(B, C, PIX))
    L["cv1T"], L["opT"], L["cv2T"] = (T(a[f"L0_conv_{n}_w"].T) for n in ("cv1", "op", "cv2"))
    L["vpT"] = T(np.concatenate([a["L0_conv_vp_w"].T, a["L0_conv_vp_b"][None]]))
    L["dww"] = T(a["L0_conv_dw_w"].reshape(C, K))
    for n, k in (("cv1_b", "L0_conv_cv1_b"), ("dw_b", "L0_conv_dw_b"), ("bn_g", "L0_conv_bn_g"), ("bn_b", "L0_conv_bn_b"),
                 ("bn_m", "L0_conv_bn_m"), ("bn_v", "L0_conv_bn_v"), ("b_out", "L1_conv_b_out")):
        L[n] = T(a[k].reshape(C, 1))
    om = np.concatenate([a["L0_conv_om_w"], a["L0_conv_om_b"][:, None]], 1)[:G * K * 3].reshape(G, 3 * K, C + 1)
    oy, ox, omk = om[:, 0:2 * K:2], om[:, 1:2 * K:2], om[:, 2 * K:]
    L["omymT"] = T(np.concatenate([oy.transpose(2, 1, 0).reshape(C + 1, K * G), omk.transpose(2, 1, 0).reshape(C + 1, K * G)], 1))
    one, zero = np.ones(K * G), np.zeros(K * G)
    ky = np.repeat(np.arange(K) // 3 - 1, G)
    big = ox.reshape(NH, GH, K, C + 1).transpose(3, 2, 0, 1)[:, :, :, None, :, None]
    L["omxT"] = T(np.broadcast_to(big, (C + 1, K, NH, 2, GH, W)).reshape(C + 1, K * NH * P))
    kx = np.broadcast_to((np.arange(K) % 3 - 1)[:, None, None, None, None] - np.arange(W), (K, NH, 2, GH, W)).reshape(-1)
    L["omxC"] = np.stack([np.ones(kx.size), np.zeros(kx.size), kx]).astype(f)
    L["omymC"] = np.stack([np.concatenate([zero, zero]), np.concatenate([one, zero]), np.concatenate([ky, zero])]).astype(f)
    pix = np.arange(PIX)
    L["pixC"] = np.stack([np.ones(PIX), pix % W, pix // W, np.ones(PIX)]).astype(f)
    r = np.arange(P)
    L["ident"] = np.eye(P, dtype=f)
    L["negb"] = -(r >= P // 2).astype(f)[:, None]
    L["gmask"] = ((r[:, None] // W) % GH == np.arange(GH)).astype(f)
    L["iota"] = np.broadcast_to(np.arange(W, dtype=f), (P, W)).copy()
    L["bmask"] = (r[:, None] // DH == r // DH).astype(f)
    pad = CPE0 * CH0 - HID0

    def up0(w):
        return T(np.pad(w, ((0, 0), (0, pad), (0, 0))).transpose(2, 0, 1).reshape(C, -1))
    L["w1T"], L["w3T"] = up0(a["L0_ffn_w1"]), up0(a["L0_ffn_w3"])
    w2 = np.pad(a["L0_ffn_w2"], ((0, 0), (0, 0), (0, pad))).reshape(E0, C, CPE0, CH0)
    L["w2T"] = T(w2.transpose(3, 0, 2, 1).reshape(CH0, NC0, C))
    L["rwT"] = T(a["L0_ffn_router_w"].T)
    qkv = a["L1_conv_w_qkv"].T
    L["wqT"], L["wkT"], L["wvT"] = (T(qkv[:, j * HD:(j + 1) * HD]) for j in range(3))
    L["woT"] = T(a["L1_conv_w_out"].T.reshape(2, P, C).transpose(1, 0, 2))
    L["gwT"] = T(np.concatenate([a["L1_ffn_gate_w"], a["L1_ffn_gate_b"][None]]))
    L["u1T"], L["u2T"] = (T(a[f"L1_ffn_w{j}"].transpose(1, 0, 2).reshape(C, -1)) for j in (1, 2))
    L["u3T"] = T(a["L1_ffn_w3"].transpose(1, 0, 2))
    return L


def kernel(**inputs):
    import concourse.bacc as bacc
    from concourse.bass_utils import run_bass_kernel_spmd

    arrays = lay_out(inputs)
    nc = bacc.Bacc("TRN2", target_bir_lowering=False, num_devices=1)
    A = {k: nc.dram_tensor("in_" + k, v.shape, mybir.dt.from_np(v.dtype), kind="ExternalInput").ap() for k, v in arrays.items()}
    out = nc.dram_tensor("out", (B, C, PIX), mybir.dt.float32, kind="ExternalOutput").ap()
    build(nc, A, out)
    r = run_bass_kernel_spmd(nc, [{"in_" + k: v for k, v in arrays.items()}], core_ids=[0])
    return r.results[0]["out"].reshape(B, C, H, W)
```

```python
from contextlib import ExitStack

import concourse.bass as bass
from concourse import mybir

B, C, H, W = 8, 64, 16, 16
PIX = H * W
P = 128
TT = PIX // P
G, GC, K = 8, 8, 9
GH = 4
NH = G // GH
E0, HID0, CH0 = 8, 682, 114
CPE0 = -(-HID0 // CH0)
E1, CH1 = 16, 128
NC0, NC1 = E0 * CPE0, E1
PAIRS0, PAIRS1 = NC0 // 2, NC1 // 2
PAIRS = PAIRS0 + PAIRS1
PPE0 = CPE0 // 2
UNITS = K * TT * NH
ADDS = UNITS - TT * NH
GU0, GU1 = E0 // 2, E1 // 2
SLOTS = 4
HEADS, DH = 8, 32
HD = HEADS * DH
SCALE = DH ** -0.5
AUG = C + 4
STAGE = 1024
LAG = 2
RING, HALVES = 4, 2


WEAVE = {
    "pe": """
        abbbaabbbb abbbbbbabb abbbbbbbba abbbbaabbb baabbbabab babbaaabbb babbbbbaba aababaabab aabbbaaaba ababaaaaba
        aabaabbbba ababaaabbb bbabbababa bbbbababba aaa
        """,
    "act": """
        bbbbbaabbb bbbbbaabbb babbbbabbb baabbbbbbb babbbbbbbb abbbbbbbba bbbababbba bbbbabbbbb bbbbbabbba abbbbbbaab
        abaaaa
        """,
    "dve": """
        abbabababb abbabbbbba abaaabbbaa bbaababbaa bbababaaba aabaabbaba ababaabaab abbaaaaaba bbbaababab aabaababab
        bbaabbabaa abaaaa
        """,
    "pool": """
        abbbbbbbbb babbbbbbbb abbabbabba aabaaaaaaa aabaaaaaaa aaabaaaaba aabbbabbb
        """,
}


def stream_a():
    pre = [("x_tokens",), ("stats", 0), ("norm", 0), ("xn_channels",), ("cv1",), ("y",), ("values",), ("depthwise",),
           ("diagonal",), ("offsets",), ("row_distances",), ("row_weights",)]
    taps = []
    for k in range(K):
        taps.append(("columns", k))
        if k:
            taps += [("tap" if k > 1 else "first_tap", k - 1, q) for q in range(TT * NH)]
    taps += [("tap", K - 1, q) for q in range(TT * NH)]
    tail = [("sampled",), ("op",), ("cv2",), ("x1",), ("stats", 1), ("norm", 1), ("stack", 0), ("logits", 0), ("top", 0),
            ("exp", 0), ("gates", 0)]
    return pre + taps + tail + [("gate_unit", 0, u) for u in range(GU0)]


def stream_b():
    def pairs(first, end, late=[]):
        out = []
        for j in range(first, end):
            out += [("up", j)] + ([("split", j - 1)] if j > first else [])
            out += late[j - first:j - first + 1] + ([("down", j - LAG)] if j >= first + LAG else [])
        return out + [("down", end - LAG), ("split", end - 1)] + [("down", j) for j in range(end - LAG + 1, end)]
    att = [("x2",), ("x2_tokens",), ("stats", 2), ("norm", 2), ("xn2_channels",), ("qkv",), ("maxima",), ("exps",),
           ("k_tokens",), ("context",), ("q_norm",), ("q_channels",), ("mix",), ("attend",), ("x3_tokens",), ("stats", 3), ("norm", 3),
           ("stack", 1), ("logits", 1), ("top", 1), ("exp", 1), ("gates", 1)]
    att += [("gate_unit", 1, u) for u in range(SLOTS)]
    late = [("none",)] + [("gate_unit", 1, u) for u in range(SLOTS, GU1)]
    return pairs(0, PAIRS0) + att + pairs(PAIRS0, PAIRS, late) + [("x4",)]


def merge(*lists):
    out = sorted((((i + 1) / (len(l) + 1), m, i, s) for m, l in enumerate(lists) for i, s in enumerate(l)), key=lambda x: x[:3])
    return [s for _, _, _, s in out]


def start_order(n_pieces):
    steps = [("a",) + s for s in stream_a()]
    return merge(steps[:-GU0], [("w", "piece", j) for j in range(n_pieces)]) + steps[-GU0:]


def steady_order(weave, steps):
    left = {s: iter([(s,) + x for x in stream if x[0] in steps]) for s, stream in (("a", stream_a()), ("b", stream_b()))}
    order = [next(left[s]) for s in "".join(weave.split())]
    assert not any(list(x) for x in left.values())
    return order


class Image:

    def __init__(self, reg, plus, times=1):
        self.reg, self.plus, self.times = reg, plus, times

    def __add__(self, other):
        return Image(self.reg, self.plus + other, self.times)

    def __sub__(self, other):
        return self + -other

    def __mul__(self, other):
        return Image(self.reg, self.plus * other, self.times * other)

    __radd__, __rmul__ = __add__, __mul__


def count(x):
    if isinstance(x, int):
        return x
    value = x.reg if x.times == 1 else x.reg * x.times
    return value if x.plus == 0 else value + x.plus if x.plus > 0 else value - -x.plus


def build(nc, A, out):
    f32, f32r, u32 = mybir.dt.float32, mybir.dt.float32r, mybir.dt.uint32
    ACT, ALU, AX = mybir.ActivationFunctionType, mybir.AluOpType, mybir.AxisListType.X

    def V(base, dims):
        return bass.AP(base.tensor, base.offset, [list(base.ap[0])] + [list(d) for d in dims])

    with ExitStack() as ctx:
        def sb(name, shape, dt=f32):
            return ctx.enter_context(nc.sbuf_tensor("sb_" + name, shape, dt))

        def ps(name, shape):
            return ctx.enter_context(nc.psum_tensor("ps_" + name, shape, f32))

        def sem(name):
            return ctx.enter_context(nc.semaphore(name))

        w1s = sb("w1s", [P, NC0 * CH0], f32r)
        w3s = sb("w3s", [P, NC0 * CH0], f32r)
        w2s = sb("w2s", [P, NC0, 2 * C], f32r)
        u1s = sb("u1s", [P, NC1 * CH1], f32r)
        u2s = sb("u2s", [P, NC1 * CH1], f32r)
        u3s = sb("u3s", [P, NC1, 2 * C], f32r)
        def parts(tile, widths):
            at, views = 0, []
            for w in widths:
                views.append(tile[:, at:at + w])
                at += w
            return views

        wide = sb("wide", [P, A["wide"].shape[1]])
        ident, negb, gmask, iota, bmask, wo = parts(wide, (P, 1, GH, W, P, 2 * C))
        wo = wo.rearrange("p (c o) -> p c o", c=2)
        flat = sb("flat", [C, A["flat"].shape[1]])
        cv1, opw, cv2, dww, vecs, rw, wq, wk, wv = parts(flat, (C, C, C, K, 7, E0, HD, HD, HD))
        vp = sb("vp", [C + 1, C])
        bns = sb("bns", [C, 4])
        omx = sb("omx", [AUG, K * NH * P])
        omym = sb("omym", [AUG, 2 * K * G])
        gw = sb("gw", [C + 1, E1])
        epst = sb("epst", [P, 2, TT])
        mhalf = sb("mhalf", [P, TT])

        xT = sb("xT", [C, PIX])
        xnT = sb("xnT", [C, PIX])
        ypad = sb("ypad", [C + 1, H + 2, W + 2])
        dwT = sb("dwT", [AUG, PIX])
        bdh = sb("bdh", [P, NH, GH * GC * H], f32r)
        bdl = sb("bdl", [P, NH, GH * GC * H], f32r)
        ym = sb("ym", [P, TT, 2 * K * G])
        hy = sb("hy", [P, TT, K * G * H])
        hat = sb("hat", [P, NH * PIX])
        hatr = sb("hatr", [P, NH * PIX], f32r)
        hx = sb("hx", [P, 3, NH, PIX], f32r)
        prod = sb("prod", [P, 2, GH * GC * H])
        acc = sb("acc", [P, TT, NH, GH * GC * H])
        yrep = [acc[0:C + 1, 1, :, :].rearrange("p h n -> p (h n)"), prod[0:C + 1, :, :].rearrange("p a n -> p (a n)")]
        dsum = sb("dsum", [P, TT, C])
        oT = sb("oT", [C, PIX])
        dT = zT = xnT
        x1T = sb("x1T", [C, PIX])

        hid = sb("hid", [P, RING, 2 * PIX])
        hh = sb("hh", [P, HALVES, 2 * PIX], f32r)
        hl = sb("hl", [P, HALVES, 2 * PIX], f32r)
        xgh = sb("xgh", [P, SLOTS, 2 * PIX], f32r)
        xgl = sb("xgl", [P, SLOTS, 2 * PIX], f32r)
        NE = (E0, E1)
        st = [sb(f"st{j}", [P, TT, 6]) for j in range(4)]
        mv = [sb(f"mv{j}", [P, TT, 2]) for j in range(4)]
        rs = [sb(f"rs{j}", [P, TT]) for j in range(4)]
        xn = [sb(f"xn{j}", [P, TT, (1 + j % 2) * C]) for j in range(4)]
        xh = [sb(f"xh{m}", [P, PIX], f32r) for m in range(2)]
        xl = [sb(f"xl{m}", [P, PIX], f32r) for m in range(2)]
        xf = [sb(f"xf{m}", [C + 1, PIX]) for m in range(2)]
        lg = [sb(f"lg{m}", [P, TT, NE[m]]) for m in range(2)]
        ex = [sb(f"ex{m}", [P, TT, NE[m]]) for m in range(2)]
        mx = [sb(f"mx{m}", [P, TT, 8]) for m in range(2)]
        ix = [sb(f"ix{m}", [P, TT, 8], u32) for m in range(2)]
        ixf = [sb(f"ixf{m}", [P, TT, 2]) for m in range(2)]
        nm = [sb(f"nm{m}", [P, TT]) for m in range(2)]
        sm = [sb(f"sm{m}", [P, TT]) for m in range(2)]
        em = [sb(f"em{m}", [P, TT, 2]) for m in range(2)]
        pk = [sb(f"pk{m}", [P, TT, 2]) for m in range(2)]
        ks_ = [sb(f"ks{m}", [P, TT, 2]) for m in range(2)]
        oh = [sb(f"oh{m}", [P, TT, 2, NE[m]]) for m in range(2)]
        gt = [sb(f"gt{m}", [P, TT, NE[m]]) for m in range(2)]
        xg = sb("xg", [P, 2, TT, 2, 2 * C])

        ylo = sb("ylo", [C, PIX])
        x2T = sb("x2T", [C, PIX])
        xn2T = ylo
        qT = sb("qT", [P, 2, PIX])
        qm = sb("qm", [P, TT * HEADS])
        qz = sb("qz", [P, TT * HEADS])
        qr = sb("qr", [P, TT * HEADS])
        km = sb("km", [P, 2])
        kz = sb("kz", [P, 2])
        kr = sb("kr", [P, 2, 2])
        cT = sb("cT", [P, 2, P])
        mT = sb("mT", [P, 2, C])
        x3T = sb("x3T", [C, PIX])
        outT = ylo
        q_s, k_s, v_s, kT_s = (hid[:, j, :] for j in range(4))

        h1 = [ps(f"h1_{j}", [P, 2 * PIX]) for j in range(2)]
        h3 = [ps(f"h3_{j}", [P, 2 * PIX]) for j in range(2)]
        yb = ps("y", [P, PIX * 2])
        tb = [ps(f"t_{j}", [P, 2 * PIX]) for j in range(2)]
        mb = ps("m", [P, 2 * PIX])

        s_const = sem("s_const")
        s_stage = [sem(f"s_stage{j}") for j in range(2)]
        s_act_whi = sem("s_act_whi")
        s_dve_w = sem("s_dve_w")
        s_dve_set = sem("s_dve_set")
        s_dve_bn = sem("s_dve_bn")
        s_act_bn = sem("s_act_bn")
        s_ld_x = sem("s_ld_x")
        s_st = sem("s_st")
        s_pe_xt, s_pe_xnt, s_pe_y, s_pe_v, s_pe_ym = map(sem, ("s_pe_xt", "s_pe_xnt", "s_pe_y", "s_pe_v", "s_pe_ym"))
        s_pe_xr, s_pe_t = sem("s_pe_xr"), sem("s_pe_t")
        s_pe_dt, s_pe_o, s_pe_z, s_pe_x1t = map(sem, ("s_pe_dt", "s_pe_o", "s_pe_z", "s_pe_x1t"))
        s_act_xnt, s_act_y, s_act_bh, s_act_ym = map(sem, ("s_act_xnt", "s_act_y", "s_act_bh", "s_act_ym"))
        s_act_hyabs, s_act_hy = sem("s_act_hyabs"), sem("s_act_hy")
        s_act_abs, s_act_hat = sem("s_act_abs"), sem("s_act_hat")
        s_act_dt, s_act_o, s_act_z = map(sem, ("s_act_dt", "s_act_o", "s_act_z"))
        s_dve_yr = sem("s_dve_yr")
        s_dve_dw, s_dve_bd = sem("s_dve_dw"), sem("s_dve_bd")
        s_dve_hr, s_dve_hx = sem("s_dve_hr"), sem("s_dve_hx")
        s_dve_p, s_dve_dr = sem("s_dve_p"), sem("s_dve_dr")
        s_dve_x1 = sem("s_dve_x1")
        s_dve_bl, s_dve_dy = sem("s_dve_bl"), sem("s_dve_dy")
        s_pool_hy, s_pool_acc = map(sem, ("s_pool_hy", "s_pool_acc"))
        s_dve_st = [sem(f"s_dve_st{j}") for j in range(4)]
        s_dve_mv = [sem(f"s_dve_mv{j}") for j in range(4)]
        s_pool_ve = [sem(f"s_pool_ve{j}") for j in range(4)]
        s_pool_rs = [sem(f"s_pool_rs{j}") for j in range(4)]
        s_dve_xn = [sem(f"s_dve_xn{j}") for j in range(4)]
        def two(name):
            return [sem(f"{name}{m}") for m in range(2)]
        s_pe_xs, s_act_xh, s_act_xf, s_dve_xl = two("s_pe_xs"), two("s_act_xh"), two("s_act_xf"), two("s_dve_xl")
        s_pe_lg, s_act_lg = two("s_pe_lg"), two("s_act_lg")
        s_dve_mx, s_dve_ix, s_dve_nm = two("s_dve_mx"), two("s_dve_ix"), two("s_dve_nm")  
        s_act_ex = two("s_act_ex")
        s_dve_gt = two("s_dve_gt")
        s_act_xg, s_pe_g, s_act_g, s_dve_g = two("s_act_xg"), two("s_pe_g"), two("s_act_g"), two("s_dve_g")
        GT, GU = (12, 11), (GU0, GU1)
        s_pe_h1, s_pe_h3, s_pe_y2 = map(sem, ("s_pe_h1", "s_pe_h3", "s_pe_down"))
        s_act_s, s_act_hh, s_dve_hid, s_pool_hl = map(sem, ("s_act_s", "s_act_hh", "s_dve_hid", "s_pool_hl"))
        s_act_yl, s_dve_ys, s_dve_x2, s_dve_ys4, s_dve_x4, s_act_yl4 = map(sem, ("s_act_yl", "s_dve_ys", "s_dve_x2", "s_dve_ys4", "s_dve_x4", "s_act_yl4"))
        (s_pe_x2t, s_pe_xn2t, s_act_xn2t, s_pe_q, s_pe_k, s_pe_vv, s_act_v, s_dve_qm, s_dve_qs, s_act_q,
         s_dve_qz, s_dve_qr, s_dve_qn, s_pe_qt, s_act_qt, s_dve_km, s_act_k, s_pe_kt, s_act_kt, s_pe_c,
         s_dve_c, s_dve_kr, s_pe_mm, s_dve_m, s_pe_at, s_dve_x3, s_pe_x3t) = map(sem, (
            "s_pe_x2t", "s_pe_xn2t", "s_act_xn2t", "s_pe_q", "s_pe_k", "s_pe_vv", "s_act_v", "s_dve_qm", "s_dve_qs", "s_act_q",
            "s_dve_qz", "s_dve_qr", "s_dve_qn", "s_pe_qt", "s_act_qt", "s_dve_km", "s_act_k", "s_pe_kt", "s_act_kt", "s_pe_c",
            "s_dve_c", "s_dve_kr", "s_pe_mm", "s_dve_m", "s_pe_at", "s_dve_x3", "s_pe_x3t"))

        pieces = []
        half = CPE0 * CH0
        for name, dst in (("w1T", w1s), ("w3T", w3s)):
            for e in range(E0):
                pieces.append((A[name][:, e * half:(e + 1) * half], half, "rows", dst[:, e * half:(e + 1) * half]))
        per = STAGE // C
        for c in range(0, NC0, per):
            pieces.append((A["w2T"][:, c:c + per, :], STAGE, "cols", w2s[0:CH0, c:c + per, :]))
        for name, dst in (("u1T", u1s), ("u2T", u2s)):
            for c in range(0, NC1 * CH1, STAGE):
                pieces.append((A[name][:, c:c + STAGE], STAGE, "rows", dst[:, c:c + STAGE]))
        for c in range(0, NC1, per):
            pieces.append((A["u3T"][:, c:c + per, :], STAGE, "cols", u3s[:, c:c + per, :]))
        stage = [hid[:, 2 * j:2 * j + 2, :].rearrange("p a n -> p (a n)") for j in range(2)]
        stage_hi = [xgh[:, 2 * j:2 * j + 2, :].rearrange("p a n -> p (a n)") for j in range(2)]
        staged = [0, 0]
        piece_ready = []
        for j, (_, _, kind, _) in enumerate(pieces):
            staged[j % 2] += 32 if kind == "rows" else 16
            piece_ready.append(staged[j % 2])

        consts = [(wide[:, :], "wide"), (flat[:, :], "flat"), (vp[:, :], "vpT"), (gw[:, :], "gwT"), (omym[:, :], "omymT"),
                  (omx[:, :], "omxT"), (dwT[C:AUG, :], "pixC")]
        n_const = 16 * len(consts)

        gate_bank = ([tb[u % 2] for u in range(GU0)],
                     [h1[0], h3[0], h1[1], h3[1], h1[0], h1[1], h1[0], h1[1]])
        first, final = start_order(len(pieces)), [("b",) + s for s in stream_b()]

        block = ctx.enter_context(nc.Block())

        def settled(eng):
            eng.wait_ge(s_const, n_const)

        @block.sync
        def _(sp):
            sp.dma_start(xT[:, :], A["x"][0]).then_inc(s_ld_x, 16)
            for dst, name in consts[0::2]:
                sp.dma_start(dst, A[name]).then_inc(s_const, 16)
            for j, (src, cols, kind, _dst) in enumerate(pieces):
                if j >= 2:
                    sp.wait_ge(s_dve_w, j - 1)
                if kind == "rows":
                    for r in range(2):
                        sp.dma_start(stage[j % 2][C * r:C * r + C, 0:cols], src).then_inc(s_stage[j % 2], 16)
                else:
                    rows = src.shape[0]
                    sp.dma_start(stage[j % 2][0:rows, 0:cols], src.rearrange("p c n -> p (c n)")).then_inc(s_stage[j % 2], 16)
            with sp.Fori(1, B) as n:
                sp.wait_ge(s_dve_x1, n)
                sp.dma_start(xT[:, :], A["x"][n]).then_inc(s_ld_x, 16)
                sp.wait_ge(s_dve_x4, n + 1)
                sp.dma_start(out[n - 1], outT[:, :]).then_inc(s_st, 16)
            sp.wait_ge(s_dve_x4, B + 1)
            sp.dma_start(out[B - 1], outT[:, :]).then_inc(s_st, 16)
            sp.wait_ge(s_st, 16 * B + 16)

        @block.tensor
        def _(pe):
            mm, tr = nc.tensor.matmul, nc.tensor.transpose

            def transposes_to_tokens(bank, src):
                for t in range(TT):
                    last = tr(bank[:, t * C:(t + 1) * C], src[:, t * P:(t + 1) * P], ident[0:C, 0:C])
                return last

            def transposes_to_channels(bank, src):
                for t in range(TT):
                    last = tr(bank[0:C, t * P:(t + 1) * P], src[:, t, :], ident[:, :])
                return last

            def x_tokens(n):
                pe.wait_ge(s_ld_x, count(16 * n + 16))
                for t in range(TT):
                    last = mm(mb[:, t * C:(t + 1) * C], xT[:, t * P:(t + 1) * P], ident[0:C, 0:C], start=True, stop=True)
                last.then_inc(s_pe_xt, 1)

            def xn_channels(n):
                pe.wait_ge(s_dve_xn[0], count(n + 1))
                for t in range(TT):
                    last = mm(mb[0:C, t * P:(t + 1) * P], xn[0][:, t, :], ident[:, :], start=True, stop=True)
                last.then_inc(s_pe_xnt, 1)

            def cv1_product(n):
                settled(pe)
                pe.wait_ge(s_act_xnt, count(n + 1))
                mm(mb[0:C, 0:PIX], cv1[:, :], xnT[:, :], start=True, stop=True).then_inc(s_pe_y, 1)

            def values(n):
                for b in range(2):
                    pe.wait_ge(s_dve_yr, count(2 * n + b + 1))
                    for r in range(H // 2):
                        last = mm(tb[b][:, r * C:(r + 1) * C], yrep[b][:, r * P:(r + 1) * P], vp[:, :],
                                  start=True, stop=True)
                    last.then_inc(s_pe_v, 1)

            def offsets(n):
                pe.wait_ge(s_dve_dw, count(K * n + K))
                for t in range(TT):
                    last = mm(mb[:, t * 2 * K * G:(t + 1) * 2 * K * G], dwT[:, t * P:(t + 1) * P], omym[:, :],
                              start=True, stop=True)
                last.then_inc(s_pe_ym, 1)

            def columns(n, k):
                if k == 0:
                    pe.wait_ge(s_act_ym, count(n + 1))
                else:
                    pe.wait_ge(s_act_abs, count(K * n + k))
                for h in range(NH):
                    o = (k * NH + h) * P
                    last = mm(mb[:, h * PIX:(h + 1) * PIX], omx[:, o:o + P], dwT[:, :], start=True, stop=True)
                last.then_inc(s_pe_xr, 1)

            def tap(n, k, q):
                t, h = divmod(q, NH)
                u = k * TT * NH + q
                if q == 0:
                    pe.wait_ge(s_dve_hx, count(K * n + k + 1))
                if u == 0:
                    pe.wait_ge(s_act_bh, count(n + 1))
                    pe.wait_ge(s_dve_bl, count(n + 1))
                if u >= 2:
                    pe.wait_ge(s_dve_p, count(UNITS * n + u - 1))
                w = hx[:, k % 3, h, t * P:(t + 1) * P]
                mm(tb[u % 2][:, :], w, bdh[:, h, :], start=True, stop=False)
                mm(tb[u % 2][:, :], w, bdl[:, h, :], start=False, stop=True).then_inc(s_pe_t, 1)

            def sampled(n):
                settled(pe)
                pe.wait_ge(s_dve_dr, count(n + 1))
                transposes_to_channels(mb, dsum).then_inc(s_pe_dt, 1)

            def op_product(n):
                settled(pe)
                pe.wait_ge(s_act_dt, count(n + 1))
                mm(mb[0:C, 0:PIX], opw[:, :], dT[:, :], start=True, stop=True).then_inc(s_pe_o, 1)

            def cv2_product(n):
                settled(pe)
                pe.wait_ge(s_act_o, count(n + 1))
                mm(mb[0:C, 0:PIX], cv2[:, :], oT[:, :], start=True, stop=True).then_inc(s_pe_z, 1)

            def x1(n):
                settled(pe)
                pe.wait_ge(s_dve_x1, count(n + 1))
                transposes_to_tokens(mb, x1T).then_inc(s_pe_x1t, 1)

            def stack(n, m):
                bx = (mb, h1[1])[m]
                pe.wait_ge(s_dve_xn[1 + 2 * m], count(n + 1))
                for t in range(TT):
                    last = tr(bx[:, t * P:(t + 1) * P], xn[1 + 2 * m][:, t, :], ident[:, :])
                last.then_inc(s_pe_xs[m], 1)

            def logits(n, m):
                bl = (mb, h3[0])[m]
                pe.wait_ge(s_act_xf[m], count(n + 1))
                pe.wait_ge(s_dve_xl[m], count(n + 1))
                rows, w = (C, rw) if m == 0 else (C + 1, gw)
                for t in range(TT):
                    last = mm(bl[:, t * NE[m]:(t + 1) * NE[m]], xf[m][0:rows, t * P:(t + 1) * P], w[:, :],
                              start=True, stop=True)
                last.then_inc(s_pe_lg[m], 1)

            def gate_unit(n, m, u):
                pe.wait_ge(s_act_xg[m], count(GU[m] * n + u + 1))
                if m == 0 and u >= 2:
                    pe.wait_ge(s_dve_g[0], count(GU0 * n + u - 1))
                if m == 1 and u >= SLOTS:
                    pe.wait_ge(s_act_s, count(PAIRS * n + PAIRS0 + u - SLOTS + 1))
                bank = gate_bank[m][u]
                for e in range(2):
                    for t in range(TT):
                        last = tr(bank[:, (e * TT + t) * P:(e * TT + t + 1) * P],
                                  xg[:, u % 2, t, e, :], ident[:, :])
                last.then_inc(s_pe_g[m], 1)

            def up(n, j):
                first, m = (0, 0) if j < PAIRS0 else (PAIRS0, 1)
                ch = (CH0, CH1)[m]
                wa, wb = ((w1s, w3s), (u1s, u2s))[m]
                if j == 0:
                    pe.wait_ge(s_dve_g[0], count(GU0 * n + 1))
                    pe.wait_ge(s_act_xh[0], count(n + 1))
                if PAIRS0 <= j < PAIRS0 + 2:
                    pe.wait_ge(s_dve_g[1], count(GU1 * n + (1, 3)[j - PAIRS0]))
                elif j >= PAIRS0 + 2:
                    pe.wait_ge(s_dve_g[1], count(GU1 * n + min(GU1, SLOTS + j - PAIRS0 - 1)))
                if j % PAIRS0 >= 2:
                    pe.wait_ge(s_act_s, count(PAIRS * n + j - 1))
                for c in range(2):
                    o = (2 * (j - first) + c) * ch
                    d = h1[j % 2][0:ch, c * PIX:(c + 1) * PIX]
                    mm(d, wa[:, o:o + ch], xh[m][:, :], start=True, stop=False)
                    last = mm(d, wa[:, o:o + ch], xl[m][:, :], start=False, stop=True)
                last.then_inc(s_pe_h1, 1)
                if 0 < j < PAIRS0 and j % (2 * PPE0) == 0:
                    pe.wait_ge(s_dve_g[0], count(GU0 * n + j // (2 * PPE0) + 1))
                if PAIRS0 <= j < PAIRS0 + 2:
                    pe.wait_ge(s_dve_g[1], count(GU1 * n + (2, 4)[j - PAIRS0]))
                elif j >= 2:
                    pe.wait_ge(s_dve_hid, count(PAIRS * n + j - 1))
                for c in range(2):
                    o = (2 * (j - first) + c) * ch
                    e = j // PPE0 if m == 0 else 2 * (j - first) + c
                    slot, x = (e // 2) % SLOTS, slice((e % 2) * PIX, (e % 2 + 1) * PIX)
                    d = h3[j % 2][0:ch, c * PIX:(c + 1) * PIX]
                    mm(d, wb[:, o:o + ch], xgh[:, slot, x], start=True, stop=False)
                    last = mm(d, wb[:, o:o + ch], xgl[:, slot, x], start=False, stop=True)
                last.then_inc(s_pe_h3, 1)

            def down(n, j):
                first, end, m = (0, PAIRS0, 0) if j < PAIRS0 else (PAIRS0, PAIRS, 1)
                ch, w = ((CH0, w2s), (CH1, u3s))[m]
                pe.wait_ge(s_pool_hl, count(PAIRS * n + j + 1))
                if j == 0:
                    pe.wait_ge(s_dve_x4, count(n + 1))
                for c in range(2):
                    for z, part in enumerate((hh, hl)):
                        last = mm(yb[:, 0:PIX], w[0:ch, 2 * (j - first) + c, :], part[0:ch, j % HALVES, c * PIX:(c + 1) * PIX],
                                  start=(j == first and c == 0 and z == 0), stop=(j == end - 1 and c == 1 and z == 1))
                last.then_inc(s_pe_y2, 1)

            def x2_tokens(n):
                settled(pe)
                pe.wait_ge(s_dve_x2, count(n + 1))
                transposes_to_tokens(h1[0], x2T).then_inc(s_pe_x2t, 1)

            def xn2_channels(n):
                settled(pe)
                pe.wait_ge(s_dve_xn[2], count(n + 1))
                transposes_to_channels(h1[1], xn[2]).then_inc(s_pe_xn2t, 1)

            def qkv(n):
                pe.wait_ge(s_act_xn2t, count(n + 1))
                for t in range(TT):
                    last = mm(h1[0][:, t * HD:(t + 1) * HD], xn2T[:, t * P:(t + 1) * P], wq[:, :], start=True, stop=True)
                last.then_inc(s_pe_q, 1)
                for c in range(2):
                    last = mm(h1[1][:, c * PIX:(c + 1) * PIX], wk[:, c * P:(c + 1) * P], xn2T[:, :], start=True, stop=True)
                last.then_inc(s_pe_k, 1)
                for t in range(TT):
                    last = mm(h3[0][:, t * HD:(t + 1) * HD], xn2T[:, t * P:(t + 1) * P], wv[:, :], start=True, stop=True)
                last.then_inc(s_pe_vv, 1)

            def k_tokens(n):
                pe.wait_ge(s_act_k, count(2 * n + 2))
                for t in range(TT):
                    for c in range(2):
                        last = tr(h3[1][:, t * HD + c * P:t * HD + (c + 1) * P],
                                  k_s[:, c * PIX + t * P:c * PIX + (t + 1) * P], ident[:, :])
                last.then_inc(s_pe_kt, 1)

            def context(n):
                pe.wait_ge(s_act_v, count(n + 1))
                pe.wait_ge(s_act_kt, count(n + 1))
                for c in range(2):
                    for t in range(TT):
                        o = t * HD + c * P
                        last = mm(h3[0][:, c * P:(c + 1) * P], v_s[:, o:o + P], kT_s[:, o:o + P], start=(t == 0), stop=(t == TT - 1))
                last.then_inc(s_pe_c, 1)

            def q_channels(n):
                pe.wait_ge(s_dve_qn, count(n + 1))
                for c in range(2):
                    for t in range(TT):
                        last = tr(h1[0][:, c * PIX + t * P:c * PIX + (t + 1) * P],
                                  q_s[:, t * HD + c * P:t * HD + (c + 1) * P], ident[:, :])
                last.then_inc(s_pe_qt, 1)

            def mix(n):
                pe.wait_ge(s_dve_c, count(n + 1))
                for c in range(2):
                    last = mm(h1[1][:, c * C:(c + 1) * C], cT[:, c, :], wo[:, c, :], start=True, stop=True)
                last.then_inc(s_pe_mm, 1)

            def attend(n):
                pe.wait_ge(s_dve_m, count(n + 1))
                pe.wait_ge(s_act_qt, count(n + 1))
                for c in range(2):
                    last = mm(yb[0:C, 0:PIX], mT[:, c, :], qT[:, c, :], start=(c == 0), stop=(c == 1))
                last.then_inc(s_pe_at, 1)

            def x3_tokens(n):
                settled(pe)
                pe.wait_ge(s_dve_x3, count(n + 1))
                transposes_to_tokens(h1[0], x3T).then_inc(s_pe_x3t, 1)

            steps = {"x_tokens": x_tokens, "xn_channels": xn_channels, "cv1": cv1_product, "values": values, "offsets": offsets,
                     "columns": columns, "first_tap": tap, "tap": tap, "sampled": sampled, "op": op_product, "cv2": cv2_product, "x1": x1,
                     "stack": stack, "logits": logits, "gate_unit": gate_unit, "up": up, "down": down,
                     "x2_tokens": x2_tokens, "xn2_channels": xn2_channels, "qkv": qkv, "k_tokens": k_tokens,
                     "context": context, "q_channels": q_channels, "mix": mix, "attend": attend, "x3_tokens": x3_tokens}

            def walk(order, images):
                for stream, name, *args in order:
                    if name in steps:
                        steps[name](images[stream], *args)

            pe.wait_ge(s_const, n_const)
            pe.wait_ge(s_dve_set, 7)
            walk(first, {"a": 0, "w": 0})
            pe.wait_ge(s_dve_w, len(pieces))
            with pe.Fori(1, B) as i:
                walk(steady_order(WEAVE["pe"], steps), {"a": Image(i, 0), "b": Image(i, -1)})
            walk(final, {"b": B - 1})

        @block.scalar
        def _(act):
            af = nc.scalar.activation

            for dst, name in consts[1::2]:
                act.dma_start(dst, A[name]).then_inc(s_const, 16)
            act.wait_ge(s_const, n_const)
            act.wait_ge(s_dve_bn, 1)
            af(bns[:, 1:2], bns[:, 0:1], ACT.Sqrt).then_inc(s_act_bn, 1)

            def piece(n, j):
                _src, cols, kind, dst = pieces[j]
                act.wait_ge(s_stage[j % 2], piece_ready[j])
                if kind == "rows":
                    if j >= 2:
                        act.wait_ge(s_dve_w, j - 1)
                    af(stage_hi[j % 2][:, 0:cols], stage[j % 2][:, 0:cols], ACT.Copy).then_inc(s_act_whi, 1)
                else:
                    rows = dst.shape[0]
                    af(dst[:, :, 0:C], stage[j % 2][0:rows, 0:cols].rearrange("p (c n) -> p c n", n=C),
                       ACT.Copy).then_inc(s_act_whi, 1)

            def xn_channels(n):
                act.wait_ge(s_pe_xnt, count(n + 1))
                af(xnT[:, :], mb[0:C, 0:PIX], ACT.Copy).then_inc(s_act_xnt, 1)

            def cv1_bias(n):
                act.wait_ge(s_pe_y, count(n + 1))
                af(ypad[0:C, 1:1 + H, 1:1 + W], mb[0:C, 0:PIX].rearrange("p (h w) -> p h w", w=W),
                   ACT.Identity, bias=vecs[:, 0:1]).then_inc(s_act_y, 1)

            def diagonal(n):
                act.wait_ge(s_dve_bd, count(4 * n + 4))
                af(bdh[:, :, :], acc[:, 0, :, :], ACT.Copy).then_inc(s_act_bh, 1)

            def offsets(n):
                act.wait_ge(s_pe_ym, count(n + 1))
                af(ym[:, :, :], mb[:, 0:TT * 2 * K * G].rearrange("p (t c) -> p t c", t=TT), ACT.Copy).then_inc(s_act_ym, 1)

            def row_distances(n):
                for t in range(TT):
                    act.wait_ge(s_dve_dy, count(TT * n + t + 1))
                    af(hy[:, t, :], hy[:, t, :], ACT.Abs).then_inc(s_act_hyabs, 1)

            def row_weights(n):
                for t in range(TT):
                    act.wait_ge(s_act_hyabs, count(TT * n + t + 1))
                    af(hy[:, t, :], hy[:, t, :], ACT.Relu, scale=-1.0, bias=1.0).then_inc(s_act_hy, 1)

            def columns(n, k):
                act.wait_ge(s_pe_xr, count(K * n + k + 1))
                if k > 0 or not isinstance(n, int):
                    act.wait_ge(s_dve_hx, count(K * n + k))
                af(hat[:, :], mb[:, :], ACT.Abs).then_inc(s_act_abs, 1)
                act.wait_ge(s_act_abs, count(K * n + k + 1))
                af(hat[:, :], hat[:, :], ACT.Relu, scale=-1.0, bias=1.0).then_inc(s_act_hat, 1)

            def sampled(n):
                act.wait_ge(s_pe_dt, count(n + 1))
                af(dT[:, :], mb[0:C, 0:PIX], ACT.Copy).then_inc(s_act_dt, 1)

            def op_product(n):
                act.wait_ge(s_pe_o, count(n + 1))
                af(oT[:, :], mb[0:C, 0:PIX], ACT.Copy).then_inc(s_act_o, 1)

            def cv2_silu(n):
                act.wait_ge(s_pe_z, count(n + 1))
                af(zT[:, :], mb[0:C, 0:PIX], ACT.Silu, scale=bns[:, 2:3], bias=bns[:, 3:4]).then_inc(s_act_z, 1)

            def stack(n, m):
                bx = (mb, h1[1])[m]
                act.wait_ge(s_pe_xs[m], count(n + 1))
                if m == 0 and not isinstance(n, int):
                    act.wait_ge(s_pe_h1, count(PAIRS * n - PAIRS1))
                af(xf[m][0:C, :], bx[0:C, 0:PIX], ACT.Copy).then_inc(s_act_xf[m], 1)
                af(xh[m][:, :], bx[:, 0:PIX], ACT.Copy).then_inc(s_act_xh[m], 1)

            def logits(n, m):
                bl = (mb, h3[0])[m]
                act.wait_ge(s_pe_lg[m], count(n + 1))
                af(lg[m][:, :, :], bl[:, 0:TT * NE[m]].rearrange("p (t e) -> p t e", t=TT), ACT.Copy).then_inc(s_act_lg[m], 1)

            def exp_top(n, m):
                act.wait_ge(s_act_lg[m], count(n + 1))
                act.wait_ge(s_dve_nm[m], count(n + 1))
                for t in range(TT):
                    af(ex[m][:, t, :], lg[m][:, t, :], ACT.Exp, bias=nm[m][:, t:t + 1],
                       accum_out=sm[m][:, t:t + 1]).then_inc(s_act_ex[m], 1)
                    af(em[m][:, t, :], mx[m][:, t, 0:2], ACT.Exp, bias=nm[m][:, t:t + 1]).then_inc(s_act_ex[m], 1)

            def gate_unit(n, m, u):
                if u == 0:
                    act.wait_ge(s_dve_gt[m], count(GT[m] * n + GT[m]))
                    if m == 1:
                        act.wait_ge(s_pe_g[0], count(GU0 * n + GU0))
                    elif not isinstance(n, int):
                        act.wait_ge(s_pe_g[1], count(GU1 * n))
                elif u >= 2:
                    act.wait_ge(s_pe_g[m], count(GU[m] * n + u - 1))
                for t in range(TT):
                    for e in range(2):
                        last = af(xg[:, u % 2, t, e, :], xn[1 + 2 * m][:, t, :], ACT.Copy, scale=gt[m][:, t, 2 * u + e:2 * u + e + 1])
                last.then_inc(s_act_xg[m], 1)
                if m == 0 and isinstance(n, int):
                    act.wait_ge(s_dve_w, len(pieces))
                elif m == 0:
                    act.wait_ge(s_pe_h3, count(PAIRS * n - (SLOTS - 1 - u)))
                act.wait_ge(s_pe_g[m], count(GU[m] * n + u + 1))
                af(xgh[:, u % SLOTS, :], gate_bank[m][u][:, :], ACT.Copy).then_inc(s_act_g[m], 1)

            def silu(n, j):
                ch = CH0 if j < PAIRS0 else CH1
                act.wait_ge(s_pe_h1, count(PAIRS * n + j + 1))
                if j % PAIRS0 >= RING:
                    act.wait_ge(s_pool_hl, count(PAIRS * n + j - RING + 1))
                af(hid[0:ch, j % RING, :], h1[j % 2][0:ch, :], ACT.Silu).then_inc(s_act_s, 1)

            def high(n, j):
                ch = CH0 if j < PAIRS0 else CH1
                act.wait_ge(s_dve_hid, count(PAIRS * n + j + 1))
                if j % PAIRS0 >= HALVES:
                    act.wait_ge(s_pe_y2, count(PAIRS * n + j - HALVES + 1))
                af(hh[0:ch, j % HALVES, :], hid[0:ch, j % RING, :], ACT.Copy).then_inc(s_act_hh, 1)

            def x2(n):
                act.wait_ge(s_pe_y2, count(PAIRS * n + PAIRS0))
                act.wait_ge(s_st, count(16 * n + 16))
                af(ylo[:, :], yb[C:P, 0:PIX], ACT.Copy).then_inc(s_act_yl, 1)

            def x4(n):
                act.wait_ge(s_pe_y2, count(PAIRS * n + PAIRS))
                af(ylo[:, :], yb[C:P, 0:PIX], ACT.Copy).then_inc(s_act_yl4, 1)

            def xn2_channels(n):
                act.wait_ge(s_pe_xn2t, count(n + 1))
                af(xn2T[:, :], h1[1][0:C, 0:PIX], ACT.Copy).then_inc(s_act_xn2t, 1)

            def exps(n):
                act.wait_ge(s_dve_km, count(n + 1))
                for c in range(2):
                    af(k_s[:, c * PIX:(c + 1) * PIX], h1[1][:, c * PIX:(c + 1) * PIX], ACT.Exp, bias=km[:, c:c + 1],
                       accum_out=kz[:, c:c + 1]).then_inc(s_act_k, 1)
                act.wait_ge(s_pe_vv, count(n + 1))
                af(v_s, h3[0][:, :], ACT.Copy).then_inc(s_act_v, 1)
                act.wait_ge(s_dve_qs, count(n + 1))
                af(q_s, q_s, ACT.Exp).then_inc(s_act_q, 1)

            def k_tokens(n):
                act.wait_ge(s_pe_kt, count(n + 1))
                af(kT_s, h3[1][:, :], ACT.Copy).then_inc(s_act_kt, 1)

            def q_channels(n):
                act.wait_ge(s_pe_qt, count(n + 1))
                af(qT[:, :, :], h1[0][:, :].rearrange("p (c n) -> p c n", c=2), ACT.Copy).then_inc(s_act_qt, 1)

            steps = {"piece": piece, "xn_channels": xn_channels, "cv1": cv1_bias, "diagonal": diagonal, "offsets": offsets,
                     "row_distances": row_distances, "row_weights": row_weights, "columns": columns, "sampled": sampled,
                     "op": op_product, "cv2": cv2_silu, "stack": stack, "logits": logits, "exp": exp_top,
                     "gate_unit": gate_unit, "up": silu, "split": high, "x2": x2, "x4": x4, "xn2_channels": xn2_channels,
                     "exps": exps, "k_tokens": k_tokens, "q_channels": q_channels}

            def walk(order, images):
                for stream, name, *args in order:
                    if name in steps:
                        steps[name](images[stream], *args)

            walk(first, {"a": 0, "w": 0})
            with act.Fori(1, B) as i:
                walk(steady_order(WEAVE["act"], steps), {"a": Image(i, 0), "b": Image(i, -1)})
            walk(final, {"b": B - 1})

        @block.vector
        def _(dve):
            v = nc.vector
            v.memset(ypad[0:C, :, :], 0.0).then_inc(s_dve_set, 1)
            v.memset(ypad[C:C + 1, :, :], 1.0).then_inc(s_dve_set, 1)
            v.memset(xf[1][C:C + 1, :], 1.0).then_inc(s_dve_set, 1)
            v.memset(epst[:, 0, :], 1e-6).then_inc(s_dve_set, 1)
            v.memset(epst[:, 1, :], 1e-5).then_inc(s_dve_set, 1)
            v.memset(mhalf[:, :], -0.5).then_inc(s_dve_set, 1)
            v.memset(xf[0][C:C + 1, :], 1.0).then_inc(s_dve_set, 1)
            dve.wait_ge(s_const, n_const)
            v.tensor_scalar(bns[:, 0:1], vecs[:, 5:6], 1e-5, None, ALU.add).then_inc(s_dve_bn, 1)
            dve.wait_ge(s_act_bn, 1)
            v.reciprocal(bns[:, 0:1], bns[:, 1:2]).then_inc(s_dve_bn, 1)
            dve.wait_ge(s_dve_bn, 2)
            v.tensor_tensor(bns[:, 2:3], vecs[:, 2:3], bns[:, 0:1], ALU.mult).then_inc(s_dve_bn, 1)
            dve.wait_ge(s_dve_bn, 3)
            v.tensor_tensor(bns[:, 1:2], vecs[:, 4:5], bns[:, 2:3], ALU.mult).then_inc(s_dve_bn, 1)
            dve.wait_ge(s_dve_bn, 4)
            v.tensor_tensor(bns[:, 3:4], vecs[:, 3:4], bns[:, 1:2], ALU.subtract).then_inc(s_dve_bn, 1)

            def piece(n, j):
                _src, cols, kind, dst = pieces[j]
                dve.wait_ge(s_act_whi, j + 1)
                if kind == "rows":
                    v.scalar_tensor_tensor(out=dst, in0=stage_hi[j % 2][:, 0:cols], scalar=negb[:, 0:1],
                                           in1=stage[j % 2][:, 0:cols], op0=ALU.mult, op1=ALU.add).then_inc(s_dve_w, 1)
                else:
                    rows = dst.shape[0]
                    v.tensor_tensor(dst[:, :, C:2 * C], stage[j % 2][0:rows, 0:cols].rearrange("p (c n) -> p c n", n=C),
                                    dst[:, :, 0:C], ALU.subtract).then_inc(s_dve_w, 1)

            def stats(n, j):
                bank, ready = ((mb, s_pe_xt), (mb, s_pe_x1t), (h1[0], s_pe_x2t), (h1[0], s_pe_x3t))[j]
                dve.wait_ge(ready, count(n + 1))
                for t in range(TT):
                    last = v.bn_stats(st[j][:, t, :], bank[:, t * C:(t + 1) * C])
                last.then_inc(s_dve_st[j], 1)
                settled(dve)
                dve.wait_ge(s_dve_st[j], count(n + 1))
                for t in range(TT):
                    last = v.bn_aggr(mv[j][:, t, :], st[j][:, t, :])
                last.then_inc(s_dve_mv[j], 1)

            def norm(n, j):
                bank = mb if j < 2 else h1[0]
                dve.wait_ge(s_pool_rs[j], count(n + 1))
                d = 1 + j % 2
                for t in range(TT):
                    last = v.tensor_scalar(V(xn[j][:, t, :], [[C, d], [1, C]]), V(bank[:, t * C:TT * C], [[0, d], [1, C]]),
                                           mv[j][:, t, 0:1], rs[j][:, t:t + 1], ALU.subtract, ALU.mult)
                last.then_inc(s_dve_xn[j], 1)

            def y_rows(n):
                dve.wait_ge(s_act_y, count(n + 1))
                for b in range(2):
                    row = ypad[:, 1 + b * (H // 2), 1:1 + W]
                    v.tensor_copy(V(yrep[b], [[P, H // 2], [W, P // W], [1, W]]),
                                  V(row, [[W + 2, H // 2], [0, P // W], [1, W]])).then_inc(s_dve_yr, 1)

            def depthwise(n):
                for k in range(K):
                    win = ypad[0:C, k // 3:k // 3 + H, k % 3:k % 3 + W]
                    o = dwT[0:C, :].rearrange("p (h w) -> p h w", w=W)
                    if k == 0:
                        v.tensor_scalar(o, win, dww[:, 0:1], vecs[:, 1:2], ALU.mult, ALU.add).then_inc(s_dve_dw, 1)
                    else:
                        dve.wait_ge(s_dve_dw, count(K * n + k))
                        v.scalar_tensor_tensor(out=o, in0=win, scalar=dww[:, k:k + 1], in1=o, op0=ALU.mult,
                                               op1=ALU.add).then_inc(s_dve_dw, 1)

            def diagonal(n):
                for b in range(2):
                    dve.wait_ge(s_pe_v, count(2 * n + b + 1))
                    for h in range(NH):
                        o = V(acc[:, 0, h, b * (H // 2):GH * GC * H], [[1, H // 2], [GC * H, GH], [H, GC]])
                        src = V(tb[b][:, h * GH * GC:2 * PIX], [[C, H // 2], [GC, GH], [1, GC]])
                        v.tensor_tensor(o, src, V(gmask[:, :], [[0, H // 2], [1, GH], [0, GC]]), ALU.mult).then_inc(s_dve_bd, 1)
                dve.wait_ge(s_dve_bd, count(4 * n + 4))
                dve.wait_ge(s_act_bh, count(n + 1))
                v.tensor_tensor(bdl[:, :, :], acc[:, 0, :, :], bdh[:, :, :], ALU.subtract).then_inc(s_dve_bl, 1)

            def row_distances(n):
                dve.wait_ge(s_act_ym, count(n + 1))
                for t in range(TT):
                    v.tensor_tensor(V(hy[:, t, :], [[H, K * G], [1, H]]), V(ym[:, t, :], [[1, K * G], [0, H]]),
                                    V(iota[:, :], [[0, K * G], [1, H]]), ALU.subtract).then_inc(s_dve_dy, 1)

            def columns(n, k):
                dve.wait_ge(s_act_hat, count(K * n + k + 1))
                v.tensor_copy(hatr[:, :], hat[:, :]).then_inc(s_dve_hr, 1)
                dve.wait_ge(s_dve_hr, count(K * n + k + 1))
                if k >= 3:
                    dve.wait_ge(s_pe_t, count(UNITS * n + (k - 2) * TT * NH))
                v.scalar_tensor_tensor(out=V(hx[:, k % 3, :, :], [[1, NH * PIX]]), in0=hatr[:, :], scalar=negb[:, 0:1],
                                       in1=hat[:, :], op0=ALU.mult, op1=ALU.add).then_inc(s_dve_hx, 1)

            def tap(n, k, q):
                t, h = divmod(q, NH)
                u = k * TT * NH + q
                if u == 0:
                    dve.wait_ge(s_pool_hy, count(TT * n + TT))
                    dve.wait_ge(s_dve_bl, count(n + 1))
                dve.wait_ge(s_pe_t, count(UNITS * n + u + 1))
                o = acc[:, t, h, :] if k == 0 else prod[:, u % 2, :]
                if u >= TT * NH + 2:
                    dve.wait_ge(s_pool_acc, count(ADDS * n + u - TT * NH - 1))
                w = V(hy[:, t, (k * G + h * GH) * H:K * G * H], [[H, GH], [0, GC], [1, H]])
                v.tensor_tensor(o.rearrange("p (g c q) -> p g c q", g=GH, q=H),
                                tb[u % 2][:, :].rearrange("p (g c q) -> p g c q", g=GH, q=H), w,
                                ALU.mult).then_inc(s_dve_p, 1)

            def sampled(n):
                dve.wait_ge(s_pool_acc, count(ADDS * n + ADDS))
                for t in range(TT):
                    last = v.tensor_reduce(dsum[:, t, :], V(acc[:, t, :, :], [[H, C], [1, H]]), AX, ALU.add)
                last.then_inc(s_dve_dr, 1)

            def x1(n):
                dve.wait_ge(s_act_z, count(n + 1))
                if not isinstance(n, int):
                    dve.wait_ge(s_dve_x2, count(1 * n))
                v.tensor_tensor(x1T[:, :], xT[:, :], zT[:, :], ALU.add).then_inc(s_dve_x1, 1)

            def stack(n, m):
                bx = (mb, h1[1])[m]
                dve.wait_ge(s_act_xh[m], count(n + 1))
                v.tensor_tensor(xl[m][:, :], bx[:, 0:PIX], xh[m][:, :], ALU.subtract).then_inc(s_dve_xl[m], 1)

            def top(n, m):
                settled(dve)
                dve.wait_ge(s_act_lg[m], count(n + 1))
                for t in range(TT):
                    last = v.max(mx[m][:, t, :], lg[m][:, t, :])
                last.then_inc(s_dve_mx[m], 1)
                dve.wait_ge(s_dve_mx[m], count(n + 1))
                v.tensor_scalar(nm[m][:, :], mx[m][:, :, 0], -1.0, None, ALU.mult).then_inc(s_dve_nm[m], 1)
                for t in range(TT):
                    last = v.max_index(ix[m][:, t, :], mx[m][:, t, :], lg[m][:, t, :])
                last.then_inc(s_dve_ix[m], 1)

            def gates(n, m):
                done = [0]

                def step(ins):
                    done[0] += 1
                    ins.then_inc(s_dve_gt[m], 1)
                    dve.wait_ge(s_dve_gt[m], count(GT[m] * n + done[0]))

                dve.wait_ge(s_dve_ix[m], count(n + 1))
                step(v.tensor_copy(ixf[m][:, :, :], ix[m][:, :, 0:2]))
                dve.wait_ge(s_act_ex[m], count(2 * TT * n + 2 * TT))
                step(v.reciprocal(sm[m][:, :], sm[m][:, :]))
                step(v.tensor_tensor(pk[m][:, :, :], em[m][:, :, :], V(sm[m][:, :], [[1, TT], [0, 2]]), ALU.mult))
                step(v.tensor_tensor(ks_[m][:, :, 0], pk[m][:, :, 0], pk[m][:, :, 1], ALU.add))
                if m == 0:
                    step(v.tensor_scalar(ks_[m][:, :, 0], ks_[m][:, :, 0], 1e-9, None, ALU.add))
                step(v.reciprocal(ks_[m][:, :, 1], ks_[m][:, :, 0]))
                step(v.tensor_tensor(pk[m][:, :, :], pk[m][:, :, :], V(ks_[m][:, :, 1:2], [[2, TT], [0, 2]]), ALU.mult))
                for t in range(TT):
                    for z in range(2):
                        done[0] += 1
                        v.tensor_scalar(oh[m][:, t, z, :], iota[:, 0:NE[m]], ixf[m][:, t, z:z + 1], pk[m][:, t, z:z + 1],
                                        ALU.is_equal, ALU.mult).then_inc(s_dve_gt[m], 1)
                dve.wait_ge(s_dve_gt[m], count(GT[m] * n + done[0]))
                done[0] += 1
                v.tensor_tensor(gt[m][:, :, :], oh[m][:, :, 0, :], oh[m][:, :, 1, :], ALU.add).then_inc(s_dve_gt[m], 1)
                assert done[0] == GT[m]

            def gate_unit(n, m, u):
                dve.wait_ge(s_act_g[m], count(GU[m] * n + u + 1))
                v.tensor_tensor(xgl[:, u % SLOTS, :], gate_bank[m][u][:, :], xgh[:, u % SLOTS, :],
                                ALU.subtract).then_inc(s_dve_g[m], 1)

            def up(n, j):
                ch = CH0 if j < PAIRS0 else CH1
                dve.wait_ge(s_act_s, count(PAIRS * n + j + 1))
                dve.wait_ge(s_pe_h3, count(PAIRS * n + j + 1))
                v.tensor_tensor(hid[0:ch, j % RING, :], h3[j % 2][0:ch, :], hid[0:ch, j % RING, :], ALU.mult).then_inc(s_dve_hid, 1)

            def x2(n):
                dve.wait_ge(s_act_yl, count(n + 1))
                v.tensor_tensor(ylo[:, :], ylo[:, :], x1T[:, :], ALU.add).then_inc(s_dve_ys, 1)
                dve.wait_ge(s_dve_ys, count(n + 1))
                v.tensor_tensor(x2T[:, :], yb[0:C, 0:PIX], ylo[:, :], ALU.add).then_inc(s_dve_x2, 1)

            def x4(n):
                dve.wait_ge(s_act_yl4, count(n + 1))
                v.tensor_tensor(ylo[:, :], ylo[:, :], x3T[:, :], ALU.add).then_inc(s_dve_ys4, 1)
                dve.wait_ge(s_dve_ys4, count(n + 1))
                v.tensor_tensor(outT[:, :], yb[0:C, 0:PIX], ylo[:, :], ALU.add).then_inc(s_dve_x4, 1)

            q3 = V(q_s, [[DH, TT * HEADS], [1, DH]])

            def maxima(n):
                dve.wait_ge(s_pe_k, count(n + 1))
                v.tensor_reduce(km[:, :], h1[1][:, :].rearrange("p (c n) -> p c n", c=2), AX, ALU.max, negate=True).then_inc(s_dve_km, 1)
                v.tensor_reduce(qm[:, :], h1[0][:, :].rearrange("p (a d) -> p a d", d=DH), AX, ALU.max).then_inc(s_dve_qm, 1)
                dve.wait_ge(s_dve_qm, count(n + 1))
                v.tensor_tensor(q3, h1[0][:, :].rearrange("p (a d) -> p a d", d=DH), V(qm[:, :], [[1, TT * HEADS], [0, DH]]),
                                ALU.subtract).then_inc(s_dve_qs, 1)

            def q_norm(n):
                dve.wait_ge(s_act_q, count(n + 1))
                v.tensor_reduce(qz[:, :], q3, AX, ALU.add).then_inc(s_dve_qz, 1)
                dve.wait_ge(s_dve_qz, count(n + 1))
                v.reciprocal(qr[:, :], qz[:, :]).then_inc(s_dve_qr, 1)
                dve.wait_ge(s_dve_qr, count(n + 1))
                v.tensor_tensor(q3, q3, V(qr[:, :], [[1, TT * HEADS], [0, DH]]), ALU.mult).then_inc(s_dve_qn, 1)
                dve.wait_ge(s_act_k, count(2 * n + 2))
                v.reciprocal(kr[:, :, 0], kz[:, :]).then_inc(s_dve_kr, 1)

            def context(n):
                dve.wait_ge(s_pe_c, count(n + 1))
                v.tensor_tensor(cT[:, :, :], h3[0][:, 0:2 * P].rearrange("p (c d) -> p c d", c=2),
                                V(bmask[:, :], [[0, 2], [1, P]]), ALU.mult).then_inc(s_dve_c, 1)

            def mix(n):
                dve.wait_ge(s_dve_kr, count(2 * n + 1))
                v.tensor_scalar(kr[:, :, 1], kr[:, :, 0], SCALE, None, ALU.mult).then_inc(s_dve_kr, 1)
                dve.wait_ge(s_dve_kr, count(2 * n + 2))
                dve.wait_ge(s_pe_mm, count(n + 1))
                v.tensor_tensor(mT[:, :, :], h1[1][:, 0:2 * C].rearrange("p (c o) -> p c o", c=2),
                                V(kr[:, :, 1:2], [[2, 2], [0, C]]), ALU.mult).then_inc(s_dve_m, 1)

            def attend(n):
                dve.wait_ge(s_pe_at, count(n + 1))
                v.scalar_tensor_tensor(out=x3T[:, :], in0=yb[0:C, 0:PIX], scalar=vecs[:, 6:7], in1=x2T[:, :], op0=ALU.add,
                                       op1=ALU.add).then_inc(s_dve_x3, 1)

            steps = {"piece": piece, "stats": stats, "norm": norm, "y": y_rows, "depthwise": depthwise, "diagonal": diagonal,
                     "row_distances": row_distances, "columns": columns, "first_tap": tap, "tap": tap, "sampled": sampled, "x1": x1,
                     "stack": stack, "top": top, "gates": gates, "gate_unit": gate_unit, "up": up, "x2": x2, "x4": x4,
                     "maxima": maxima, "q_norm": q_norm, "context": context, "mix": mix, "attend": attend}

            def walk(order, images):
                for stream, name, *args in order:
                    if name in steps:
                        steps[name](images[stream], *args)

            walk(first, {"a": 0, "w": 0})
            with dve.Fori(1, B) as i:
                walk(steady_order(WEAVE["dve"], steps), {"a": Image(i, 0), "b": Image(i, -1)})
            walk(final, {"b": B - 1})

        @block.gpsimd
        def _(pool):
            g = nc.gpsimd
            pool.wait_ge(s_const, n_const)
            pool.wait_ge(s_dve_set, 7)
            pool.sem_inc(s_st, 16)
            pool.sem_inc(s_dve_x4, 1)

            def rsqrt(n, j):
                pool.wait_ge(s_dve_mv[j], count(n + 1))
                g.tensor_tensor(rs[j][:, :], mv[j][:, :, 1], epst[:, j % 2, :], ALU.add).then_inc(s_pool_ve[j], 1)
                pool.wait_ge(s_pool_ve[j], count(n + 1))
                g.tensor_tensor(rs[j][:, :], rs[j][:, :], mhalf[:, :], ALU.pow).then_inc(s_pool_rs[j], 1)

            def row_weights(n):
                for t in range(TT):
                    pool.wait_ge(s_act_hy, count(TT * n + t + 1))
                    w = V(hy[:, t, :], [[H, K * G], [1, H]])
                    g.tensor_tensor(w, w, V(ym[:, t, K * G:2 * K * G], [[1, K * G], [0, H]]), ALU.mult).then_inc(s_pool_hy, 1)

            def tap(n, k, q):
                t, h = divmod(q, NH)
                u = k * TT * NH + q
                a = u - TT * NH
                pool.wait_ge(s_dve_p, count(UNITS * n + u + 1))
                if a >= TT * NH:
                    pool.wait_ge(s_pool_acc, count(ADDS * n + a - TT * NH + 1))
                g.tensor_tensor(acc[:, t, h, :], acc[:, t, h, :], prod[:, u % 2, :], ALU.add).then_inc(s_pool_acc, 1)

            def low(n, j):
                ch = CH0 if j < PAIRS0 else CH1
                pool.wait_ge(s_act_hh, count(PAIRS * n + j + 1))
                g.tensor_tensor(hl[0:ch, j % HALVES, :], hid[0:ch, j % RING, :], hh[0:ch, j % HALVES, :],
                                ALU.subtract).then_inc(s_pool_hl, 1)

            steps = {"stats": rsqrt, "row_weights": row_weights, "tap": tap, "split": low}

            def walk(order, images):
                for stream, name, *args in order:
                    if name in steps:
                        steps[name](images[stream], *args)

            walk(first, {"a": 0, "w": 0})
            with pool.Fori(1, B) as i:
                walk(steady_order(WEAVE["pool"], steps), {"a": Image(i, 0), "b": Image(i, -1)})
            walk(final, {"b": B - 1})


def lay_out(i):
    import numpy as np
    a = {k: np.asarray(v) for k, v in i.items()}
    f = np.float32
    L = {}
    T = np.ascontiguousarray
    L["x"] = T(a["x"].reshape(B, C, PIX))
    L["vpT"] = T(np.concatenate([a["L0_conv_vp_w"].T, a["L0_conv_vp_b"][None]]))
    vecs = [a[k][:, None] for k in ("L0_conv_cv1_b", "L0_conv_dw_b", "L0_conv_bn_g", "L0_conv_bn_b", "L0_conv_bn_m",
                                    "L0_conv_bn_v", "L1_conv_b_out")]
    L["flat"] = T(np.concatenate([a[f"L0_conv_{n}_w"].T for n in ("cv1", "op", "cv2")] + [a["L0_conv_dw_w"].reshape(C, K)]
                                 + vecs + [a["L0_ffn_router_w"].T, a["L1_conv_w_qkv"].T], 1))
    om = np.concatenate([a["L0_conv_om_w"], a["L0_conv_om_b"][:, None]], 1)[:G * K * 3].reshape(G, 3 * K, C + 1)
    oy, ox, omk = om[:, 0:2 * K:2], om[:, 1:2 * K:2], om[:, 2 * K:]
    omym = np.concatenate([oy.transpose(2, 1, 0).reshape(C + 1, K * G), omk.transpose(2, 1, 0).reshape(C + 1, K * G)], 1)
    one, zero = np.ones(K * G), np.zeros(K * G)
    ky = np.repeat(np.arange(K) // 3 - 1, G)
    big = ox.reshape(NH, GH, K, C + 1).transpose(3, 2, 0, 1)[:, :, :, None, :, None]
    omx = T(np.broadcast_to(big, (C + 1, K, NH, 2, GH, W)).reshape(C + 1, K * NH * P))
    kx = np.broadcast_to((np.arange(K) % 3 - 1)[:, None, None, None, None] - np.arange(W), (K, NH, 2, GH, W)).reshape(-1)
    L["omxT"] = np.concatenate([omx, np.stack([np.ones(kx.size), np.zeros(kx.size), kx]).astype(f)])
    L["omymT"] = np.concatenate([omym, np.stack([np.concatenate(x) for x in ((zero, zero), (one, zero), (ky, zero))]).astype(f)])
    pix = np.arange(PIX)
    L["pixC"] = np.stack([np.ones(PIX), pix % W, pix // W, np.ones(PIX)]).astype(f)
    r = np.arange(P)
    fixed = [np.eye(P), -(r >= P // 2)[:, None].astype(f), (r[:, None] // W) % GH == np.arange(GH),
             np.broadcast_to(np.arange(W), (P, W)), r[:, None] // DH == r // DH]
    L["wide"] = np.concatenate([x.astype(f) for x in fixed]
                               + [a["L1_conv_w_out"].T.reshape(2, P, C).transpose(1, 0, 2).reshape(P, 2 * C)], 1)
    pad = CPE0 * CH0 - HID0

    def up0(w):
        return T(np.pad(w, ((0, 0), (0, pad), (0, 0))).transpose(2, 0, 1).reshape(C, -1))
    L["w1T"], L["w3T"] = up0(a["L0_ffn_w1"]), up0(a["L0_ffn_w3"])
    w2 = np.pad(a["L0_ffn_w2"], ((0, 0), (0, 0), (0, pad))).reshape(E0, C, CPE0, CH0)
    L["w2T"] = T(w2.transpose(3, 0, 2, 1).reshape(CH0, NC0, C))
    L["gwT"] = T(np.concatenate([a["L1_ffn_gate_w"], a["L1_ffn_gate_b"][None]]))
    L["u1T"], L["u2T"] = (T(a[f"L1_ffn_w{j}"].transpose(1, 0, 2).reshape(C, -1)) for j in (1, 2))
    L["u3T"] = T(a["L1_ffn_w3"].transpose(1, 0, 2))
    return L


def kernel(**inputs):
    import concourse.bacc as bacc
    from concourse.bass_utils import run_bass_kernel_spmd

    arrays = lay_out(inputs)
    nc = bacc.Bacc("TRN2", target_bir_lowering=False, num_devices=1)
    A = {k: nc.dram_tensor("in_" + k, v.shape, mybir.dt.from_np(v.dtype), kind="ExternalInput").ap() for k, v in arrays.items()}
    out = nc.dram_tensor("out", (B, C, PIX), mybir.dt.float32, kind="ExternalOutput").ap()
    build(nc, A, out)
    r = run_bass_kernel_spmd(nc, [{"in_" + k: v for k, v in arrays.items()}], core_ids=[0])
    return r.results[0]["out"].reshape(B, C, H, W)
```

```python
from contextlib import ExitStack

import concourse.bass as bass
from concourse import mybir

B, C, H, W = 8, 64, 16, 16
PIX = H * W
P = 128
TT = PIX // P
G, GC, K = 8, 8, 9
GH = 4
NH = G // GH
E0, HID0, CH0 = 8, 682, 114
CPE0 = -(-HID0 // CH0)
E1, CH1 = 16, 128
NC0, NC1 = E0 * CPE0, E1
PAIRS0, PAIRS1 = NC0 // 2, NC1 // 2
PAIRS = PAIRS0 + PAIRS1
PPE0 = CPE0 // 2
UNITS = K * TT * NH
ADDS = UNITS - TT * NH
GU0, GU1 = E0 // 2, E1 // 2
SLOTS = 4
HEADS, DH = 8, 32
HD = HEADS * DH
SCALE = DH ** -0.5
AUG = C + 4
STAGE = 1024
LAG = 2
RING = 6


def gating(m, first, end):
    out = []
    for u in range(first, end):
        out += [("gated", m, u)] + ([("gate_unit", m, u - 1)] if u > first else [])
    return out + [("gate_unit", m, end - 1)]


WEAVE = {
    "pe": """
        bbabbbbabb bbbbbabbbb bbbababbba bbbbbbbbbb bbbbabbaba abbaababba bbabaaaaba bababababa aabbabbaaa abaabaaaaa
        abaabaabbb abaabaabab bbabaababa bbabbbbbab ababa
        """,
    "act": """
        bbbabbbbab bbbbaabbba abbaabbaba bbbbaababb bbababbbab babbbbbbbb bbbbbbbaab abbabaabbb aaaaaaaa
        """,
    "dve": """
        babbabbbba bbaabababb baabbbbbba aaababbaab aabbaabaaa abbaaaabba baababaaba baabaabaaa aaabaabbab abababaaab
        bababaabab aabbababaa
        """,
    "pool": """
        aaaaabaaaa aaaaaaabaa aaaaaaaaaa aaaaaaaa
        """,
}


def stream_a():
    pre = [("x_tokens",), ("stats", 0), ("norm", 0), ("xn_channels",), ("cv1",), ("y",), ("values",)]
    pre += [("depthwise", r) for r in range(3)] + [("diagonal",), ("offsets",)]
    pre += [("row_distances", t) for t in range(TT)] + [("row_weights", t) for t in range(TT)]
    taps = [("columns", 0), ("column_weights", 0), ("columns", 1)]
    for k in range(K):
        units = [("tap" if k else "first_tap", k, q) for q in range(TT * NH)]
        taps += units[:1] + ([("column_weights", k + 1)] if k + 1 < K else [])
        taps += units[1:2] + ([("columns", k + 2)] if k + 2 < K else []) + units[2:]
    tail = [("sampled",), ("op",), ("cv2",), ("x1",), ("stats", 1), ("norm", 1), ("stack", 0), ("logits", 0), ("top", 0),
            ("exp", 0), ("gates", 0)]
    return pre + taps + tail + gating(0, 0, GU0)


def stream_b():
    def pairs(first, end, late=()):
        out = []
        for j in range(first, end):
            out += [("up", j)]
            out += (late[j - first] if j - first < len(late) else []) + ([("down", j - LAG)] if j >= first + LAG else [])
        return out + [("down", j) for j in range(end - LAG, end)]
    att = [("x2",), ("x2_tokens",), ("stats", 2), ("norm", 2), ("xn2_channels",), ("queries",), ("keys",),
           ("attn_values",), ("k_maxima",), ("q_maxima",), ("k_exp",), ("v_copy",), ("q_exp",), ("k_tokens",), ("context",),
           ("q_norm",), ("q_channels",), ("mix",), ("attend",), ("x3_tokens",), ("stats", 3), ("norm", 3), ("stack", 1),
           ("logits", 1), ("top", 1), ("exp", 1), ("gates", 1)]
    att += gating(1, 0, SLOTS)
    late = [[]] + [[("gated", 1, u), ("gate_unit", 1, u)] for u in range(SLOTS, GU1)]
    return pairs(0, PAIRS0) + att + pairs(PAIRS0, PAIRS, late) + [("x4",)]


def merge(*lists):
    out = sorted((((i + 1) / (len(l) + 1), m, i, s) for m, l in enumerate(lists) for i, s in enumerate(l)), key=lambda x: x[:3])
    return [s for _, _, _, s in out]


def start_order(n_pieces):
    return merge([("a",) + s for s in stream_a()], [("w", "piece", j) for j in range(n_pieces)])


def steady_order(weave, steps):
    left = {s: iter([(s,) + x for x in stream if x[0] in steps]) for s, stream in (("a", stream_a()), ("b", stream_b()))}
    order = [next(left[s]) for s in "".join(weave.split())]
    assert not any(list(x) for x in left.values())
    return order


class Image:

    def __init__(self, reg, plus, times=1):
        self.reg, self.plus, self.times = reg, plus, times

    def __add__(self, other):
        return Image(self.reg, self.plus + other, self.times)

    def __sub__(self, other):
        return self + -other

    def __mul__(self, other):
        return Image(self.reg, self.plus * other, self.times * other)

    __radd__, __rmul__ = __add__, __mul__


def count(x):
    if isinstance(x, int):
        return x
    value = x.reg if x.times == 1 else x.reg * x.times
    return value if x.plus == 0 else value + x.plus if x.plus > 0 else value - -x.plus


def build(nc, A, out):
    f32, f32r, u32 = mybir.dt.float32, mybir.dt.float32r, mybir.dt.uint32
    ACT, ALU, AX = mybir.ActivationFunctionType, mybir.AluOpType, mybir.AxisListType.X

    def V(base, dims):
        return bass.AP(base.tensor, base.offset, [list(base.ap[0])] + [list(d) for d in dims])

    with ExitStack() as ctx:
        def sb(name, shape, dt=f32):
            return ctx.enter_context(nc.sbuf_tensor("sb_" + name, shape, dt))

        def ps(name, shape):
            return ctx.enter_context(nc.psum_tensor("ps_" + name, shape, f32))

        def sem(name):
            return ctx.enter_context(nc.semaphore(name))

        w1s = sb("w1s", [P, NC0 * CH0], f32r)
        w3s = sb("w3s", [P, NC0 * CH0], f32r)
        w2s = sb("w2s", [CH0, NC0, C])
        u1s = sb("u1s", [P, NC1 * CH1], f32r)
        u2s = sb("u2s", [P, NC1 * CH1], f32r)
        u3s = sb("u3s", [CH1, NC1, C])
        def parts(tile, widths):
            at, views = 0, []
            for w in widths:
                views.append(tile[:, at:at + w])
                at += w
            return views

        wide = sb("wide", [P, A["wide"].shape[1]])
        ident, negb, gmask, iota, bmask, wo = parts(wide, (P, 1, GH, W, P, 2 * C))
        wo = wo.rearrange("p (c o) -> p c o", c=2)
        flat = sb("flat", [C, A["flat"].shape[1]])
        cv1, opw, cv2, dww, vecs, rw, wq, wk, wv = parts(flat, (C, C, C, K, 7, E0, HD, HD, HD))
        vp = sb("vp", [C + 1, C])
        bns = sb("bns", [C, 4])
        omx = sb("omx", [AUG, K * NH * P])
        omym = sb("omym", [AUG, 2 * K * G])
        gw = sb("gw", [C + 1, E1])
        epst = sb("epst", [P, 2, TT])
        mhalf = sb("mhalf", [P, TT])

        xT = sb("xT", [C, PIX])
        xnT = sb("xnT", [C, PIX])
        ypad = sb("ypad", [C + 1, H + 2, W + 2])
        dwT = sb("dwT", [AUG, PIX])
        bdh = sb("bdh", [P, NH, GH * GC * H], f32r)
        bdl = sb("bdl", [P, NH, GH * GC * H], f32r)
        ym = sb("ym", [P, TT, 2 * K * G])
        hy = sb("hy", [P, TT, K * G * H])
        hat = sb("hat", [P, NH * PIX])
        hx = sb("hx", [P, 3, NH, PIX], f32r)
        prod = sb("prod", [P, 2, GH * GC * H])
        acc = sb("acc", [P, TT, NH, GH * GC * H])
        yrep = [acc[0:C + 1, 1, :, :].rearrange("p h n -> p (h n)"), prod[0:C + 1, :, :].rearrange("p a n -> p (a n)")]
        dsum = sb("dsum", [P, TT, C])
        oT = sb("oT", [C, PIX])
        dT = zT = xnT
        x1T = sb("x1T", [C, PIX])

        hid = sb("hid", [P, RING, 2 * PIX])
        xgh = [sb(f"xgh{m}", [P, SLOTS, 2 * PIX], f32r) for m in range(2)]
        xgl = [sb(f"xgl{m}", [P, SLOTS, 2 * PIX], f32r) for m in range(2)]
        NE = (E0, E1)
        st = [sb(f"st{j}", [P, TT, 6]) for j in range(4)]
        mv = [sb(f"mv{j}", [P, TT, 2]) for j in range(4)]
        rs = [sb(f"rs{j}", [P, TT]) for j in range(4)]
        xn = [sb(f"xn{j}", [P, TT, (1 + j % 2) * C]) for j in range(4)]
        xh = [sb(f"xh{m}", [P, PIX], f32r) for m in range(2)]
        xl = [sb(f"xl{m}", [P, PIX], f32r) for m in range(2)]
        xf = [sb(f"xf{m}", [C + 1, PIX]) for m in range(2)]
        lg = [sb(f"lg{m}", [P, TT, NE[m]]) for m in range(2)]
        ex = [sb(f"ex{m}", [P, TT, NE[m]]) for m in range(2)]
        mx = [sb(f"mx{m}", [P, TT, 8]) for m in range(2)]
        ix = [sb(f"ix{m}", [P, TT, 8], u32) for m in range(2)]
        ixf = [sb(f"ixf{m}", [P, TT, 2]) for m in range(2)]
        nm = [sb(f"nm{m}", [P, TT]) for m in range(2)]
        sm = [sb(f"sm{m}", [P, TT]) for m in range(2)]
        em = [sb(f"em{m}", [P, TT, 2]) for m in range(2)]
        pk = [sb(f"pk{m}", [P, TT, 2]) for m in range(2)]
        ks_ = [sb(f"ks{m}", [P, TT, 2]) for m in range(2)]
        oh = [sb(f"oh{m}", [P, TT, 2, NE[m]]) for m in range(2)]
        gt = [sb(f"gt{m}", [P, TT, NE[m]]) for m in range(2)]
        xg = [sb(f"xg{m}", [P, 2, TT, 2, 2 * C]) for m in range(2)]

        x2T = sb("x2T", [C, PIX])
        xn2T = sb("xn2T", [C, PIX])
        qm = sb("qm", [P, TT * HEADS])
        qz = sb("qz", [P, TT * HEADS])
        qr = sb("qr", [P, TT * HEADS])
        km = sb("km", [P, 2])
        kz = sb("kz", [P, 2])
        kr = sb("kr", [P, 2, 2])
        x3T = sb("x3T", [C, PIX])
        outT = sb("outT", [C, PIX])
        q_s, k_s, v_s, kT_s = (hid[:, j, :] for j in range(4))
        qT = k_s.rearrange("p (c n) -> p c n", c=2)
        cT = v_s[:, 0:2 * P].rearrange("p (c d) -> p c d", c=2)
        mT = v_s[:, 2 * P:2 * P + 2 * C].rearrange("p (c o) -> p c o", c=2)

        h1 = [ps(f"h1_{j}", [P, 2 * PIX]) for j in range(2)]
        h3 = [ps(f"h3_{j}", [P, 2 * PIX]) for j in range(2)]
        yb = ps("y", [P, PIX * 2])
        tb = [ps(f"t_{j}", [P, 2 * PIX]) for j in range(2)]
        mb = ps("m", [P, 2 * PIX])

        s_const = sem("s_const")
        s_stage = [sem(f"s_stage{j}") for j in range(2)]
        s_down = sem("s_down")
        s_act_whi = sem("s_act_whi")
        s_dve_w = sem("s_dve_w")
        s_dve_set = sem("s_dve_set")
        s_dve_bn = sem("s_dve_bn")
        s_act_bn = sem("s_act_bn")
        s_ld_x = sem("s_ld_x")
        s_st = sem("s_st")
        s_pe_xt, s_pe_xnt, s_pe_y, s_pe_v, s_pe_ym = map(sem, ("s_pe_xt", "s_pe_xnt", "s_pe_y", "s_pe_v", "s_pe_ym"))
        s_pe_xr, s_pe_t = sem("s_pe_xr"), sem("s_pe_t")
        s_pe_dt, s_pe_o, s_pe_z, s_pe_x1t = map(sem, ("s_pe_dt", "s_pe_o", "s_pe_z", "s_pe_x1t"))
        s_act_xnt, s_act_y, s_act_bh, s_act_ym = map(sem, ("s_act_xnt", "s_act_y", "s_act_bh", "s_act_ym"))
        s_act_hyabs, s_act_hy = sem("s_act_hyabs"), sem("s_act_hy")
        s_act_abs, s_act_hat = sem("s_act_abs"), sem("s_act_hat")
        s_act_dt, s_act_o, s_act_z = map(sem, ("s_act_dt", "s_act_o", "s_act_z"))
        s_dve_yr = sem("s_dve_yr")
        s_dve_dw, s_dve_bd = sem("s_dve_dw"), sem("s_dve_bd")
        s_dve_hr, s_dve_hx = sem("s_dve_hr"), sem("s_dve_hx")
        s_dve_p, s_dve_dr = sem("s_dve_p"), sem("s_dve_dr")
        s_dve_x1 = sem("s_dve_x1")
        s_dve_bl, s_dve_dy = sem("s_dve_bl"), sem("s_dve_dy")
        s_pool_hy, s_pool_acc = map(sem, ("s_pool_hy", "s_pool_acc"))
        s_dve_st = [sem(f"s_dve_st{j}") for j in range(4)]
        s_dve_mv = [sem(f"s_dve_mv{j}") for j in range(4)]
        s_pool_ve = [sem(f"s_pool_ve{j}") for j in range(4)]
        s_pool_rs = [sem(f"s_pool_rs{j}") for j in range(4)]
        s_dve_xn = [sem(f"s_dve_xn{j}") for j in range(4)]
        def two(name):
            return [sem(f"{name}{m}") for m in range(2)]
        s_pe_xs, s_act_xh, s_act_xf, s_dve_xl = two("s_pe_xs"), two("s_act_xh"), two("s_act_xf"), two("s_dve_xl")
        s_pe_lg, s_act_lg = two("s_pe_lg"), two("s_act_lg")
        s_dve_mx, s_dve_ix, s_dve_nm = two("s_dve_mx"), two("s_dve_ix"), two("s_dve_nm")  
        s_act_ex = two("s_act_ex")
        s_dve_gt = two("s_dve_gt")
        s_act_xg, s_pe_g, s_act_g, s_dve_g = two("s_act_xg"), two("s_pe_g"), two("s_act_g"), two("s_dve_g")
        GT, GU = (12, 11), (GU0, GU1)
        s_pe_h1, s_pe_h3, s_pe_y2 = map(sem, ("s_pe_h1", "s_pe_h3", "s_pe_down"))
        s_act_s, s_dve_hid, s_dve_x2, s_dve_x4 = map(sem, ("s_act_s", "s_dve_hid", "s_dve_x2", "s_dve_x4"))
        (s_pe_x2t, s_pe_xn2t, s_act_xn2t, s_pe_q, s_pe_k, s_pe_vv, s_act_v, s_dve_qm, s_dve_qs, s_act_q,
         s_dve_qz, s_dve_qr, s_dve_qn, s_pe_qt, s_act_qt, s_dve_km, s_act_k, s_pe_kt, s_act_kt, s_pe_c,
         s_dve_c, s_dve_kr, s_pe_mm, s_dve_m, s_pe_at, s_dve_x3, s_pe_x3t) = map(sem, (
            "s_pe_x2t", "s_pe_xn2t", "s_act_xn2t", "s_pe_q", "s_pe_k", "s_pe_vv", "s_act_v", "s_dve_qm", "s_dve_qs", "s_act_q",
            "s_dve_qz", "s_dve_qr", "s_dve_qn", "s_pe_qt", "s_act_qt", "s_dve_km", "s_act_k", "s_pe_kt", "s_act_kt", "s_pe_c",
            "s_dve_c", "s_dve_kr", "s_pe_mm", "s_dve_m", "s_pe_at", "s_dve_x3", "s_pe_x3t"))

        pieces = []
        for names, dsts, total, size in ((("w1T", "w3T"), (w1s, w3s), NC0 * CH0, CPE0 * CH0), (("u1T", "u2T"), (u1s, u2s), NC1 * CH1, STAGE)):
            for name, dst in zip(names, dsts):
                for c in range(0, total, size):
                    pieces.append((A[name][:, c:c + size], size, dst[:, c:c + size]))
        stage = [hid[:, 2 * j:2 * j + 2, :].rearrange("p a n -> p (a n)") for j in range(2)]
        stage_hi = [xgh[1][:, 2 * j:2 * j + 2, :].rearrange("p a n -> p (a n)") for j in range(2)]
        staged = [0, 0]
        piece_ready = []
        for j in range(len(pieces)):
            staged[j % 2] += 32
            piece_ready.append(staged[j % 2])

        consts = [(wide[:, :], "wide"), (flat[:, :], "flat"), (vp[:, :], "vpT"), (gw[:, :], "gwT"), (omym[:, :], "omymT"),
                  (omx[:, :], "omxT"), (dwT[C:AUG, :], "pixC")]
        n_const = 16 * len(consts)

        gate_bank = ([tb[u % 2] for u in range(GU0)],
                     [h1[0], h3[0], h1[1], h3[1], h1[0], h1[1], h1[0], h1[1]])
        first, final = start_order(len(pieces)), [("b",) + s for s in stream_b()]

        block = ctx.enter_context(nc.Block())

        def settled(eng):
            eng.wait_ge(s_const, n_const)

        @block.sync
        def _(sp):
            sp.dma_start(xT[:, :], A["x"][0]).then_inc(s_ld_x, 16)
            for dst, name in consts[0::2]:
                sp.dma_start(dst, A[name]).then_inc(s_const, 16)
            for j, (src, cols, _dst) in enumerate(pieces):
                if j >= 2:
                    sp.wait_ge(s_dve_w, j - 1)
                for r in range(2):
                    sp.dma_start(stage[j % 2][C * r:C * r + C, 0:cols], src).then_inc(s_stage[j % 2], 16)
            sp.wait_ge(s_dve_x1, 1)
            sp.dma_start(xT[:, :], A["x"][1]).then_inc(s_ld_x, 16)
            with sp.Fori(1, B - 1) as n:
                sp.wait_ge(s_dve_x1, n + 1)
                sp.dma_start(xT[:, :], A["x"][n + 1]).then_inc(s_ld_x, 16)
                sp.wait_ge(s_dve_x4, n + 1)
                sp.dma_start(out[n - 1], outT[:, :]).then_inc(s_st, 16)
            for n in (B - 2, B - 1):
                sp.wait_ge(s_dve_x4, n + 2)
                sp.dma_start(out[n], outT[:, :]).then_inc(s_st, 16)
            sp.wait_ge(s_st, 16 * B + 16)

        @block.tensor
        def _(pe):
            mm, tr = nc.tensor.matmul, nc.tensor.transpose

            def transposes_to_tokens(bank, src):
                for t in range(TT):
                    last = tr(bank[:, t * C:(t + 1) * C], src[:, t * P:(t + 1) * P], ident[0:C, 0:C])
                return last

            def transposes_to_channels(bank, src):
                for t in range(TT):
                    last = tr(bank[0:C, t * P:(t + 1) * P], src[:, t, :], ident[:, :])
                return last

            def x_tokens(n):
                pe.wait_ge(s_ld_x, count(16 * n + 16))
                for t in range(TT):
                    last = mm(mb[:, t * C:(t + 1) * C], xT[:, t * P:(t + 1) * P], ident[0:C, 0:C], start=True, stop=True)
                last.then_inc(s_pe_xt, 1)

            def xn_channels(n):
                pe.wait_ge(s_dve_xn[0], count(n + 1))
                for t in range(TT):
                    last = mm(mb[0:C, t * P:(t + 1) * P], xn[0][:, t, :], ident[:, :], start=True, stop=True)
                last.then_inc(s_pe_xnt, 1)

            def cv1_product(n):
                settled(pe)
                pe.wait_ge(s_act_xnt, count(n + 1))
                mm(mb[0:C, 0:PIX], cv1[:, :], xnT[:, :], start=True, stop=True).then_inc(s_pe_y, 1)

            def values(n):
                for b in range(2):
                    pe.wait_ge(s_dve_yr, count(2 * n + b + 1))
                    for r in range(H // 2):
                        last = mm(tb[b][:, r * C:(r + 1) * C], yrep[b][:, r * P:(r + 1) * P], vp[:, :],
                                  start=True, stop=True)
                    last.then_inc(s_pe_v, 1)

            def offsets(n):
                pe.wait_ge(s_dve_dw, count(K * n + K))
                for t in range(TT):
                    last = mm(mb[:, t * 2 * K * G:(t + 1) * 2 * K * G], dwT[:, t * P:(t + 1) * P], omym[:, :],
                              start=True, stop=True)
                last.then_inc(s_pe_ym, 1)

            def columns(n, k):
                if k == 0:
                    pe.wait_ge(s_act_ym, count(n + 1))
                else:
                    pe.wait_ge(s_act_abs, count(K * n + k))
                for h in range(NH):
                    o = (k * NH + h) * P
                    last = mm(mb[:, h * PIX:(h + 1) * PIX], omx[:, o:o + P], dwT[:, :], start=True, stop=True)
                last.then_inc(s_pe_xr, 1)

            def tap(n, k, q):
                t, h = divmod(q, NH)
                u = k * TT * NH + q
                if q == 0:
                    pe.wait_ge(s_dve_hx, count(K * n + k + 1))
                if u == 0:
                    pe.wait_ge(s_act_bh, count(n + 1))
                    pe.wait_ge(s_dve_bl, count(n + 1))
                if u >= 2:
                    pe.wait_ge(s_dve_p, count(UNITS * n + u - 1))
                w = hx[:, k % 3, h, t * P:(t + 1) * P]
                mm(tb[u % 2][:, :], w, bdh[:, h, :], start=True, stop=False)
                mm(tb[u % 2][:, :], w, bdl[:, h, :], start=False, stop=True).then_inc(s_pe_t, 1)

            def sampled(n):
                settled(pe)
                pe.wait_ge(s_dve_dr, count(n + 1))
                transposes_to_channels(mb, dsum).then_inc(s_pe_dt, 1)

            def op_product(n):
                settled(pe)
                pe.wait_ge(s_act_dt, count(n + 1))
                mm(mb[0:C, 0:PIX], opw[:, :], dT[:, :], start=True, stop=True).then_inc(s_pe_o, 1)

            def cv2_product(n):
                settled(pe)
                pe.wait_ge(s_act_o, count(n + 1))
                mm(mb[0:C, 0:PIX], cv2[:, :], oT[:, :], start=True, stop=True).then_inc(s_pe_z, 1)

            def x1(n):
                settled(pe)
                pe.wait_ge(s_dve_x1, count(n + 1))
                transposes_to_tokens(mb, x1T).then_inc(s_pe_x1t, 1)

            def stack(n, m):
                bx = (mb, h1[1])[m]
                pe.wait_ge(s_dve_xn[1 + 2 * m], count(n + 1))
                for t in range(TT):
                    last = tr(bx[:, t * P:(t + 1) * P], xn[1 + 2 * m][:, t, :], ident[:, :])
                last.then_inc(s_pe_xs[m], 1)

            def logits(n, m):
                bl = (mb, h3[0])[m]
                pe.wait_ge(s_act_xf[m], count(n + 1))
                pe.wait_ge(s_dve_xl[m], count(n + 1))
                rows, w = (C, rw) if m == 0 else (C + 1, gw)
                for t in range(TT):
                    last = mm(bl[:, t * NE[m]:(t + 1) * NE[m]], xf[m][0:rows, t * P:(t + 1) * P], w[:, :],
                              start=True, stop=True)
                last.then_inc(s_pe_lg[m], 1)

            def gate_unit(n, m, u):
                pe.wait_ge(s_act_xg[m], count(GU[m] * n + u + 1))
                if m == 0 and u >= 2:
                    pe.wait_ge(s_dve_g[0], count(GU0 * n + u - 1))
                if m == 1 and u >= SLOTS:
                    pe.wait_ge(s_act_s, count(PAIRS * n + PAIRS0 + u - SLOTS + 1))
                bank = gate_bank[m][u]
                for e in range(2):
                    for t in range(TT):
                        last = tr(bank[:, (e * TT + t) * P:(e * TT + t + 1) * P],
                                  xg[m][:, u % 2, t, e, :], ident[:, :])
                last.then_inc(s_pe_g[m], 1)

            def up(n, j):
                first, m = (0, 0) if j < PAIRS0 else (PAIRS0, 1)
                ch = (CH0, CH1)[m]
                wa, wb = ((w1s, w3s), (u1s, u2s))[m]
                if j == 0:
                    pe.wait_ge(s_dve_g[0], count(GU0 * n + 1))
                    pe.wait_ge(s_act_xh[0], count(n + 1))
                if PAIRS0 <= j < PAIRS0 + 2:
                    pe.wait_ge(s_dve_g[1], count(GU1 * n + (1, 3)[j - PAIRS0]))
                elif j >= PAIRS0 + 2:
                    pe.wait_ge(s_dve_g[1], count(GU1 * n + min(GU1, SLOTS + j - PAIRS0 - 1)))
                if j % PAIRS0 >= 2:
                    pe.wait_ge(s_act_s, count(PAIRS * n + j - 1))
                for c in range(2):
                    o = (2 * (j - first) + c) * ch
                    d = h1[j % 2][0:ch, c * PIX:(c + 1) * PIX]
                    mm(d, wa[:, o:o + ch], xh[m][:, :], start=True, stop=False)
                    last = mm(d, wa[:, o:o + ch], xl[m][:, :], start=False, stop=True)
                last.then_inc(s_pe_h1, 1)
                if 0 < j < PAIRS0 and j % (2 * PPE0) == 0:
                    pe.wait_ge(s_dve_g[0], count(GU0 * n + j // (2 * PPE0) + 1))
                if PAIRS0 <= j < PAIRS0 + 2:
                    pe.wait_ge(s_dve_g[1], count(GU1 * n + (2, 4)[j - PAIRS0]))
                elif j >= 2:
                    pe.wait_ge(s_dve_hid, count(PAIRS * n + j - 1))
                for c in range(2):
                    o = (2 * (j - first) + c) * ch
                    e = j // PPE0 if m == 0 else 2 * (j - first) + c
                    slot, x = (e // 2) % SLOTS, slice((e % 2) * PIX, (e % 2 + 1) * PIX)
                    d = h3[j % 2][0:ch, c * PIX:(c + 1) * PIX]
                    mm(d, wb[:, o:o + ch], xgh[m][:, slot, x], start=True, stop=False)
                    last = mm(d, wb[:, o:o + ch], xgl[m][:, slot, x], start=False, stop=True)
                last.then_inc(s_pe_h3, 1)

            def down(n, j):
                first, end, m = (0, PAIRS0, 0) if j < PAIRS0 else (PAIRS0, PAIRS, 1)
                ch, w = ((CH0, w2s), (CH1, u3s))[m]
                pe.wait_ge(s_dve_hid, count(PAIRS * n + j + 1))
                if j == 0:
                    pe.wait_ge(s_dve_x4, count(n + 1))
                for c in range(2):
                    last = mm(yb[0:C, 0:PIX], w[0:ch, 2 * (j - first) + c, :], hid[0:ch, j % RING, c * PIX:(c + 1) * PIX],
                              start=(j == first and c == 0), stop=(j == end - 1 and c == 1))
                last.then_inc(s_pe_y2, 1)

            def x2_tokens(n):
                settled(pe)
                pe.wait_ge(s_dve_x2, count(n + 1))
                transposes_to_tokens(h1[0], x2T).then_inc(s_pe_x2t, 1)

            def xn2_channels(n):
                settled(pe)
                pe.wait_ge(s_dve_xn[2], count(n + 1))
                transposes_to_channels(h1[1], xn[2]).then_inc(s_pe_xn2t, 1)

            def queries(n):
                pe.wait_ge(s_act_xn2t, count(n + 1))
                for t in range(TT):
                    last = mm(h1[0][:, t * HD:(t + 1) * HD], xn2T[:, t * P:(t + 1) * P], wq[:, :], start=True, stop=True)
                last.then_inc(s_pe_q, 1)

            def keys(n):
                for c in range(2):
                    last = mm(h1[1][:, c * PIX:(c + 1) * PIX], wk[:, c * P:(c + 1) * P], xn2T[:, :], start=True, stop=True)
                last.then_inc(s_pe_k, 1)

            def attn_values(n):
                for t in range(TT):
                    last = mm(h3[0][:, t * HD:(t + 1) * HD], xn2T[:, t * P:(t + 1) * P], wv[:, :], start=True, stop=True)
                last.then_inc(s_pe_vv, 1)

            def k_tokens(n):
                pe.wait_ge(s_act_k, count(2 * n + 2))
                for t in range(TT):
                    for c in range(2):
                        last = tr(h3[1][:, t * HD + c * P:t * HD + (c + 1) * P],
                                  k_s[:, c * PIX + t * P:c * PIX + (t + 1) * P], ident[:, :])
                last.then_inc(s_pe_kt, 1)

            def context(n):
                pe.wait_ge(s_act_v, count(n + 1))
                pe.wait_ge(s_act_kt, count(n + 1))
                for c in range(2):
                    for t in range(TT):
                        o = t * HD + c * P
                        last = mm(h3[0][:, c * P:(c + 1) * P], v_s[:, o:o + P], kT_s[:, o:o + P], start=(t == 0), stop=(t == TT - 1))
                last.then_inc(s_pe_c, 1)

            def q_channels(n):
                pe.wait_ge(s_dve_qn, count(n + 1))
                for c in range(2):
                    for t in range(TT):
                        last = tr(h1[0][:, c * PIX + t * P:c * PIX + (t + 1) * P],
                                  q_s[:, t * HD + c * P:t * HD + (c + 1) * P], ident[:, :])
                last.then_inc(s_pe_qt, 1)

            def mix(n):
                pe.wait_ge(s_dve_c, count(n + 1))
                for c in range(2):
                    last = mm(h1[1][:, c * C:(c + 1) * C], cT[:, c, :], wo[:, c, :], start=True, stop=True)
                last.then_inc(s_pe_mm, 1)

            def attend(n):
                pe.wait_ge(s_dve_m, count(n + 1))
                pe.wait_ge(s_act_qt, count(n + 1))
                for c in range(2):
                    last = mm(yb[0:C, 0:PIX], mT[:, c, :], qT[:, c, :], start=(c == 0), stop=(c == 1))
                last.then_inc(s_pe_at, 1)

            def x3_tokens(n):
                settled(pe)
                pe.wait_ge(s_dve_x3, count(n + 1))
                transposes_to_tokens(h1[0], x3T).then_inc(s_pe_x3t, 1)

            steps = {"x_tokens": x_tokens, "xn_channels": xn_channels, "cv1": cv1_product, "values": values, "offsets": offsets,
                     "columns": columns, "first_tap": tap, "tap": tap, "sampled": sampled, "op": op_product, "cv2": cv2_product, "x1": x1,
                     "stack": stack, "logits": logits, "gate_unit": gate_unit, "up": up, "down": down,
                     "x2_tokens": x2_tokens, "xn2_channels": xn2_channels, "queries": queries,
                     "keys": keys, "attn_values": attn_values, "k_tokens": k_tokens,
                     "context": context, "q_channels": q_channels, "mix": mix, "attend": attend, "x3_tokens": x3_tokens}

            def walk(order, images):
                for stream, name, *args in order:
                    if name in steps:
                        steps[name](images[stream], *args)

            pe.wait_ge(s_const, n_const)
            pe.wait_ge(s_dve_set, 7)
            walk(first, {"a": 0, "w": 0})
            pe.wait_ge(s_dve_w, len(pieces))
            pe.wait_ge(s_down, 32)
            with pe.Fori(1, B) as i:
                walk(steady_order(WEAVE["pe"], steps), {"a": Image(i, 0), "b": Image(i, -1)})
            walk(final, {"b": B - 1})

        @block.scalar
        def _(act):
            af = nc.scalar.activation

            for dst, name in consts[1::2]:
                act.dma_start(dst, A[name]).then_inc(s_const, 16)
            for dst, name in ((w2s, "w2T"), (u3s, "u3T")):
                act.dma_start(dst[:, :, :], A[name]).then_inc(s_down, 16)
            act.wait_ge(s_const, n_const)
            act.wait_ge(s_dve_bn, 1)
            af(bns[:, 1:2], bns[:, 0:1], ACT.Sqrt).then_inc(s_act_bn, 1)

            def piece(n, j):
                _src, cols, _dst = pieces[j]
                act.wait_ge(s_stage[j % 2], piece_ready[j])
                if j >= 2:
                    act.wait_ge(s_dve_w, j - 1)
                af(stage_hi[j % 2][:, 0:cols], stage[j % 2][:, 0:cols], ACT.Copy).then_inc(s_act_whi, 1)

            def xn_channels(n):
                act.wait_ge(s_pe_xnt, count(n + 1))
                af(xnT[:, :], mb[0:C, 0:PIX], ACT.Copy).then_inc(s_act_xnt, 1)

            def cv1_bias(n):
                act.wait_ge(s_pe_y, count(n + 1))
                af(ypad[0:C, 1:1 + H, 1:1 + W], mb[0:C, 0:PIX].rearrange("p (h w) -> p h w", w=W),
                   ACT.Identity, bias=vecs[:, 0:1]).then_inc(s_act_y, 1)

            def diagonal(n):
                act.wait_ge(s_dve_bd, count(4 * n + 4))
                af(bdh[:, :, :], acc[:, 0, :, :], ACT.Copy).then_inc(s_act_bh, 1)

            def offsets(n):
                act.wait_ge(s_pe_ym, count(n + 1))
                af(ym[:, :, :], mb[:, 0:TT * 2 * K * G].rearrange("p (t c) -> p t c", t=TT), ACT.Copy).then_inc(s_act_ym, 1)

            def row_distances(n, t):
                act.wait_ge(s_dve_dy, count(TT * n + t + 1))
                af(hy[:, t, :], hy[:, t, :], ACT.Abs).then_inc(s_act_hyabs, 1)

            def row_weights(n, t):
                act.wait_ge(s_act_hyabs, count(TT * n + t + 1))
                af(hy[:, t, :], hy[:, t, :], ACT.Relu, scale=-1.0, bias=1.0).then_inc(s_act_hy, 1)

            def columns(n, k):
                act.wait_ge(s_pe_xr, count(K * n + k + 1))
                if k > 0 or not isinstance(n, int):
                    act.wait_ge(s_dve_hx, count(K * n + k))
                af(hat[:, :], mb[:, :], ACT.Abs).then_inc(s_act_abs, 1)
                act.wait_ge(s_act_abs, count(K * n + k + 1))
                af(hat[:, :], hat[:, :], ACT.Relu, scale=-1.0, bias=1.0).then_inc(s_act_hat, 1)

            def sampled(n):
                act.wait_ge(s_pe_dt, count(n + 1))
                af(dT[:, :], mb[0:C, 0:PIX], ACT.Copy).then_inc(s_act_dt, 1)

            def op_product(n):
                act.wait_ge(s_pe_o, count(n + 1))
                af(oT[:, :], mb[0:C, 0:PIX], ACT.Copy).then_inc(s_act_o, 1)

            def cv2_silu(n):
                act.wait_ge(s_pe_z, count(n + 1))
                af(zT[:, :], mb[0:C, 0:PIX], ACT.Silu, scale=bns[:, 2:3], bias=bns[:, 3:4]).then_inc(s_act_z, 1)

            def stack(n, m):
                bx = (mb, h1[1])[m]
                act.wait_ge(s_pe_xs[m], count(n + 1))
                if m == 0 and not isinstance(n, int):
                    act.wait_ge(s_pe_h1, count(PAIRS * n - PAIRS1))
                af(xf[m][0:C, :], bx[0:C, 0:PIX], ACT.Copy).then_inc(s_act_xf[m], 1)
                af(xh[m][:, :], bx[:, 0:PIX], ACT.Copy).then_inc(s_act_xh[m], 1)

            def logits(n, m):
                bl = (mb, h3[0])[m]
                act.wait_ge(s_pe_lg[m], count(n + 1))
                af(lg[m][:, :, :], bl[:, 0:TT * NE[m]].rearrange("p (t e) -> p t e", t=TT), ACT.Copy).then_inc(s_act_lg[m], 1)

            def exp_top(n, m):
                act.wait_ge(s_act_lg[m], count(n + 1))
                act.wait_ge(s_dve_nm[m], count(n + 1))
                for t in range(TT):
                    af(ex[m][:, t, :], lg[m][:, t, :], ACT.Exp, bias=nm[m][:, t:t + 1],
                       accum_out=sm[m][:, t:t + 1]).then_inc(s_act_ex[m], 1)
                    af(em[m][:, t, :], mx[m][:, t, 0:2], ACT.Exp, bias=nm[m][:, t:t + 1]).then_inc(s_act_ex[m], 1)

            def gated(n, m, u):
                if u == 0:
                    act.wait_ge(s_dve_gt[m], count(GT[m] * n + GT[m]))
                elif u >= 2:
                    act.wait_ge(s_pe_g[m], count(GU[m] * n + u - 1))
                for t in range(TT):
                    for e in range(2):
                        last = af(xg[m][:, u % 2, t, e, :], xn[1 + 2 * m][:, t, :], ACT.Copy, scale=gt[m][:, t, 2 * u + e:2 * u + e + 1])
                last.then_inc(s_act_xg[m], 1)

            def gate_unit(n, m, u):
                if m == 0 and u == 0 and not isinstance(n, int):
                    act.wait_ge(s_pe_h3, count(PAIRS * n - PAIRS1))
                act.wait_ge(s_pe_g[m], count(GU[m] * n + u + 1))
                af(xgh[m][:, u % SLOTS, :], gate_bank[m][u][:, :], ACT.Copy).then_inc(s_act_g[m], 1)

            def silu(n, j):
                ch = CH0 if j < PAIRS0 else CH1
                act.wait_ge(s_pe_h1, count(PAIRS * n + j + 1))
                if j % PAIRS0 >= RING:
                    act.wait_ge(s_pe_y2, count(PAIRS * n + j - RING + 1))
                af(hid[0:ch, j % RING, :], h1[j % 2][0:ch, :], ACT.Silu).then_inc(s_act_s, 1)

            def xn2_channels(n):
                act.wait_ge(s_pe_xn2t, count(n + 1))
                af(xn2T[:, :], h1[1][0:C, 0:PIX], ACT.Copy).then_inc(s_act_xn2t, 1)

            def k_exp(n):
                act.wait_ge(s_dve_km, count(n + 1))
                for c in range(2):
                    af(k_s[:, c * PIX:(c + 1) * PIX], h1[1][:, c * PIX:(c + 1) * PIX], ACT.Exp, bias=km[:, c:c + 1],
                       accum_out=kz[:, c:c + 1]).then_inc(s_act_k, 1)

            def v_copy(n):
                act.wait_ge(s_pe_vv, count(n + 1))
                af(v_s, h3[0][:, :], ACT.Copy).then_inc(s_act_v, 1)

            def q_exp(n):
                act.wait_ge(s_dve_qs, count(n + 1))
                af(q_s, q_s, ACT.Exp).then_inc(s_act_q, 1)

            def k_tokens(n):
                act.wait_ge(s_pe_kt, count(n + 1))
                af(kT_s, h3[1][:, :], ACT.Copy).then_inc(s_act_kt, 1)

            def q_channels(n):
                act.wait_ge(s_pe_qt, count(n + 1))
                af(qT[:, :, :], h1[0][:, :].rearrange("p (c n) -> p c n", c=2), ACT.Copy).then_inc(s_act_qt, 1)

            steps = {"piece": piece, "xn_channels": xn_channels, "cv1": cv1_bias, "diagonal": diagonal, "offsets": offsets,
                     "row_distances": row_distances, "row_weights": row_weights, "columns": columns, "sampled": sampled,
                     "op": op_product, "cv2": cv2_silu, "stack": stack, "logits": logits, "exp": exp_top,
                     "gated": gated, "gate_unit": gate_unit, "up": silu, "xn2_channels": xn2_channels,
                     "k_exp": k_exp, "v_copy": v_copy, "q_exp": q_exp, "k_tokens": k_tokens, "q_channels": q_channels}

            def walk(order, images):
                for stream, name, *args in order:
                    if name in steps:
                        steps[name](images[stream], *args)

            walk(first, {"a": 0, "w": 0})
            with act.Fori(1, B) as i:
                walk(steady_order(WEAVE["act"], steps), {"a": Image(i, 0), "b": Image(i, -1)})
            walk(final, {"b": B - 1})

        @block.vector
        def _(dve):
            v = nc.vector
            v.memset(ypad[0:C, :, :], 0.0).then_inc(s_dve_set, 1)
            v.memset(ypad[C:C + 1, :, :], 1.0).then_inc(s_dve_set, 1)
            v.memset(xf[1][C:C + 1, :], 1.0).then_inc(s_dve_set, 1)
            v.memset(epst[:, 0, :], 1e-6).then_inc(s_dve_set, 1)
            v.memset(epst[:, 1, :], 1e-5).then_inc(s_dve_set, 1)
            v.memset(mhalf[:, :], -0.5).then_inc(s_dve_set, 1)
            v.memset(xf[0][C:C + 1, :], 1.0).then_inc(s_dve_set, 1)
            dve.wait_ge(s_const, n_const)
            v.tensor_scalar(bns[:, 0:1], vecs[:, 5:6], 1e-5, None, ALU.add).then_inc(s_dve_bn, 1)
            dve.wait_ge(s_act_bn, 1)
            v.reciprocal(bns[:, 0:1], bns[:, 1:2]).then_inc(s_dve_bn, 1)
            dve.wait_ge(s_dve_bn, 2)
            v.tensor_tensor(bns[:, 2:3], vecs[:, 2:3], bns[:, 0:1], ALU.mult).then_inc(s_dve_bn, 1)
            dve.wait_ge(s_dve_bn, 3)
            v.tensor_tensor(bns[:, 1:2], vecs[:, 4:5], bns[:, 2:3], ALU.mult).then_inc(s_dve_bn, 1)
            dve.wait_ge(s_dve_bn, 4)
            v.tensor_tensor(bns[:, 3:4], vecs[:, 3:4], bns[:, 1:2], ALU.subtract).then_inc(s_dve_bn, 1)

            def piece(n, j):
                _src, cols, dst = pieces[j]
                dve.wait_ge(s_act_whi, j + 1)
                v.scalar_tensor_tensor(out=dst, in0=stage_hi[j % 2][:, 0:cols], scalar=negb[:, 0:1],
                                       in1=stage[j % 2][:, 0:cols], op0=ALU.mult, op1=ALU.add).then_inc(s_dve_w, 1)

            def stats(n, j):
                bank, ready = ((mb, s_pe_xt), (mb, s_pe_x1t), (h1[0], s_pe_x2t), (h1[0], s_pe_x3t))[j]
                dve.wait_ge(ready, count(n + 1))
                for t in range(TT):
                    last = v.bn_stats(st[j][:, t, :], bank[:, t * C:(t + 1) * C])
                last.then_inc(s_dve_st[j], 1)
                settled(dve)
                dve.wait_ge(s_dve_st[j], count(n + 1))
                for t in range(TT):
                    last = v.bn_aggr(mv[j][:, t, :], st[j][:, t, :])
                last.then_inc(s_dve_mv[j], 1)

            def norm(n, j):
                bank = mb if j < 2 else h1[0]
                dve.wait_ge(s_pool_rs[j], count(n + 1))
                d = 1 + j % 2
                for t in range(TT):
                    last = v.tensor_scalar(V(xn[j][:, t, :], [[C, d], [1, C]]), V(bank[:, t * C:TT * C], [[0, d], [1, C]]),
                                           mv[j][:, t, 0:1], rs[j][:, t:t + 1], ALU.subtract, ALU.mult)
                last.then_inc(s_dve_xn[j], 1)

            def y_rows(n):
                dve.wait_ge(s_act_y, count(n + 1))
                for b in range(2):
                    row = ypad[:, 1 + b * (H // 2), 1:1 + W]
                    v.tensor_copy(V(yrep[b], [[P, H // 2], [W, P // W], [1, W]]),
                                  V(row, [[W + 2, H // 2], [0, P // W], [1, W]])).then_inc(s_dve_yr, 1)

            def depthwise(n, r):
                for k in range(3 * r, 3 * r + 3):
                    win = ypad[0:C, k // 3:k // 3 + H, k % 3:k % 3 + W]
                    o = dwT[0:C, :].rearrange("p (h w) -> p h w", w=W)
                    if k == 0:
                        v.tensor_scalar(o, win, dww[:, 0:1], vecs[:, 1:2], ALU.mult, ALU.add).then_inc(s_dve_dw, 1)
                    else:
                        dve.wait_ge(s_dve_dw, count(K * n + k))
                        v.scalar_tensor_tensor(out=o, in0=win, scalar=dww[:, k:k + 1], in1=o, op0=ALU.mult,
                                               op1=ALU.add).then_inc(s_dve_dw, 1)

            def diagonal(n):
                for b in range(2):
                    dve.wait_ge(s_pe_v, count(2 * n + b + 1))
                    for h in range(NH):
                        o = V(acc[:, 0, h, b * (H // 2):GH * GC * H], [[1, H // 2], [GC * H, GH], [H, GC]])
                        src = V(tb[b][:, h * GH * GC:2 * PIX], [[C, H // 2], [GC, GH], [1, GC]])
                        v.tensor_tensor(o, src, V(gmask[:, :], [[0, H // 2], [1, GH], [0, GC]]), ALU.mult).then_inc(s_dve_bd, 1)
                dve.wait_ge(s_dve_bd, count(4 * n + 4))
                dve.wait_ge(s_act_bh, count(n + 1))
                v.tensor_tensor(bdl[:, :, :], acc[:, 0, :, :], bdh[:, :, :], ALU.subtract).then_inc(s_dve_bl, 1)

            def row_distances(n, t):
                dve.wait_ge(s_act_ym, count(n + 1))
                v.tensor_tensor(V(hy[:, t, :], [[H, K * G], [1, H]]), V(ym[:, t, :], [[1, K * G], [0, H]]),
                                V(iota[:, :], [[0, K * G], [1, H]]), ALU.subtract).then_inc(s_dve_dy, 1)

            def column_weights(n, k):
                dve.wait_ge(s_act_hat, count(K * n + k + 1))
                if k >= 3:
                    dve.wait_ge(s_pe_t, count(UNITS * n + (k - 2) * TT * NH))
                o = V(hx[:, k % 3, :, :], [[1, NH * PIX]])
                v.tensor_copy(o, hat[:, :]).then_inc(s_dve_hr, 1)
                dve.wait_ge(s_dve_hr, count(K * n + k + 1))
                v.scalar_tensor_tensor(out=o, in0=o, scalar=negb[:, 0:1], in1=hat[:, :], op0=ALU.mult,
                                       op1=ALU.add).then_inc(s_dve_hx, 1)

            def tap(n, k, q):
                t, h = divmod(q, NH)
                u = k * TT * NH + q
                if u == 0:
                    dve.wait_ge(s_pool_hy, count(TT * n + TT))
                    dve.wait_ge(s_dve_bl, count(n + 1))
                dve.wait_ge(s_pe_t, count(UNITS * n + u + 1))
                o = acc[:, t, h, :] if k == 0 else prod[:, u % 2, :]
                if u >= TT * NH + 2:
                    dve.wait_ge(s_pool_acc, count(ADDS * n + u - TT * NH - 1))
                w = V(hy[:, t, (k * G + h * GH) * H:K * G * H], [[H, GH], [0, GC], [1, H]])
                v.tensor_tensor(o.rearrange("p (g c q) -> p g c q", g=GH, q=H),
                                tb[u % 2][:, :].rearrange("p (g c q) -> p g c q", g=GH, q=H), w,
                                ALU.mult).then_inc(s_dve_p, 1)

            def sampled(n):
                dve.wait_ge(s_pool_acc, count(ADDS * n + ADDS))
                for t in range(TT):
                    last = v.tensor_reduce(dsum[:, t, :], V(acc[:, t, :, :], [[H, C], [1, H]]), AX, ALU.add)
                last.then_inc(s_dve_dr, 1)

            def x1(n):
                dve.wait_ge(s_act_z, count(n + 1))
                if not isinstance(n, int):
                    dve.wait_ge(s_dve_x2, count(1 * n))
                v.tensor_tensor(x1T[:, :], xT[:, :], zT[:, :], ALU.add).then_inc(s_dve_x1, 1)

            def stack(n, m):
                bx = (mb, h1[1])[m]
                dve.wait_ge(s_act_xh[m], count(n + 1))
                v.tensor_tensor(xl[m][:, :], bx[:, 0:PIX], xh[m][:, :], ALU.subtract).then_inc(s_dve_xl[m], 1)

            def top(n, m):
                settled(dve)
                dve.wait_ge(s_act_lg[m], count(n + 1))
                for t in range(TT):
                    last = v.max(mx[m][:, t, :], lg[m][:, t, :])
                last.then_inc(s_dve_mx[m], 1)
                dve.wait_ge(s_dve_mx[m], count(n + 1))
                v.tensor_scalar(nm[m][:, :], mx[m][:, :, 0], -1.0, None, ALU.mult).then_inc(s_dve_nm[m], 1)
                for t in range(TT):
                    last = v.max_index(ix[m][:, t, :], mx[m][:, t, :], lg[m][:, t, :])
                last.then_inc(s_dve_ix[m], 1)

            def gates(n, m):
                done = [0]

                def step(ins):
                    done[0] += 1
                    ins.then_inc(s_dve_gt[m], 1)
                    dve.wait_ge(s_dve_gt[m], count(GT[m] * n + done[0]))

                dve.wait_ge(s_dve_ix[m], count(n + 1))
                step(v.tensor_copy(ixf[m][:, :, :], ix[m][:, :, 0:2]))
                dve.wait_ge(s_act_ex[m], count(2 * TT * n + 2 * TT))
                step(v.reciprocal(sm[m][:, :], sm[m][:, :]))
                step(v.tensor_tensor(pk[m][:, :, :], em[m][:, :, :], V(sm[m][:, :], [[1, TT], [0, 2]]), ALU.mult))
                step(v.tensor_tensor(ks_[m][:, :, 0], pk[m][:, :, 0], pk[m][:, :, 1], ALU.add))
                if m == 0:
                    step(v.tensor_scalar(ks_[m][:, :, 0], ks_[m][:, :, 0], 1e-9, None, ALU.add))
                step(v.reciprocal(ks_[m][:, :, 1], ks_[m][:, :, 0]))
                step(v.tensor_tensor(pk[m][:, :, :], pk[m][:, :, :], V(ks_[m][:, :, 1:2], [[2, TT], [0, 2]]), ALU.mult))
                for t in range(TT):
                    for z in range(2):
                        done[0] += 1
                        v.tensor_scalar(oh[m][:, t, z, :], iota[:, 0:NE[m]], ixf[m][:, t, z:z + 1], pk[m][:, t, z:z + 1],
                                        ALU.is_equal, ALU.mult).then_inc(s_dve_gt[m], 1)
                dve.wait_ge(s_dve_gt[m], count(GT[m] * n + done[0]))
                done[0] += 1
                v.tensor_tensor(gt[m][:, :, :], oh[m][:, :, 0, :], oh[m][:, :, 1, :], ALU.add).then_inc(s_dve_gt[m], 1)
                assert done[0] == GT[m]

            def gate_unit(n, m, u):
                dve.wait_ge(s_act_g[m], count(GU[m] * n + u + 1))
                v.tensor_tensor(xgl[m][:, u % SLOTS, :], gate_bank[m][u][:, :], xgh[m][:, u % SLOTS, :],
                                ALU.subtract).then_inc(s_dve_g[m], 1)

            def up(n, j):
                ch = CH0 if j < PAIRS0 else CH1
                dve.wait_ge(s_act_s, count(PAIRS * n + j + 1))
                dve.wait_ge(s_pe_h3, count(PAIRS * n + j + 1))
                v.tensor_tensor(hid[0:ch, j % RING, :], h3[j % 2][0:ch, :], hid[0:ch, j % RING, :], ALU.mult).then_inc(s_dve_hid, 1)

            def x2(n):
                dve.wait_ge(s_pe_y2, count(PAIRS * n + PAIRS0))
                v.tensor_tensor(x2T[:, :], yb[0:C, 0:PIX], x1T[:, :], ALU.add).then_inc(s_dve_x2, 1)

            def x4(n):
                dve.wait_ge(s_pe_y2, count(PAIRS * n + PAIRS))
                dve.wait_ge(s_st, count(16 * n + 16))
                v.tensor_tensor(outT[:, :], yb[0:C, 0:PIX], x3T[:, :], ALU.add).then_inc(s_dve_x4, 1)

            q3 = V(q_s, [[DH, TT * HEADS], [1, DH]])

            def k_maxima(n):
                dve.wait_ge(s_pe_k, count(n + 1))
                v.tensor_reduce(km[:, :], h1[1][:, :].rearrange("p (c n) -> p c n", c=2), AX, ALU.max, negate=True).then_inc(s_dve_km, 1)

            def q_maxima(n):
                dve.wait_ge(s_pe_q, count(n + 1))
                v.tensor_reduce(qm[:, :], h1[0][:, :].rearrange("p (a d) -> p a d", d=DH), AX, ALU.max).then_inc(s_dve_qm, 1)
                dve.wait_ge(s_dve_qm, count(n + 1))
                v.tensor_tensor(q3, h1[0][:, :].rearrange("p (a d) -> p a d", d=DH), V(qm[:, :], [[1, TT * HEADS], [0, DH]]),
                                ALU.subtract).then_inc(s_dve_qs, 1)

            def q_norm(n):
                dve.wait_ge(s_act_q, count(n + 1))
                v.tensor_reduce(qz[:, :], q3, AX, ALU.add).then_inc(s_dve_qz, 1)
                dve.wait_ge(s_dve_qz, count(n + 1))
                v.reciprocal(qr[:, :], qz[:, :]).then_inc(s_dve_qr, 1)
                dve.wait_ge(s_dve_qr, count(n + 1))
                v.tensor_tensor(q3, q3, V(qr[:, :], [[1, TT * HEADS], [0, DH]]), ALU.mult).then_inc(s_dve_qn, 1)
                dve.wait_ge(s_act_k, count(2 * n + 2))
                v.reciprocal(kr[:, :, 0], kz[:, :]).then_inc(s_dve_kr, 1)

            def context(n):
                dve.wait_ge(s_pe_c, count(n + 1))
                v.tensor_tensor(cT[:, :, :], h3[0][:, 0:2 * P].rearrange("p (c d) -> p c d", c=2),
                                V(bmask[:, :], [[0, 2], [1, P]]), ALU.mult).then_inc(s_dve_c, 1)

            def mix(n):
                dve.wait_ge(s_dve_kr, count(2 * n + 1))
                v.tensor_scalar(kr[:, :, 1], kr[:, :, 0], SCALE, None, ALU.mult).then_inc(s_dve_kr, 1)
                dve.wait_ge(s_dve_kr, count(2 * n + 2))
                dve.wait_ge(s_pe_mm, count(n + 1))
                v.tensor_tensor(mT[:, :, :], h1[1][:, 0:2 * C].rearrange("p (c o) -> p c o", c=2),
                                V(kr[:, :, 1:2], [[2, 2], [0, C]]), ALU.mult).then_inc(s_dve_m, 1)

            def attend(n):
                dve.wait_ge(s_pe_at, count(n + 1))
                v.scalar_tensor_tensor(out=x3T[:, :], in0=yb[0:C, 0:PIX], scalar=vecs[:, 6:7], in1=x2T[:, :], op0=ALU.add,
                                       op1=ALU.add).then_inc(s_dve_x3, 1)

            steps = {"piece": piece, "stats": stats, "norm": norm, "y": y_rows, "depthwise": depthwise, "diagonal": diagonal,
                     "row_distances": row_distances, "column_weights": column_weights, "first_tap": tap, "tap": tap, "sampled": sampled, "x1": x1,
                     "stack": stack, "top": top, "gates": gates, "gate_unit": gate_unit, "up": up, "x2": x2, "x4": x4,
                     "k_maxima": k_maxima, "q_maxima": q_maxima, "q_norm": q_norm, "context": context, "mix": mix, "attend": attend}

            def walk(order, images):
                for stream, name, *args in order:
                    if name in steps:
                        steps[name](images[stream], *args)

            walk(first, {"a": 0, "w": 0})
            with dve.Fori(1, B) as i:
                walk(steady_order(WEAVE["dve"], steps), {"a": Image(i, 0), "b": Image(i, -1)})
            walk(final, {"b": B - 1})

        @block.gpsimd
        def _(pool):
            g = nc.gpsimd
            pool.wait_ge(s_const, n_const)
            pool.wait_ge(s_dve_set, 7)
            pool.sem_inc(s_st, 16)
            pool.sem_inc(s_dve_x4, 1)

            def rsqrt(n, j):
                pool.wait_ge(s_dve_mv[j], count(n + 1))
                g.tensor_tensor(rs[j][:, :], mv[j][:, :, 1], epst[:, j % 2, :], ALU.add).then_inc(s_pool_ve[j], 1)
                pool.wait_ge(s_pool_ve[j], count(n + 1))
                g.tensor_tensor(rs[j][:, :], rs[j][:, :], mhalf[:, :], ALU.pow).then_inc(s_pool_rs[j], 1)

            def row_weights(n, t):
                pool.wait_ge(s_act_hy, count(TT * n + t + 1))
                w = V(hy[:, t, :], [[H, K * G], [1, H]])
                g.tensor_tensor(w, w, V(ym[:, t, K * G:2 * K * G], [[1, K * G], [0, H]]), ALU.mult).then_inc(s_pool_hy, 1)

            def tap(n, k, q):
                t, h = divmod(q, NH)
                u = k * TT * NH + q
                a = u - TT * NH
                pool.wait_ge(s_dve_p, count(UNITS * n + u + 1))
                if a >= TT * NH:
                    pool.wait_ge(s_pool_acc, count(ADDS * n + a - TT * NH + 1))
                g.tensor_tensor(acc[:, t, h, :], acc[:, t, h, :], prod[:, u % 2, :], ALU.add).then_inc(s_pool_acc, 1)

            steps = {"stats": rsqrt, "row_weights": row_weights, "tap": tap}

            def walk(order, images):
                for stream, name, *args in order:
                    if name in steps:
                        steps[name](images[stream], *args)

            walk(first, {"a": 0, "w": 0})
            with pool.Fori(1, B) as i:
                walk(steady_order(WEAVE["pool"], steps), {"a": Image(i, 0), "b": Image(i, -1)})
            walk(final, {"b": B - 1})


def lay_out(i):
    import numpy as np
    a = {k: np.asarray(v) for k, v in i.items()}
    f = np.float32
    L = {}
    T = np.ascontiguousarray
    L["x"] = T(a["x"].reshape(B, C, PIX))
    L["vpT"] = T(np.concatenate([a["L0_conv_vp_w"].T, a["L0_conv_vp_b"][None]]))
    vecs = [a[k][:, None] for k in ("L0_conv_cv1_b", "L0_conv_dw_b", "L0_conv_bn_g", "L0_conv_bn_b", "L0_conv_bn_m",
                                    "L0_conv_bn_v", "L1_conv_b_out")]
    L["flat"] = T(np.concatenate([a[f"L0_conv_{n}_w"].T for n in ("cv1", "op", "cv2")] + [a["L0_conv_dw_w"].reshape(C, K)]
                                 + vecs + [a["L0_ffn_router_w"].T, a["L1_conv_w_qkv"].T], 1))
    om = np.concatenate([a["L0_conv_om_w"], a["L0_conv_om_b"][:, None]], 1)[:G * K * 3].reshape(G, 3 * K, C + 1)
    oy, ox, omk = om[:, 0:2 * K:2], om[:, 1:2 * K:2], om[:, 2 * K:]
    omym = np.concatenate([oy.transpose(2, 1, 0).reshape(C + 1, K * G), omk.transpose(2, 1, 0).reshape(C + 1, K * G)], 1)
    one, zero = np.ones(K * G), np.zeros(K * G)
    ky = np.repeat(np.arange(K) // 3 - 1, G)
    big = ox.reshape(NH, GH, K, C + 1).transpose(3, 2, 0, 1)[:, :, :, None, :, None]
    omx = T(np.broadcast_to(big, (C + 1, K, NH, 2, GH, W)).reshape(C + 1, K * NH * P))
    kx = np.broadcast_to((np.arange(K) % 3 - 1)[:, None, None, None, None] - np.arange(W), (K, NH, 2, GH, W)).reshape(-1)
    L["omxT"] = np.concatenate([omx, np.stack([np.ones(kx.size), np.zeros(kx.size), kx]).astype(f)])
    L["omymT"] = np.concatenate([omym, np.stack([np.concatenate(x) for x in ((zero, zero), (one, zero), (ky, zero))]).astype(f)])
    pix = np.arange(PIX)
    L["pixC"] = np.stack([np.ones(PIX), pix % W, pix // W, np.ones(PIX)]).astype(f)
    r = np.arange(P)
    fixed = [np.eye(P), -(r >= P // 2)[:, None].astype(f), (r[:, None] // W) % GH == np.arange(GH),
             np.broadcast_to(np.arange(W), (P, W)), r[:, None] // DH == r // DH]
    L["wide"] = np.concatenate([x.astype(f) for x in fixed]
                               + [a["L1_conv_w_out"].T.reshape(2, P, C).transpose(1, 0, 2).reshape(P, 2 * C)], 1)
    pad = CPE0 * CH0 - HID0

    def up0(w):
        return T(np.pad(w, ((0, 0), (0, pad), (0, 0))).transpose(2, 0, 1).reshape(C, -1))
    L["w1T"], L["w3T"] = up0(a["L0_ffn_w1"]), up0(a["L0_ffn_w3"])
    w2 = np.pad(a["L0_ffn_w2"], ((0, 0), (0, 0), (0, pad))).reshape(E0, C, CPE0, CH0)
    L["w2T"] = T(w2.transpose(3, 0, 2, 1).reshape(CH0, NC0, C))
    L["gwT"] = T(np.concatenate([a["L1_ffn_gate_w"], a["L1_ffn_gate_b"][None]]))
    L["u1T"], L["u2T"] = (T(a[f"L1_ffn_w{j}"].transpose(1, 0, 2).reshape(C, -1)) for j in (1, 2))
    L["u3T"] = T(a["L1_ffn_w3"].transpose(1, 0, 2))
    return L


def kernel(**inputs):
    import concourse.bacc as bacc
    from concourse.bass_utils import run_bass_kernel_spmd

    arrays = lay_out(inputs)
    nc = bacc.Bacc("TRN2", target_bir_lowering=False, num_devices=1)
    A = {k: nc.dram_tensor("in_" + k, v.shape, mybir.dt.from_np(v.dtype), kind="ExternalInput").ap() for k, v in arrays.items()}
    out = nc.dram_tensor("out", (B, C, PIX), mybir.dt.float32, kind="ExternalOutput").ap()
    build(nc, A, out)
    r = run_bass_kernel_spmd(nc, [{"in_" + k: v for k, v in arrays.items()}], core_ids=[0])
    return r.results[0]["out"].reshape(B, C, H, W)
```
